# Optimizing a Trainium2 kernel written in Bass

```python
import numpy as np
import jax
import jax.numpy as jnp

def _softmax(x, axis=-1):
    return jax.nn.softmax(x, axis=axis)

def _gelu(x):
    return jax.nn.gelu(x, approximate=True)

def _silu(x):
    return jax.nn.silu(x)

def _sigmoid(x):
    return jax.nn.sigmoid(x)

def _layernorm(x, axis=-1, eps=1e-05):
    m = jnp.mean(x, axis=axis, keepdims=True)
    v = jnp.var(x, axis=axis, keepdims=True)
    return (x - m) / jnp.sqrt(v + eps)

def _scatter_add(tgt, idx, src, axis=0):
    return tgt.at[idx].add(src)

def _segment_sum(src, seg, n):
    return jax.ops.segment_sum(src, seg, n)
kernel_name = 'mk_gps_d1_gnn_r8_853ba5'

def setup_inputs(seed: int=0):
    np.random.seed(seed)
    _w = jnp.asarray

    def _rec_inputs():
        import jax
        import jax.numpy as jnp
        _gk = jax.random.key(seed)
        x = -0.0003713 + 1 * jax.random.normal(jax.random.fold_in(_gk, 1), (12500, 256), jnp.float32)
        src = jax.random.randint(jax.random.fold_in(_gk, 2), (200000,), 0, 12500, jnp.int32)
        dst = jax.random.randint(jax.random.fold_in(_gk, 3), (200000,), 0, 12500, jnp.int32)
        _o = jnp.argsort(dst, stable=True)
        src = src[_o]
        dst = dst[_o]
        return (x, src, dst)
    x, src, dst = _rec_inputs()

    def _L0_gnn_setup():
        import jax, jax.numpy as jnp
        import numpy as np
        N_NODES = 6250
        N_EDGES = 100000
        D_IN = 256
        D_OUT = 256
        BN_EPS = 1e-05

        def _forward(x, edge_index, w1, b1, gamma, beta, w2, b2, w_gcn, b_gcn):
            n = x.shape[0]
            h = x @ w1.T + b1
            mean = jnp.mean(h, axis=0)
            var = jnp.var(h, axis=0)
            h = (h - mean) * jax.lax.rsqrt(var + BN_EPS) * gamma + beta
            h = jax.nn.relu(h)
            h = h @ w2.T + b2
            xw = h @ w_gcn.T
            src = jnp.concatenate([edge_index[0], jnp.arange(n, dtype=edge_index.dtype)])
            dst = jnp.concatenate([edge_index[1], jnp.arange(n, dtype=edge_index.dtype)])
            deg = jax.ops.segment_sum(jnp.ones_like(dst, dtype=xw.dtype), dst, num_segments=n)
            dinv = jnp.where(deg > 0, jax.lax.rsqrt(jnp.maximum(deg, 1.0)), 0.0)
            norm = dinv[src] * dinv[dst]
            msgs = xw[src] * norm[:, None]
            out = jax.ops.segment_sum(msgs, dst, num_segments=n) + b_gcn
            return out
        key = jax.random.key(seed)
        ks = jax.random.split(key, 8)
        x = jax.random.normal(ks[0], (N_NODES, D_IN), dtype=jnp.float32)
        edge_index = jax.random.randint(ks[1], (2, N_EDGES), 0, N_NODES, dtype=jnp.int64)
        s1 = 1.0 / np.sqrt(D_IN)
        s2 = 1.0 / np.sqrt(D_OUT)
        w1 = jax.random.uniform(ks[2], (D_OUT, D_IN), jnp.float32, -s1, s1)
        b1 = jax.random.uniform(ks[3], (D_OUT,), jnp.float32, -s1, s1)
        gamma = jnp.ones((D_OUT,), jnp.float32)
        beta = jnp.zeros((D_OUT,), jnp.float32)
        w2 = jax.random.uniform(ks[4], (D_OUT, D_OUT), jnp.float32, -s2, s2)
        b2 = jax.random.uniform(ks[5], (D_OUT,), jnp.float32, -s2, s2)
        w_gcn = jax.random.uniform(ks[6], (D_OUT, D_OUT), jnp.float32, -s2, s2)
        b_gcn = jnp.zeros((D_OUT,), jnp.float32)
        return {'x': x, 'edge_index': edge_index, 'w1': w1, 'b1': b1, 'gamma': gamma, 'beta': beta, 'w2': w2, 'b2': b2, 'w_gcn': w_gcn, 'b_gcn': b_gcn}
    _L0_gnn_all = _L0_gnn_setup()
    _L0_gnn_in = {k: v for k, v in _L0_gnn_all.items() if k in ('w1', 'b1', 'gamma', 'beta', 'w2', 'b2', 'w_gcn', 'b_gcn')}
    del _L0_gnn_all

    def _L0_mix_setup():
        import jax, jax.numpy as jnp
        import numpy as np
        D_MODEL = 256
        NUM_HEADS = 8
        DEPTH = D_MODEL // NUM_HEADS
        B, L = (32, 512)

        def _feature_map(x):
            return jax.nn.elu(x) + 1.0
        key = jax.random.key(seed)
        ks = jax.random.split(key, 9)
        sc = 1.0 / np.sqrt(D_MODEL)
        return {'x': jax.random.normal(ks[0], (B, L, D_MODEL), dtype=jnp.float32), 'wq': jax.random.normal(ks[1], (D_MODEL, D_MODEL), dtype=jnp.float32) * sc, 'bq': jnp.zeros((D_MODEL,), dtype=jnp.float32), 'wk': jax.random.normal(ks[2], (D_MODEL, D_MODEL), dtype=jnp.float32) * sc, 'bk': jnp.zeros((D_MODEL,), dtype=jnp.float32), 'wv': jax.random.normal(ks[3], (D_MODEL, D_MODEL), dtype=jnp.float32) * sc, 'bv': jnp.zeros((D_MODEL,), dtype=jnp.float32), 'wo': jax.random.normal(ks[4], (D_MODEL, D_MODEL), dtype=jnp.float32) * sc, 'bo': jnp.zeros((D_MODEL,), dtype=jnp.float32)}
    _L0_mix_all = _L0_mix_setup()
    _L0_mix_in = {k: v for k, v in _L0_mix_all.items() if k in ('wq', 'bq', 'wk', 'bk', 'wv', 'bv', 'wo', 'bo')}
    del _L0_mix_all

    def _L0_ffn_setup():
        import jax, jax.numpy as jnp
        import numpy as np
        B, N, D = (16, 512, 256)
        NUM_EXPERTS, TOP_K, HEADS = (4, 2, 4)
        N_EDGES = 131072
        LN_EPS = 1e-05

        def _layernorm(x, g, b):
            mu = x.mean(-1, keepdims=True)
            var = ((x - mu) ** 2).mean(-1, keepdims=True)
            return (x - mu) * jax.lax.rsqrt(var + LN_EPS) * g + b

        def _forward(x, edge_index, W_gat, att_src, att_dst, b_gat, ln_gamma, ln_beta, W1, b1, W2, b2):
            Bc, Nc, Dc = x.shape
            M = Bc * Nc
            x_flat = x.reshape(M, Dc)
            h = (x_flat @ W_gat).reshape(M, HEADS, NUM_EXPERTS)
            loops = jnp.arange(M, dtype=edge_index.dtype)
            src = jnp.concatenate([edge_index[0], loops])
            dst = jnp.concatenate([edge_index[1], loops])
            a_src = (h * att_src).sum(-1)
            a_dst = (h * att_dst).sum(-1)
            e = jax.nn.leaky_relu(a_src[src] + a_dst[dst], negative_slope=0.2)
            e_max = jax.ops.segment_max(e, dst, num_segments=M)
            ee = jnp.exp(e - e_max[dst])
            denom = jax.ops.segment_sum(ee, dst, num_segments=M)
            alpha = ee / (denom[dst] + 1e-16)
            msg = h[src] * alpha[:, :, None]
            agg = jax.ops.segment_sum(msg, dst, num_segments=M).reshape(M, HEADS * NUM_EXPERTS) + b_gat
            scores = _layernorm(agg, ln_gamma, ln_beta).reshape(M, HEADS, NUM_EXPERTS).mean(1)
            scores = scores.reshape(Bc, Nc, NUM_EXPERTS)
            topk_s, topk_i = jax.lax.top_k(scores, TOP_K)
            w = jax.nn.softmax(topk_s, axis=-1)
            out = jnp.zeros_like(x)
            for ei in range(NUM_EXPERTS):
                g = jnp.where(topk_i == ei, w, 0.0).sum(-1)
                hh = jax.nn.gelu(x @ W1[ei] + b1[ei], approximate=False)
                out = out + g[..., None] * (hh @ W2[ei] + b2[ei])
            return out
        key = jax.random.key(seed)
        ks = jax.random.split(key, 8)
        s = 0.05
        return {'x': jax.random.normal(ks[0], (B, N, D), jnp.float32), 'W_gat': jax.random.normal(ks[1], (D, HEADS * NUM_EXPERTS), jnp.float32) * s, 'att_src': jax.random.normal(ks[2], (HEADS, NUM_EXPERTS), jnp.float32) * s, 'att_dst': jax.random.normal(ks[3], (HEADS, NUM_EXPERTS), jnp.float32) * s, 'b_gat': jnp.zeros((HEADS * NUM_EXPERTS,), jnp.float32), 'ln_gamma': jnp.ones((HEADS * NUM_EXPERTS,), jnp.float32), 'ln_beta': jnp.zeros((HEADS * NUM_EXPERTS,), jnp.float32), 'W1': jax.random.normal(ks[4], (NUM_EXPERTS, D, 2 * D), jnp.float32) * s, 'b1': jnp.zeros((NUM_EXPERTS, 2 * D), jnp.float32), 'W2': jax.random.normal(ks[5], (NUM_EXPERTS, 2 * D, D), jnp.float32) * s, 'b2': jnp.zeros((NUM_EXPERTS, D), jnp.float32), 'edge_index': jax.random.randint(ks[6], (2, N_EDGES), 0, B * N, jnp.int32)}
    _L0_ffn_all = _L0_ffn_setup()
    _L0_ffn_in = {k: v for k, v in _L0_ffn_all.items() if k in ('W_gat', 'att_src', 'att_dst', 'b_gat', 'ln_gamma', 'ln_beta', 'W1', 'b1', 'W2', 'b2', 'edge_index')}
    del _L0_ffn_all
    return {'x': x, 'src': src, 'dst': dst, 'L0_gnn_w1': _L0_gnn_in['w1'], 'L0_gnn_b1': _L0_gnn_in['b1'], 'L0_gnn_gamma': _L0_gnn_in['gamma'], 'L0_gnn_beta': _L0_gnn_in['beta'], 'L0_gnn_w2': _L0_gnn_in['w2'], 'L0_gnn_b2': _L0_gnn_in['b2'], 'L0_gnn_w_gcn': _L0_gnn_in['w_gcn'], 'L0_gnn_b_gcn': _L0_gnn_in['b_gcn'], 'L0_mix_wq': _L0_mix_in['wq'], 'L0_mix_bq': _L0_mix_in['bq'], 'L0_mix_wk': _L0_mix_in['wk'], 'L0_mix_bk': _L0_mix_in['bk'], 'L0_mix_wv': _L0_mix_in['wv'], 'L0_mix_bv': _L0_mix_in['bv'], 'L0_mix_wo': _L0_mix_in['wo'], 'L0_mix_bo': _L0_mix_in['bo'], 'L0_ffn_W_gat': _L0_ffn_in['W_gat'], 'L0_ffn_att_src': _L0_ffn_in['att_src'], 'L0_ffn_att_dst': _L0_ffn_in['att_dst'], 'L0_ffn_b_gat': _L0_ffn_in['b_gat'], 'L0_ffn_ln_gamma': _L0_ffn_in['ln_gamma'], 'L0_ffn_ln_beta': _L0_ffn_in['ln_beta'], 'L0_ffn_W1': _L0_ffn_in['W1'], 'L0_ffn_b1': _L0_ffn_in['b1'], 'L0_ffn_W2': _L0_ffn_in['W2'], 'L0_ffn_b2': _L0_ffn_in['b2'], 'L0_ffn_edge_index': _L0_ffn_in['edge_index']}

def reference(x, src, dst, L0_gnn_w1, L0_gnn_b1, L0_gnn_gamma, L0_gnn_beta, L0_gnn_w2, L0_gnn_b2, L0_gnn_w_gcn, L0_gnn_b_gcn, L0_mix_wq, L0_mix_bq, L0_mix_wk, L0_mix_bk, L0_mix_wv, L0_mix_bv, L0_mix_wo, L0_mix_bo, L0_ffn_W_gat, L0_ffn_att_src, L0_ffn_att_dst, L0_ffn_b_gat, L0_ffn_ln_gamma, L0_ffn_ln_beta, L0_ffn_W1, L0_ffn_b1, L0_ffn_W2, L0_ffn_b2, L0_ffn_edge_index):
    import jax
    import jax.numpy as jnp

    def _L0_gnn_ref(x, edge_index, w1, b1, gamma, beta, w2, b2, w_gcn, b_gcn):
        import jax, jax.numpy as jnp
        import numpy as np
        N_NODES = 6250
        N_EDGES = 100000
        D_IN = 256
        D_OUT = 256
        BN_EPS = 1e-05

        def _forward(x, edge_index, w1, b1, gamma, beta, w2, b2, w_gcn, b_gcn):
            n = x.shape[0]
            h = x @ w1.T + b1
            mean = jnp.mean(h, axis=0)
            var = jnp.var(h, axis=0)
            h = (h - mean) * jax.lax.rsqrt(var + BN_EPS) * gamma + beta
            h = jax.nn.relu(h)
            h = h @ w2.T + b2
            xw = h @ w_gcn.T
            src = jnp.concatenate([edge_index[0], jnp.arange(n, dtype=edge_index.dtype)])
            dst = jnp.concatenate([edge_index[1], jnp.arange(n, dtype=edge_index.dtype)])
            deg = jax.ops.segment_sum(jnp.ones_like(dst, dtype=xw.dtype), dst, num_segments=n)
            dinv = jnp.where(deg > 0, jax.lax.rsqrt(jnp.maximum(deg, 1.0)), 0.0)
            norm = dinv[src] * dinv[dst]
            msgs = xw[src] * norm[:, None]
            out = jax.ops.segment_sum(msgs, dst, num_segments=n) + b_gcn
            return out
        return _forward(x, edge_index, w1, b1, gamma, beta, w2, b2, w_gcn, b_gcn)

    def _L0_mix_ref(x, wq, bq, wk, bk, wv, bv, wo, bo):
        import jax, jax.numpy as jnp
        import numpy as np
        D_MODEL = 256
        NUM_HEADS = 8
        DEPTH = D_MODEL // NUM_HEADS
        B, L = (32, 512)

        def _feature_map(x):
            return jax.nn.elu(x) + 1.0
        b, l, _ = x.shape
        q = (x @ wq + bq).reshape(b, l, NUM_HEADS, DEPTH)
        k = (x @ wk + bk).reshape(b, l, NUM_HEADS, DEPTH)
        v = (x @ wv + bv).reshape(b, l, NUM_HEADS, DEPTH)
        q = _feature_map(q)
        k = _feature_map(k)
        kv = jnp.einsum('blhd,blhe->bhde', k, v)
        k_sum = jnp.sum(k, axis=1)
        qkv = jnp.einsum('blhd,bhde->blhe', q, kv)
        normalizer = jnp.einsum('blhd,bhd->blh', q, k_sum) + 1e-06
        out = qkv / normalizer[..., None]
        out = out.reshape(b, l, D_MODEL)
        return out @ wo + bo

    def _L0_ffn_ref(x, W_gat, att_src, att_dst, b_gat, ln_gamma, ln_beta, W1, b1, W2, b2, edge_index):
        import jax, jax.numpy as jnp
        import numpy as np
        B, N, D = (16, 512, 256)
        NUM_EXPERTS, TOP_K, HEADS = (4, 2, 4)
        N_EDGES = 131072
        LN_EPS = 1e-05

        def _layernorm(x, g, b):
            mu = x.mean(-1, keepdims=True)
            var = ((x - mu) ** 2).mean(-1, keepdims=True)
            return (x - mu) * jax.lax.rsqrt(var + LN_EPS) * g + b

        def _forward(x, edge_index, W_gat, att_src, att_dst, b_gat, ln_gamma, ln_beta, W1, b1, W2, b2):
            Bc, Nc, Dc = x.shape
            M = Bc * Nc
            x_flat = x.reshape(M, Dc)
            h = (x_flat @ W_gat).reshape(M, HEADS, NUM_EXPERTS)
            loops = jnp.arange(M, dtype=edge_index.dtype)
            src = jnp.concatenate([edge_index[0], loops])
            dst = jnp.concatenate([edge_index[1], loops])
            a_src = (h * att_src).sum(-1)
            a_dst = (h * att_dst).sum(-1)
            e = jax.nn.leaky_relu(a_src[src] + a_dst[dst], negative_slope=0.2)
            e_max = jax.ops.segment_max(e, dst, num_segments=M)
            ee = jnp.exp(e - e_max[dst])
            denom = jax.ops.segment_sum(ee, dst, num_segments=M)
            alpha = ee / (denom[dst] + 1e-16)
            msg = h[src] * alpha[:, :, None]
            agg = jax.ops.segment_sum(msg, dst, num_segments=M).reshape(M, HEADS * NUM_EXPERTS) + b_gat
            scores = _layernorm(agg, ln_gamma, ln_beta).reshape(M, HEADS, NUM_EXPERTS).mean(1)
            scores = scores.reshape(Bc, Nc, NUM_EXPERTS)
            topk_s, topk_i = jax.lax.top_k(scores, TOP_K)
            w = jax.nn.softmax(topk_s, axis=-1)
            out = jnp.zeros_like(x)
            for ei in range(NUM_EXPERTS):
                g = jnp.where(topk_i == ei, w, 0.0).sum(-1)
                hh = jax.nn.gelu(x @ W1[ei] + b1[ei], approximate=False)
                out = out + g[..., None] * (hh @ W2[ei] + b2[ei])
            return out
        return _forward(x, edge_index, W_gat, att_src, att_dst, b_gat, ln_gamma, ln_beta, W1, b1, W2, b2)
    edge_index = jnp.stack([src, dst])
    xn = _layernorm(x, axis=-1)
    x = x + _L0_gnn_ref(xn, edge_index, L0_gnn_w1, L0_gnn_b1, L0_gnn_gamma, L0_gnn_beta, L0_gnn_w2, L0_gnn_b2, L0_gnn_w_gcn, L0_gnn_b_gcn) + _L0_mix_ref(xn[None], L0_mix_wq, L0_mix_bq, L0_mix_wk, L0_mix_bk, L0_mix_wv, L0_mix_bv, L0_mix_wo, L0_mix_bo)[0]
    x = x + _L0_ffn_ref(_layernorm(x, axis=-1)[None], L0_ffn_W_gat, L0_ffn_att_src, L0_ffn_att_dst, L0_ffn_b_gat, L0_ffn_ln_gamma, L0_ffn_ln_beta, L0_ffn_W1, L0_ffn_b1, L0_ffn_W2, L0_ffn_b2, L0_ffn_edge_index)[0]
    return x

_drawn_inputs = setup_inputs


def setup_inputs(seed=0):
    import zlib

    import numpy as np

    out = dict(_drawn_inputs(seed))
    spreads = {'L0_gnn_gamma': (1.0, 0.2),
     'L0_gnn_beta': (0.0, 0.1),
     'L0_gnn_b_gcn': (0.0, 0.1),
     'L0_mix_bq': (0.0, 2.0),
     'L0_mix_bk': (0.0, 2.0),
     'L0_mix_bv': (0.0, 0.1),
     'L0_mix_bo': (0.0, 0.1),
     'L0_ffn_b_gat': (0.0, 0.1),
     'L0_ffn_ln_gamma': (1.0, 0.2),
     'L0_ffn_ln_beta': (0.0, 0.1),
     'L0_ffn_b1': (0.0, 0.1),
     'L0_ffn_b2': (0.0, 0.1)}
    factors = {'L0_gnn_b1': 64.0, 'L0_mix_wq': 11.285}
    for name, (base, spread) in spreads.items():
        noise = np.random.default_rng([zlib.crc32(name.encode()), seed]).standard_normal(out[name].shape)
        drawn = base * np.exp(spread * noise) if base else spread * noise
        out[name] = jnp.asarray(drawn.astype(out[name].dtype))
    for name, factor in factors.items():
        out[name] = (out[name] * factor).astype(out[name].dtype)
    return out
```

```python
from contextlib import ExitStack

import concourse.bass as bass
from concourse import mybir

F32 = mybir.dt.float32
I32 = mybir.dt.int32
U32 = mybir.dt.uint32
U16 = mybir.dt.uint16
BF16 = mybir.dt.bfloat16
ALU = mybir.AluOpType
ACT = mybir.ActivationFunctionType
AX = mybir.AxisListType

N = 12500
D = 256
P = 128
TN = 125
NT = N // TN
SUB = 4
BN = SUB * TN
NB = N // BN
KC = D // P
HD = 32
EPS = 1e-5
E_GCN, GCN_P = 200000, 125
E_GAT, GAT_P = 131072, 128
GCN_C, GAT_C = E_GCN // GCN_P, E_GAT // GAT_P
BATCH = 8
HALVES = 2


def steps_for(edges):
    most = (edges + NT * (P - 1)) // P
    body = BATCH * HALVES
    return -(-most // body) * body


S_GCN, S_GAT = steps_for(E_GCN), steps_for(E_GAT)
G_GCN, G_GAT = -(-S_GCN // P), -(-S_GAT // P)
NE, FF = 4, 512
GH = 4
GW = GH * NE
ROW = GW + GH


def blocks(eng, body):
    with eng.Fori(0, NB // 2) as i:
        body(i * 2, i, 0)
        body(i * 2 + 1, i, 1)
    if NB % 2:
        body(NB - 1, NB // 2, 0)


class Mem:

    def __init__(self, nc, ctx):
        self.nc, self.ctx, self.sems = nc, ctx, []
        ctx.callback(self.clear)

    def clear(self):
        if not self.sems:
            return
        with self.nc.Block() as block:
            @block.gpsimd
            def _(pool):
                for s in self.sems:
                    pool.sem_clear(s)
        for s in self.sems:
            self.nc.release_semaphore(s)

    def sb(self, name, shape, dt=F32):
        return self.ctx.enter_context(self.nc.sbuf_tensor(name, shape, dt))

    def ps(self, name, shape, dt=F32):
        return self.ctx.enter_context(self.nc.psum_tensor(name, shape, dt))

    def sem(self, name):
        self.sems.append(self.nc.alloc_semaphore(name))
        return self.sems[-1]

    def dram(self, name, shape, dt=F32):
        return self.nc.dram_tensor(name, shape, dt).ap()


def constants(nc, m, K):
    K.ident = m.sb("ident", [P, P])
    K.ones = m.sb("ones", [P, P])
    K.before = m.sb("before", [P, P])
    K.iota = m.sb("iota", [P, P])
    K.iota_h = m.sb("iota_h", [P, P], BF16)
    K.head = m.sb("head", [P, P])
    K.part = m.sb("part", [P, 1])
    iota_i = m.sb("iota_i", [P, P], I32)
    part_i = m.sb("part_i", [P, 1], I32)
    q_s, j_s, v_s = m.sem("c_set"), m.sem("c_sel"), m.sem("c_copied")
    with nc.Block() as block:
        @block.gpsimd
        def _(pool):
            pool.memset(K.ident[:], 0.0).then_inc(q_s, 1)
            pool.memset(K.ones[:], 1.0).then_inc(q_s, 1)
            pool.memset(K.before[:], 0.0).then_inc(q_s, 1)
            pool.iota(iota_i[:], [[1, P]], base=0, channel_multiplier=0).then_inc(q_s, 1)
            pool.iota(part_i[:], [[1, 1]], base=0, channel_multiplier=1).then_inc(q_s, 1)
            pool.wait_ge(q_s, 5)
            pool.affine_select(out=K.ident[:], in_=K.ident[:], compare_op=ALU.not_equal, fill=1.0, base=0,
                               pattern=[[-1, P]], channel_multiplier=1).then_inc(j_s, 1)
            pool.affine_select(out=K.before[:], in_=K.before[:], compare_op=ALU.is_ge, fill=1.0, base=0,
                               pattern=[[-1, P]], channel_multiplier=1).then_inc(j_s, 1)
            hv = K.head[:].rearrange("p (g j) -> p g j", j=HD)
            pool.affine_select(out=hv, in_=K.ones[:].rearrange("p (g j) -> p g j", j=HD), compare_op=ALU.is_ge,
                               fill=0.0, base=0, pattern=[[-HD, P // HD], [0, HD]],
                               channel_multiplier=1).then_inc(j_s, 1)
            pool.wait_ge(j_s, 3)
            pool.affine_select(out=hv, in_=hv, compare_op=ALU.is_ge, fill=0.0, base=HD - 1,
                               pattern=[[HD, P // HD], [0, HD]], channel_multiplier=-1).then_inc(j_s, 1)

        @block.vector
        def _(dve):
            dve.wait_ge(q_s, 5)
            dve.tensor_copy(K.iota[:], iota_i[:]).then_inc(v_s, 1)
            dve.tensor_copy(K.iota_h[:], iota_i[:]).then_inc(v_s, 1)
            dve.tensor_copy(K.part[:], part_i[:]).then_inc(v_s, 1)
            dve.wait_ge(v_s, 3)


def sort_edges(nc, K, tag, pairs, n_part, cols, tile_h, pay, count_only=False):
    with ExitStack() as ctx:
        m = Mem(nc, ctx)
        passed = m.sem(tag + "_passed")
        cnt = m.sb(tag + "_cnt", [P, NT])
        eq = m.sb(tag + "_eq", [P, cols], U16)
        run = m.sb(tag + "_run", [P, cols])
        place_f = m.sb(tag + "_place_f", [P, cols])
        place = m.sb(tag + "_place", [P, cols], U32)
        incl = m.sb(tag + "_incl", [P, NT])
        off = m.sb(tag + "_off", [P, NT])
        ptot = m.ps(tag + "_ptot", [P, NT])
        ppre = m.ps(tag + "_ppre", [P, NT])
        counted, summed, chain, placed = (m.sem(tag + x) for x in ("_counted", "_summed", "_chain", "_placed"))
        q = slice(0, n_part)
        with nc.Block() as block:
            @block.vector
            def _(dve):
                with dve.Fori(0, NT) as t:
                    dve.wait_ge(counted, t)
                    dve.tensor_scalar(eq[q], tile_h[q], K.iota[q, bass.ds(t, 1)], None, ALU.is_equal, ALU.add,
                                      accum_out=cnt[q, bass.ds(t, 1)]).then_inc(counted, 1)
                dve.wait_ge(summed, 2)
                dve.tensor_copy(K.cnt[:], ptot[:]).then_inc(chain, 1)
                dve.wait_ge(chain, 1)
                dve.tensor_tensor_scan(incl[:], K.cnt[:], K.cnt[:], 0.0, ALU.add, ALU.bypass).then_inc(chain, 1)
                dve.wait_ge(chain, 2)
                dve.tensor_tensor(K.base[:], incl[:], K.cnt[:], ALU.subtract).then_inc(chain, 1)
                dve.wait_ge(chain, 3)
                dve.scalar_tensor_tensor(off[q], ppre[q], -1.0, K.base[q], ALU.add, ALU.add).then_inc(chain, 1)
                dve.wait_ge(chain, 4)
                if not count_only:
                    dve.wait_ge(placed, 1)
                    with dve.Fori(0, NT) as t:
                        dve.tensor_scalar(eq[q], tile_h[q], K.iota[q, bass.ds(t, 1)], None,
                                          ALU.is_equal).then_inc(chain, 1)
                        dve.wait_ge(chain, t * 3 + 5)
                        dve.tensor_tensor_scan(run[q], eq[q], eq[q], off[q, bass.ds(t, 1)], ALU.add,
                                               ALU.bypass).then_inc(chain, 1)
                        dve.wait_ge(chain, t * 3 + 6)
                        dve.sem_inc(passed, 1)
                        dve.copy_predicated(place_f[q], eq[q], run[q]).then_inc(chain, 1)
                        dve.wait_ge(chain, t * 3 + 7)
                    dve.tensor_copy(place[q], place_f[q]).then_inc(placed, 1)

            @block.gpsimd
            def _(pool):
                pool.memset(place_f[:], 0.0).then_inc(placed, 1)

            @block.tensor
            def _(pe):
                pe.wait_ge(counted, NT)
                pe.matmul(ptot[:], K.ones[q, :], cnt[q], start=True, stop=True).then_inc(summed, 1)
                pe.matmul(ppre[q], K.before[q, q], cnt[q], start=True, stop=True).then_inc(summed, 1)
        if count_only:
            return
        at = m.sb(tag + "_at", [P, HALVES, BATCH], U32)
        row = m.sb(tag + "_row", [P, HALVES, BATCH, 2], I32)
        staged = m.sem(tag + "_staged")
        sent = [m.sem(f"{tag}_sent{h}") for h in range(HALVES)]
        nq = n_part
        with nc.Block() as block:
            @block.gpsimd
            def _(pool):
                with pool.Fori(0, cols // (BATCH * HALVES)) as i:
                    for h in range(HALVES):
                        c = i * (BATCH * HALVES) + h * BATCH
                        pool.wait_ge(sent[h], i * (16 * BATCH))
                        pool.tensor_copy(at[0:nq, h], place[0:nq, bass.ds(c, BATCH)]).then_inc(staged, 1)
                        pool.tensor_copy(row[0:nq, h], pay[0:nq, bass.ds(c, BATCH), :]).then_inc(staged, 1)
                        pool.wait_ge(staged, i * 4 + 2 * h + 2)
                        pool.sem_inc(passed, 1)
                        for b in range(BATCH):
                            pool.indirect_dma_start(
                                out=pairs, out_offset=bass.IndirectOffsetOnAxis(ap=at[0:nq, h, b:b + 1], axis=0),
                                in_=row[0:nq, h, b, :], in_offset=None).then_inc(sent[h], 16)
                for h in range(HALVES):
                    pool.wait_ge(sent[h], 16 * BATCH * (cols // (BATCH * HALVES)))


def step_tables(nc, K, tag, pairs, edges, groups, src_T, dst_T, tile_row, tile_dram):
    with ExitStack() as ctx:
        m = Mem(nc, ctx)
        nch = m.sb(tag + "_nch", [P, NT])
        nch_i = m.sb(tag + "_nch_i", [P, NT], I32)
        ch_end = m.sb(tag + "_ch_end", [P, NT])
        ch_start = m.sb(tag + "_ch_start", [P, NT])
        shift = m.sb(tag + "_shift", [P, NT])
        ended = m.sb(tag + "_ended", [P, groups, NT])
        mine = m.sb(tag + "_mine", [P, groups, NT])
        step = m.sb(tag + "_step", [P, groups])
        tile = m.sb(tag + "_tile", [P, groups])
        tile_i = m.sb(tag + "_tile_i", [P, groups], I32)
        first = m.sb(tag + "_first", [P, groups])
        first_i = m.sb(tag + "_first_i", [P, groups], U32)
        node0 = m.sb(tag + "_node0", [P, groups])
        rows = m.sb(tag + "_rows", [P, 2, P, 2], I32)
        cols = m.sb(tag + "_cols", [P, 2, 2, P])
        ptr = m.ps(tag + "_ptr", [P, 2, 2, P])
        c, fetched, split, turned, used, out_s = (m.sem(tag + x) for x in (
            "_st", "_fetched", "_split", "_turned", "_used", "_outs"))
        fetch = [m.sem(f"{tag}_fetch{h}") for h in range(2)]
        with nc.Block() as block:
            @block.vector
            def _(dve):
                n = [0]

                def done(ins):
                    n[0] += 1
                    ins.then_inc(c, 1)
                    dve.wait_ge(c, n[0])

                done(dve.tensor_scalar(nch_i[:], K.cnt[:], 1.0 / P, (P - 1) / (2.0 * P), ALU.mult, ALU.add))
                done(dve.tensor_copy(nch[:], nch_i[:]))
                done(dve.tensor_tensor_scan(ch_end[:], nch[:], nch[:], 0.0, ALU.add, ALU.bypass))
                done(dve.tensor_tensor(ch_start[:], ch_end[:], nch[:], ALU.subtract))
                done(dve.scalar_tensor_tensor(shift[:], ch_start[:], -float(P), K.base[:], ALU.mult, ALU.add))
                for g in range(groups):
                    dve.tensor_scalar(step[:, g:g + 1], K.part[:], float(P * g), None, ALU.add).then_inc(c, 1)
                n[0] += groups
                dve.wait_ge(c, n[0])
                both = [P, groups, NT]
                st = step[:].unsqueeze(2).to_broadcast(both)
                done(dve.tensor_tensor(ended[:], ch_end[:].unsqueeze(1).to_broadcast(both), st, ALU.is_le))
                done(dve.tensor_tensor(mine[:], ch_start[:].unsqueeze(1).to_broadcast(both), st, ALU.is_le))
                done(dve.tensor_tensor(mine[:], mine[:], ended[:], ALU.subtract))
                done(dve.tensor_tensor(mine[:], mine[:], shift[:].unsqueeze(1).to_broadcast(both), ALU.mult))
                done(dve.tensor_reduce(first[:], mine[:], AX.X, ALU.add))
                done(dve.scalar_tensor_tensor(first[:], step[:], float(P), first[:], ALU.mult, ALU.add))
                done(dve.tensor_scalar(first_i[:], first[:], float(edges), None, ALU.min))
                done(dve.tensor_reduce(tile[:], ended[:], AX.X, ALU.add))
                done(dve.tensor_scalar(tile[:], tile[:], float(NT - 1), None, ALU.min))
                done(dve.tensor_copy(tile_i[:], tile[:]))
                done(dve.tensor_scalar(node0[:], tile[:], float(TN), None, ALU.mult))
                dve.sem_inc(fetched, 1)
                for g in range(groups):
                    s = g % 2
                    dve.wait_ge(fetch[s], 16 * (g // 2 + 1))
                    if g >= 2:
                        dve.wait_ge(turned, 2 * (g - 1))
                    dve.tensor_copy(cols[:, s, 0], rows[:, s, :, 0]).then_inc(split, 1)
                    dve.tensor_scalar(cols[:, s, 1], rows[:, s, :, 1], node0[:, g:g + 1], None,
                                      ALU.subtract).then_inc(split, 1)
                    dve.wait_ge(turned, 2 * (g + 1))
                    dve.tensor_copy(src_T[:, g * P:(g + 1) * P], ptr[:, s, 0]).then_inc(used, 1)
                    dve.tensor_copy(dst_T[:, g * P:(g + 1) * P], ptr[:, s, 1]).then_inc(used, 1)

            @block.gpsimd
            def _(pool):
                pool.wait_ge(fetched, 1)
                for g in range(groups):
                    s = g % 2
                    if g >= 2:
                        pool.wait_ge(split, 2 * (g - 1))
                    pool.indirect_dma_start(out=rows[:, s].rearrange("p a b -> p (a b)"), out_offset=None, in_=pairs,
                                            in_offset=bass.IndirectOffsetOnAxis(ap=first_i[:, g:g + 1], axis=0)
                                            ).then_inc(fetch[s], 16)

            @block.tensor
            def _(pe):
                for g in range(groups):
                    s = g % 2
                    pe.wait_ge(split, 2 * (g + 1))
                    if g >= 2:
                        pe.wait_ge(used, 2 * (g - 1))
                    for a in range(2):
                        pe.transpose(ptr[:, s, a], cols[:, s, a], K.ident[:]).then_inc(turned, 1)

            @block.sync
            def _(sp):
                sp.wait_ge(fetched, 1)
                with nc.allow_non_contiguous_dma(reason="a small table"):
                    sp.dma_start(tile_dram.rearrange("(g p) -> p g", p=P), tile_i[:]).then_inc(out_s, 16)
                sp.wait_ge(out_s, 16)
                sp.dma_start(tile_row[:], tile_dram.rearrange("(a s) -> a s", a=1)).then_inc(out_s, 16)
                sp.wait_ge(out_s, 32)


def load_edges(nc, m, K, A):
    K.gat_pay = m.sb("gat_pay", [P, GAT_C, 2], I32)
    K.gat_tile = m.sb("gat_tile", [P, GAT_C], BF16)
    K.gcn_pay = m.sb("gcn_pay", [P, GCN_C, 2], I32)
    K.gcn_tile = m.sb("gcn_tile", [P, GCN_C], BF16)
    K.gcn_node = m.sb("gcn_node", [P, GCN_C], BF16)
    with ExitStack() as ctx:
        m = Mem(nc, ctx)
        raw = m.sb("raw", [P, 2, GCN_C], I32)
        raw2 = m.sb("raw2", [P, 2, GAT_C], I32)
        ti = m.sb("ti", [P, GCN_C], I32)
        tail = m.sb("tail", [P, 2], I32)
        copied = m.sem("le_copied")
        loaded, chain, out_s, pad = m.sem("le_loaded"), m.sem("le_chain"), m.sem("le_out"), m.sem("le_pad")
        c = GCN_P
        with nc.Block() as block:
            @block.sync
            def _(sp):
                sp.dma_start(raw[0:c, 0], A.src.rearrange("(p c) -> p c", p=c)).then_inc(loaded, 16)
                sp.dma_start(raw[0:c, 1], A.dst.rearrange("(p c) -> p c", p=c)).then_inc(loaded, 16)
                sp.dma_start(raw2[:, 0], A.edge_index[0].rearrange("(p c) -> p c", p=P)).then_inc(loaded, 16)
                sp.dma_start(raw2[:, 1], A.edge_index[1].rearrange("(p c) -> p c", p=P)).then_inc(loaded, 16)
                sp.wait_ge(pad, 1)
                sp.dma_start(K.gcn_pairs[E_GCN:E_GCN + P], tail[:]).then_inc(out_s, 16)
                sp.dma_start(K.gat_pairs[E_GAT:E_GAT + P], tail[:]).then_inc(out_s, 16)
                sp.wait_ge(out_s, 32)

            @block.gpsimd
            def _(pool):
                pool.memset(tail[:, 0:1], 0).then_inc(chain, 1)
                pool.memset(tail[:, 1:2], -1).then_inc(chain, 1)
                pool.wait_ge(chain, 2)
                pool.sem_inc(pad, 1)
                pool.wait_ge(loaded, 64)
                for a in range(2):
                    pool.tensor_copy(K.gat_pay[:, :, a], raw2[:, a]).then_inc(chain, 1)

            @block.scalar
            def _(act):
                act.wait_ge(loaded, 64)
                for a in range(2):
                    act.copy(K.gcn_pay[0:c, :, a], raw[0:c, a]).then_inc(copied, 1)

            @block.vector
            def _(dve):
                n = [0]
                dv = m.sem("le_dve")

                def done(ins):
                    n[0] += 1
                    ins.then_inc(dv, 1)
                    dve.wait_ge(dv, n[0])

                dve.wait_ge(loaded, 64)
                scale, bias = 1.0 / TN, 0.5 / TN - 0.5
                done(dve.tensor_scalar(ti[0:c], raw[0:c, 1], scale, bias, ALU.mult, ALU.add))
                done(dve.tensor_copy(K.gcn_tile[0:c], ti[0:c]))
                done(dve.scalar_tensor_tensor(K.gcn_node[0:c], ti[0:c], -float(TN), raw[0:c, 1], ALU.mult, ALU.add))
                done(dve.tensor_scalar(ti[:, 0:GAT_C], raw2[:, 1], scale, bias, ALU.mult, ALU.add))
                done(dve.tensor_copy(K.gat_tile[:], ti[:, 0:GAT_C]))


def degrees(nc, K, A):
    HB = 16
    rounds = GCN_C // HB
    with ExitStack() as ctx:
        m = Mem(nc, ctx)
        on = m.sb("on", [P, 2, HB, TN], BF16)
        ot = m.sb("ot", [P, 2, HB, NT], BF16)
        pdeg = m.ps("pdeg", [P, NT])
        xin = m.sb("dx_in", [P, 2, SUB, D])
        st6 = m.sb("dx_st", [P, SUB, 6])
        mv = m.sb("dx_mv", [P, SUB, 2])
        var = m.sb("dx_var", [P, NT, 2])
        node_s, tile_s, used, done_s, chain, root, x_free, kept = (m.sem("dg_" + x) for x in (
            "node", "tile", "used", "done", "chain", "root", "x_free", "kept"))
        xl = [m.sem(f"dg_xl{s}") for s in range(2)]
        c = GCN_P
        with nc.Block() as block:
            def onehot(eng, out, ids, width, i, s, sem):
                k = i * 2 + s
                eng.wait_ge(used, i * 2 + s)
                shape = [c, HB, width]
                eng.tensor_tensor(out[0:c, s], K.iota_h[0:c, 0:width].unsqueeze(1).to_broadcast(shape),
                                  ids[0:c, bass.ds(k * HB, HB)].unsqueeze(2).to_broadcast(shape),
                                  ALU.is_equal).then_inc(sem, 1)

            @block.sync
            def _(sp):
                def body(k, i, s):
                    sp.wait_ge(x_free, k + 1)
                    for p0, p1 in ((0, 120), (120, TN)):
                        sp.dma_start(xin[p0:p1, s],
                                     A.x[bass.ds(k * BN, BN)].rearrange("(j p) f -> p j f", p=TN)[p0:p1]
                                     ).then_inc(xl[s], 16)
                blocks(sp, body)

            @block.tensor
            def _(pe):
                def body(i, s, first, last):
                    pe.wait_ge(node_s, i * 2 + s + 1)
                    pe.wait_ge(tile_s, i * 2 + s + 1)
                    for b in range(HB):
                        mm = pe.matmul(pdeg[0:TN], on[0:c, s, b], ot[0:c, s, b],
                                       start=first and b == 0, stop=last and b == HB - 1)
                    mm.then_inc(used, 1)
                pe.sem_inc(used, 1)
                body(0, 0, True, False)
                body(0, 1, False, False)
                with pe.Fori(1, rounds // 2 - 1) as i:
                    body(i, 0, False, False)
                    body(i, 1, False, False)
                body(rounds // 2 - 1, 0, False, False)
                body(rounds // 2 - 1, 1, False, True)

            @block.vector
            def _(dve):
                def stats(k, i, s):
                    dve.wait_ge(xl[s], i * 32 + 32)
                    for j in range(SUB):
                        dve.bn_stats(st6[0:TN, j], xin[0:TN, s, j]).then_inc(chain, 1)
                    dve.wait_ge(chain, k * (2 * SUB) + SUB)
                    dve.sem_inc(x_free, 1)
                    for j in range(SUB):
                        dve.bn_aggr(mv[0:TN, j], st6[0:TN, j]).then_inc(chain, 1)
                    dve.wait_ge(chain, k * (2 * SUB) + 2 * SUB)
                    dve.tensor_copy(K.xmv[0:TN, bass.ds(k * SUB, SUB), :], mv[0:TN]).then_inc(kept, 1)
                dve.sem_inc(x_free, 2)
                blocks(dve, stats)
                with dve.Fori(0, rounds // 2) as i:
                    for s in range(2):
                        onehot(dve, on, K.gcn_node, TN, i, s, node_s)
                        onehot(dve, ot, K.gcn_tile, NT, i, s, tile_s)
                dve.wait_ge(kept, NB)
                dve.wait_ge(used, rounds + 1)
                dve.tensor_scalar(var[0:TN, :, 0], K.xmv[0:TN, :, 1], EPS, None, ALU.add).then_inc(done_s, 1)
                dve.tensor_scalar(var[0:TN, :, 1], pdeg[0:TN], 1.0, None, ALU.add).then_inc(done_s, 1)
                dve.wait_ge(root, 1)
                dve.reciprocal(var[0:TN], var[0:TN]).then_inc(done_s, 1)
                dve.wait_ge(done_s, 3)
                dve.tensor_copy(K.xrs[0:TN], var[0:TN, :, 0]).then_inc(done_s, 1)
                dve.tensor_copy(K.dinv[0:TN], var[0:TN, :, 1]).then_inc(done_s, 1)

            @block.scalar
            def _(act):
                act.wait_ge(done_s, 2)
                act.activation(var[0:TN], var[0:TN], ACT.Sqrt).then_inc(root, 1)


def dense_first(nc, K, A):
    with ExitStack() as ctx:
        m = Mem(nc, ctx)
        w1T = m.sb("w1T", [P, KC, D])
        wq = m.sb("wq", [P, KC, D])
        wkv = m.sb("wkv", [P, KC, 2, D])
        b1c = m.sb("b1c", [P, KC])
        bqc = m.sb("bqc", [P, KC])
        bkv = m.sb("bkv", [P, 2, D])
        xin = m.sb("a_xin", [P, 2, SUB, D])
        xn = m.sb("a_xn", [P, 2, SUB, D])
        xnT = m.sb("a_xnT", [P, 2, KC, BN])
        hT = m.sb("a_hT", [P, 2, KC, BN])
        qT = m.sb("a_qT", [P, 2, KC, BN])
        qm = m.sb("a_qm", [P, KC, BN])
        kb = m.sb("a_kb", [P, 2, D])
        km = m.sb("a_km", [P, 2, D])
        ve = m.sb("a_ve", [P, 2, KC, P + 1])
        stats = m.sb("a_stats", [P, KC, NB, 6])
        hst = m.sb("a_hst", [P, KC, 6])
        ptr = m.ps("a_ptr", [P, KC, 512])
        pqh = m.ps("a_pqh", [P, KC, 512])
        pkv = m.ps("a_pkv", [P, 2, 512])
        pacc = m.ps("a_pacc", [P, KC, 512])
        S = {n: m.sem("a_" + n) for n in (
            "w", "ones", "x_free", "xn", "turned", "xnT", "q", "q_min", "q_sb", "q_exp", "q_sum", "h", "h_sb",
            "h_stat", "kv", "kb", "v", "k_min", "k_exp", "k_sum", "acc", "agg", "mean")}
        x_in = [m.sem(f"a_x_in{s}") for s in range(2)]
        stored = [m.sem(f"a_stored{s}") for s in range(2)]
        with nc.Block() as block:
            @block.sync
            def _(sp):
                sp.dma_start(w1T[:], A.w1T.rearrange("(c p) o -> p c o", p=P)).then_inc(S["w"], 16)
                sp.dma_start(wq[:], A.wq.rearrange("(c p) o -> p c o", p=P)).then_inc(S["w"], 16)
                sp.dma_start(wkv[:, :, 0], A.wk.rearrange("(c p) o -> p c o", p=P)).then_inc(S["w"], 16)
                sp.dma_start(wkv[:, :, 1], A.wv.rearrange("(c p) o -> p c o", p=P)).then_inc(S["w"], 16)
                with nc.allow_non_contiguous_dma(reason="biases"):
                    sp.dma_start(b1c[:], A.b1.rearrange("(c p) -> p c", p=P)).then_inc(S["w"], 16)
                    sp.dma_start(bqc[:], A.bq.rearrange("(c p) -> p c", p=P)).then_inc(S["w"], 16)
                sp.dma_start(bkv[:, 0], A.bk.rearrange("(a o) -> a o", a=1).to_broadcast([P, D])).then_inc(S["w"], 16)
                sp.dma_start(bkv[:, 1], A.bv.rearrange("(a o) -> a o", a=1).to_broadcast([P, D])).then_inc(S["w"], 16)

                def load(k, i, s):
                    sp.wait_ge(S["x_free"], k + 1)
                    for p0, p1 in ((0, 120), (120, TN)):
                        sp.dma_start(xin[p0:p1, s], A.x[bass.ds(k * BN, BN)].rearrange("(j p) f -> p j f", p=TN)[p0:p1]
                                     ).then_inc(x_in[s], 16)

                def store(k, i, s):
                    sp.wait_ge(S["h_sb"], k * 2 + 2)
                    sp.dma_start(K.hT_d[bass.ds(k, 1)].rearrange("a p c n -> p (a c) n"), hT[:, s]
                                 ).then_inc(stored[s], 16)
                    sp.wait_ge(S["q_sum"], k * 2 + 2)
                    sp.dma_start(K.qT_d[bass.ds(k, 1)].rearrange("a p c n -> p (a c) n"), qT[:, s]
                                 ).then_inc(stored[s], 16)

                load(0, 0, 0)
                load(1, 0, 1)
                with sp.Fori(0, (NB - 3) // 2) as i:
                    for s in range(2):
                        load(i * 2 + 2 + s, i + 1, s)
                        store(i * 2 + s, i, s)
                load(NB - 1, 0, 0)
                store(NB - 3, 0, 0)
                store(NB - 2, 0, 1)
                store(NB - 1, 0, 0)
                sp.wait_ge(stored[0], 32 * (NB // 2 + 1))
                sp.wait_ge(stored[1], 32 * (NB // 2))

            @block.tensor
            def _(pe):
                def project(w, s, sem):
                    for o in range(KC):
                        for c in range(KC):
                            mm = pe.matmul(pqh[:, o, 0:BN], w[:, c, o * P:(o + 1) * P], xnT[:, s, c],
                                           start=c == 0, stop=c == KC - 1)
                        mm.then_inc(sem, 1)

                def kv(k, s, j):
                    pe.wait_ge(S["v"], k * SUB + j)
                    for c in range(KC):
                        mm = pe.matmul(pkv[0:TN, j % 2], xnT[:, s, c, j * TN:(j + 1) * TN],
                                       wkv[:, c].rearrange("p a o -> p (a o)"), start=c == 0, stop=c == KC - 1)
                    mm.then_inc(S["kv"], 1)

                def accumulate(k, j, first, last):
                    pe.wait_ge(S["k_sum"], k * SUB + j + 1)
                    for c in range(KC):
                        mm = pe.matmul(pacc[:, c, 0:P + 1], km[0:TN, j % 2, c * P:(c + 1) * P], ve[0:TN, j % 2, c],
                                       start=first and j == 0, stop=last and j == SUB - 1)
                    mm.then_inc(S["acc"], 1)

                def body(k, s, first=False, last=False):
                    pe.wait_ge(S["xnT"], k * KC + KC)
                    pe.wait_ge(S["h_sb"], k * KC)
                    project(wq, s, S["q"])
                    kv(k, s, 0)
                    kv(k, s, 1)
                    pe.wait_ge(S["q_sb"], k * KC + KC)
                    project(w1T, s, S["h"])
                    if not last:
                        transposes_next(k, s)
                    accumulate(k, 0, first, last)
                    kv(k, s, 2)
                    accumulate(k, 1, first, last)
                    kv(k, s, 3)
                    accumulate(k, 2, first, last)
                    accumulate(k, 3, first, last)

                def transposes_next(k, s):
                    pe.wait_ge(S["xn"], k * SUB + 2 * SUB)
                    pe.wait_ge(S["xnT"], k * KC + KC)
                    turn(1 - s)

                def turn(s):
                    for c in range(KC):
                        for j in range(SUB):
                            mm = pe.transpose(ptr[:, c, j * TN:(j + 1) * TN], xn[0:TN, s, j, c * P:(c + 1) * P],
                                              K.ident[0:TN, 0:TN])
                        mm.then_inc(S["turned"], 1)

                pe.wait_ge(S["w"], 16 * 8)
                pe.wait_ge(S["ones"], 1)
                pe.wait_ge(S["xn"], SUB)
                turn(0)
                body(0, 0, first=True)
                body(1, 1)
                with pe.Fori(1, NB // 2) as i:
                    body(i * 2, 0)
                    body(i * 2 + 1, 1)
                body(NB - 1, 0, last=True)

            @block.scalar
            def _(act):
                def turned(k, s):
                    act.wait_ge(S["turned"], k * KC + KC)
                    for c in range(KC):
                        act.copy(xnT[:, s, c], ptr[:, c, 0:BN]).then_inc(S["xnT"], 1)

                def body(k, i, s, last=False):
                    act.wait_ge(stored[s], i * 32)
                    for c in range(KC):
                        act.wait_ge(S["q"], k * KC + c + 1)
                        act.activation(qT[:, s, c], pqh[:, c, 0:BN], ACT.Identity, bias=bqc[:, c:c + 1]
                                       ).then_inc(S["q_sb"], 1)
                    for c in range(KC):
                        act.wait_ge(S["q_min"], k * KC + c + 1)
                        act.activation(qm[:, c], qm[:, c], ACT.Exp).then_inc(S["q_exp"], 1)
                    k_exp(k, 0)
                    k_exp(k, 1)
                    for c in range(KC):
                        act.wait_ge(S["h"], k * KC + c + 1)
                        act.activation(hT[:, s, c], pqh[:, c, 0:BN], ACT.Identity, bias=b1c[:, c:c + 1]
                                       ).then_inc(S["h_sb"], 1)
                    if not last:
                        turned(k + 1, 1 - s)
                    k_exp(k, 2)
                    k_exp(k, 3)

                def k_exp(k, j):
                    act.wait_ge(S["k_min"], k * SUB + j + 1)
                    act.activation(km[0:TN, j % 2], km[0:TN, j % 2], ACT.Exp).then_inc(S["k_exp"], 1)

                act.wait_ge(S["w"], 16 * 8)
                turned(0, 0)
                with act.Fori(0, NB // 2) as i:
                    body(i * 2, i, 0)
                    body(i * 2 + 1, i, 1)
                body(NB - 1, NB // 2, 0, last=True)

            @block.vector
            def _(dve):
                def normalise(k, i, s):
                    dve.wait_ge(x_in[s], i * 32 + 32)
                    dve.wait_ge(S["turned"], i * (2 * KC))
                    for j in range(SUB):
                        t = k * SUB + j
                        ins = dve.tensor_scalar(xn[0:TN, s, j], xin[0:TN, s, j], K.xmv[0:TN, bass.ds(t, 1), 0],
                                                K.xrs[0:TN, bass.ds(t, 1)], ALU.subtract, ALU.mult)
                        ins.then_inc(S["xn"], 1)
                    dve.wait_ge(S["xn"], k * SUB + SUB)
                    dve.sem_inc(S["x_free"], 1)

                def k_part(k, j):
                    s = j % 2
                    dve.wait_ge(S["kv"], k * SUB + j + 1)
                    if j >= 2:
                        dve.wait_ge(S["acc"], k * SUB + j - 1)
                    else:
                        dve.wait_ge(S["acc"], k * SUB)
                    dve.tensor_tensor(kb[0:TN, s], pkv[0:TN, s, 0:D], bkv[0:TN, 0], ALU.add).then_inc(S["kb"], 1)
                    dve.tensor_tensor(ve[0:TN, s, :, 0:P], pkv[0:TN, s, D:2 * D].rearrange("p (c e) -> p c e", c=KC),
                                      bkv[0:TN, 1].rearrange("p (c e) -> p c e", c=KC), ALU.add).then_inc(S["v"], 1)
                    dve.wait_ge(S["kb"], k * SUB + j + 1)
                    dve.tensor_scalar(km[0:TN, s], kb[0:TN, s], 0.0, None, ALU.min).then_inc(S["k_min"], 1)

                def k_sum(k, j):
                    s = j % 2
                    dve.wait_ge(S["k_exp"], k * SUB + j + 1)
                    dve.scalar_tensor_tensor(km[0:TN, s], kb[0:TN, s], 0.0, km[0:TN, s], ALU.max, ALU.add
                                             ).then_inc(S["k_sum"], 1)

                def body(k, i, s, last=False):
                    dve.wait_ge(S["q_sum"], k * KC)
                    for c in range(KC):
                        dve.wait_ge(S["q_sb"], k * KC + c + 1)
                        dve.tensor_scalar(qm[:, c], qT[:, s, c], 0.0, None, ALU.min).then_inc(S["q_min"], 1)
                    if not last:
                        normalise(k + 1, *((i, 1) if s == 0 else (i + 1, 0)))
                    k_part(k, 0)
                    k_part(k, 1)
                    for c in range(KC):
                        dve.wait_ge(S["q_exp"], k * KC + c + 1)
                        dve.scalar_tensor_tensor(qT[:, s, c], qT[:, s, c], 0.0, qm[:, c], ALU.max, ALU.add
                                                 ).then_inc(S["q_sum"], 1)
                    k_sum(k, 0)
                    k_sum(k, 1)
                    for c in range(KC):
                        dve.wait_ge(S["h_sb"], k * KC + c + 1)
                        dve.bn_stats(hst[:, c], hT[:, s, c]).then_inc(S["h_stat"], 1)
                    dve.wait_ge(S["h_stat"], k * KC + KC)
                    dve.tensor_copy(stats[:, :, bass.ds(k, 1), :].rearrange("p c a b -> p c (a b)"), hst[:]).then_inc(S["agg"], 1)
                    dve.wait_ge(S["agg"], k + 1)
                    k_part(k, 2)
                    k_sum(k, 2)
                    k_part(k, 3)
                    k_sum(k, 3)

                dve.memset(ve[:, :, :, P:P + 1], 1.0).then_inc(S["ones"], 1)
                dve.sem_inc(S["x_free"], 2)
                dve.sem_inc(S["v"], 1)
                dve.wait_ge(S["w"], 16 * 8)
                dve.wait_ge(S["ones"], 1)
                normalise(0, 0, 0)
                with dve.Fori(0, NB // 2) as i:
                    body(i * 2, i, 0)
                    body(i * 2 + 1, i, 1)
                body(NB - 1, NB // 2, 0, last=True)
                for c in range(KC):
                    dve.bn_aggr(K.hmv[:, c], stats[:, c].rearrange("p n s -> p (n s)")).then_inc(S["mean"], 1)
                dve.wait_ge(S["acc"], NT)
                dve.tensor_copy(K.kv[:], pacc[:, :, 0:P + 1]).then_inc(S["mean"], 1)
                dve.wait_ge(S["mean"], 3)


def dense_second(nc, K, A):
    with ExitStack() as ctx:
        m = Mem(nc, ctx)
        w2 = m.sb("w2", [P, KC, D])
        wgT = m.sb("wgT", [P, KC, D])
        wo = m.sb("wo", [P, KC, D])
        gb = m.sb("gb", [P, 2, KC])
        b2c = m.sb("b2c", [P, KC])
        rows_b = m.sb("rows_b", [P, 2, D])
        W = m.sb("w_both", [P, KC, D])
        bW = m.sb("b_both", [P, D])
        kvm = m.sb("kvm", [P, KC, P])
        kvT = m.sb("kvT", [P, KC, P])
        kvw = m.sb("kvw", [P, KC, D])
        Z = m.sb("zmat", [P, KC, P])
        b2r = m.sb("b2r", [P, KC, P])
        bn = m.sb("bn", [P, KC, 4])
        scale, shift = m.sb("bn_scale", [P, KC]), m.sb("bn_shift", [P, KC])
        hT = m.sb("b_hT", [P, 2, KC, BN])
        qT = m.sb("b_qT", [P, 2, KC, BN])
        xin = m.sb("b_xin", [P, 2, SUB, D])
        pre = m.sb("b_pre", [P, 2, SUB, D])
        tmp = m.sb("b_tmp", [P, SUB, D])
        rz = m.sb("b_rz", [P, KC, BN])
        pz = m.ps("b_pz", [P, KC, 512])
        px = m.ps("b_px", [P, SUB, D])
        pm = m.ps("b_pm", [P, SUB, D])
        pw = m.ps("b_pw", [P, 512])
        S = {n: m.sem("b_" + n) for n in (
            "w", "v", "root", "p", "z", "rz", "qs", "relu", "px", "tmp", "acc", "pm", "pre", "in_free")}
        l_in = [m.sem(f"b_in{s}") for s in range(2)]
        tab_s = [m.sem(f"b_tab{s}") for s in range(2)]
        pre_s = [m.sem(f"b_pre_s{s}") for s in range(2)]
        with nc.Block() as block:
            @block.sync
            def _(sp):
                for t, a in ((w2, A.w2), (wgT, A.wgT), (wo, A.wo)):
                    sp.dma_start(t[:], a.rearrange("(c p) o -> p c o", p=P)).then_inc(S["w"], 16)
                with nc.allow_non_contiguous_dma(reason="biases"):
                    for t, a in ((gb[:, 0], A.gamma), (gb[:, 1], A.beta), (b2c[:], A.b2)):
                        sp.dma_start(t, a.rearrange("(c p) -> p c", p=P)).then_inc(S["w"], 16)
                for n, a in enumerate((A.bo, A.b_gcn)):
                    sp.dma_start(rows_b[:, n], a.rearrange("(a o) -> a o", a=1).to_broadcast([P, D])
                                 ).then_inc(S["w"], 16)

                def load(k, i, s):
                    sp.wait_ge(S["in_free"], k + 1)
                    sp.dma_start(hT[:, s], K.hT_d[bass.ds(k, 1)].rearrange("a p c n -> p (a c) n")).then_inc(l_in[s], 16)
                    sp.dma_start(qT[:, s], K.qT_d[bass.ds(k, 1)].rearrange("a p c n -> p (a c) n")).then_inc(l_in[s], 16)
                    for p0, p1 in ((0, 120), (120, TN)):
                        sp.dma_start(xin[p0:p1, s], A.x[bass.ds(k * BN, BN)].rearrange("(j p) f -> p j f", p=TN)[p0:p1]
                                     ).then_inc(l_in[s], 16)

                def store(k, i, s):
                    sp.wait_ge(S["acc"], k * SUB + SUB)
                    for p0, p1 in ((0, 120), (120, TN)):
                        sp.dma_start(K.table[bass.ds(k * BN, BN)].rearrange("(j p) f -> p j f", p=TN)[p0:p1],
                                     K.acc[p0:p1, bass.ds(k * SUB, SUB), :]).then_inc(tab_s[s], 16)
                    sp.wait_ge(S["pre"], k * (2 * SUB) + 2 * SUB)
                    for p0, p1 in ((0, 120), (120, TN)):
                        sp.dma_start(K.pre_d[bass.ds(k, 1)].rearrange("a p j f -> p (a j) f")[p0:p1],
                                     pre[p0:p1, s]).then_inc(pre_s[s], 16)

                load(0, 0, 0)
                load(1, 0, 1)
                with sp.Fori(0, (NB - 3) // 2) as i:
                    for s in range(2):
                        load(i * 2 + 2 + s, i + 1, s)
                        store(i * 2 + s, i, s)
                load(NB - 1, 0, 0)
                store(NB - 3, 0, 0)
                store(NB - 2, 0, 1)
                store(NB - 1, 0, 0)
                for s in range(2):
                    sp.wait_ge(tab_s[s], 32 * ((NB + 1 - s) // 2))
                    sp.wait_ge(pre_s[s], 32 * ((NB + 1 - s) // 2))

            @block.tensor
            def _(pe):
                pe.wait_ge(S["w"], 16 * 8)
                for b in range(KC):
                    for a in range(KC):
                        mm = pe.matmul(pw[:, b * D:(b + 1) * D], w2[:, a, b * P:(b + 1) * P], wgT[:, a],
                                       start=a == 0, stop=a == KC - 1, skip_group_check=True)
                mm.then_inc(S["p"], 1)
                pe.wait_ge(S["v"], 4)
                for c in range(KC):
                    mm = pe.transpose(pz[:, 0, c * P:(c + 1) * P], kvm[:, c], K.ident[:])
                mm.then_inc(S["p"], 1)
                for a in range(KC):
                    mm = pe.matmul(pz[:, 1, 0:D], b2r[:, a], wgT[:, a], start=a == 0, stop=a == KC - 1)
                mm.then_inc(S["p"], 1)
                pe.wait_ge(S["v"], 7)
                for c in range(KC):
                    mm = pe.matmul(pw[:, c * D:(c + 1) * D], kvT[:, c], wo[:, c], start=True, stop=True,
                                   skip_group_check=True)
                mm.then_inc(S["p"], 1)
                pe.wait_ge(S["v"], 8)

                def body(k, i, s):
                    pe.wait_ge(l_in[s], i * 64 + 64)
                    pe.wait_ge(S["rz"], k * KC)
                    for c in range(KC):
                        pe.matmul(pz[:, c, 0:BN], Z[:, c], qT[:, s, c], start=True, stop=True).then_inc(S["z"], 1)
                    pe.wait_ge(S["relu"], k * KC + KC)
                    pe.wait_ge(S["tmp"], k * SUB)
                    for j in range(SUB):
                        for c in range(KC):
                            mm = pe.matmul(px[0:TN, j], hT[:, s, c, j * TN:(j + 1) * TN], W[:, c],
                                           start=c == 0, stop=c == KC - 1, skip_group_check=True)
                        mm.then_inc(S["px"], 1)
                    pe.wait_ge(S["qs"], k * KC + KC)
                    pe.wait_ge(S["pre"], k * (2 * SUB))
                    for j in range(SUB):
                        for c in range(KC):
                            mm = pe.matmul(pm[0:TN, j], qT[:, s, c, j * TN:(j + 1) * TN], kvw[:, c],
                                           start=c == 0, stop=c == KC - 1, skip_group_check=True)
                        mm.then_inc(S["pm"], 1)
                blocks(pe, body)

            @block.scalar
            def _(act):
                act.wait_ge(S["v"], 5)
                act.activation(bn[:, :, 1], bn[:, :, 0], ACT.Sqrt).then_inc(S["root"], 1)
                act.wait_ge(S["v"], 8)

                def body(k, i, s):
                    act.wait_ge(l_in[s], i * 64 + 64)
                    for c in range(KC):
                        act.activation(hT[:, s, c], hT[:, s, c], ACT.Relu, bias=shift[:, c:c + 1],
                                       scale=scale[:, c:c + 1]).then_inc(S["relu"], 1)
                    for j in range(SUB):
                        t = k * SUB + j
                        act.wait_ge(S["tmp"], k * SUB + j + 1)
                        act.activation(K.acc[0:TN, bass.ds(t, 1), :].rearrange("p a f -> p (a f)"), tmp[0:TN, j],
                                       ACT.Copy, scale=K.dinv[0:TN, bass.ds(t, 1)]).then_inc(S["acc"], 1)
                blocks(act, body)

            @block.vector
            def _(dve):
                dve.wait_ge(S["w"], 16 * 8)
                for c in range(KC):
                    dve.tensor_tensor(kvm[:, c], K.kv[:, c, 0:P], K.head[:], ALU.mult).then_inc(S["v"], 1)
                for c in range(KC):
                    dve.tensor_scalar(b2r[:, c], K.ones[:], b2c[:, c:c + 1], None, ALU.mult).then_inc(S["v"], 1)
                dve.tensor_scalar(bn[:, :, 0], K.hmv[:, :, 1], EPS, None, ALU.add).then_inc(S["v"], 1)
                dve.wait_ge(S["p"], 3)
                dve.tensor_copy(W[:].rearrange("p c f -> p (c f)"), pw[:]).then_inc(S["v"], 1)
                dve.tensor_copy(kvT[:].rearrange("p c f -> p (c f)"), pz[:, 0, 0:KC * P]).then_inc(S["v"], 1)
                u = m.sem("b_u")
                for c in range(KC):
                    dve.tensor_scalar(Z[:, c], K.head[:], K.kv[:, c, P:P + 1], None, ALU.mult).then_inc(u, 1)
                dve.tensor_copy(bW[:], pz[:, 1, 0:D]).then_inc(u, 1)
                dve.tensor_tensor(rows_b[:, 0], rows_b[:, 0], rows_b[:, 1], ALU.add).then_inc(u, 1)
                dve.wait_ge(S["root"], 1)
                dve.reciprocal(bn[:, :, 2], bn[:, :, 1]).then_inc(u, 1)
                dve.wait_ge(u, 5)
                dve.tensor_tensor(scale[:], bn[:, :, 2], gb[:, 0], ALU.mult).then_inc(u, 1)
                dve.wait_ge(u, 6)
                dve.tensor_tensor(bn[:, :, 3], K.hmv[:, :, 0], scale[:], ALU.mult).then_inc(u, 1)
                dve.wait_ge(u, 7)
                dve.tensor_tensor(shift[:], gb[:, 1], bn[:, :, 3], ALU.subtract).then_inc(u, 1)
                dve.wait_ge(u, 8)
                dve.wait_ge(S["p"], 4)
                dve.tensor_copy(kvw[:].rearrange("p c f -> p (c f)"), pw[:]).then_inc(S["v"], 1)
                dve.sem_inc(S["in_free"], 2)
                dve.wait_ge(S["v"], 8)

                def body(k, i, s):
                    for c in range(KC):
                        dve.wait_ge(S["z"], k * KC + c + 1)
                        dve.tensor_scalar(rz[:, c], pz[:, c, 0:BN], 1e-6, None, ALU.add).then_inc(S["rz"], 1)
                    dve.wait_ge(S["rz"], k * KC + KC)
                    for c in range(KC):
                        dve.reciprocal(rz[:, c], rz[:, c]).then_inc(r2, 1)
                    dve.wait_ge(r2, k * KC + KC)
                    for c in range(KC):
                        dve.tensor_tensor(qT[:, s, c], qT[:, s, c], rz[:, c], ALU.mult).then_inc(S["qs"], 1)
                    dve.wait_ge(S["acc"], k * SUB)
                    for j in range(SUB):
                        if j % 2 == 0:
                            dve.wait_ge(S["px"], k * SUB + j + 2)
                        dve.tensor_tensor(tmp[0:TN, j], px[0:TN, j], bW[0:TN], ALU.add).then_inc(S["tmp"], 1)
                    dve.wait_ge(pre_s[s], i * 32)
                    for j in range(SUB):
                        dve.tensor_tensor(pre[0:TN, s, j], xin[0:TN, s, j], rows_b[0:TN, 0], ALU.add
                                          ).then_inc(S["pre"], 1)
                    dve.wait_ge(S["pre"], k * (2 * SUB) + SUB)
                    for j in range(SUB):
                        if j % 2 == 0:
                            dve.wait_ge(S["pm"], k * SUB + j + 2)
                        dve.tensor_tensor(pre[0:TN, s, j], pre[0:TN, s, j], pm[0:TN, j], ALU.add
                                          ).then_inc(S["pre"], 1)
                    dve.wait_ge(S["pre"], k * (2 * SUB) + 2 * SUB)
                    dve.sem_inc(S["in_free"], 1)
                r2 = m.sem("b_r2")
                blocks(dve, body)


def gather_sum(nc, K):
    W = BATCH
    rounds = S_GCN // (W * HALVES)
    with ExitStack() as ctx:
        m = Mem(nc, ctx)
        at = m.sb("g_at", [P, HALVES, W], U32)
        rows = m.sb("g_rows", [P, HALVES, W, D])
        hot = m.sb("g_hot", [P, HALVES, W, TN])
        ps = m.ps("g_ps", [P, HALVES, W, D])
        at_s, hot_s, mm_s, add_s, passed = (m.sem("g_" + x) for x in ("at", "hot", "mm", "add", "passed"))
        got = [m.sem(f"g_got{h}") for h in range(HALVES)]
        with nc.Block() as block:
            @block.scalar
            def _(act):
                with act.Fori(0, rounds) as i:
                    for h in range(HALVES):
                        act.wait_ge(got[h], i * (16 * W))
                        act.copy(at[:, h], K.gcn_srcT[:, bass.ds((i * HALVES + h) * W, W)]).then_inc(at_s, 1)

            @block.gpsimd
            def _(pool):
                with pool.Fori(0, rounds) as i:
                    for h in range(HALVES):
                        pool.wait_ge(at_s, i * HALVES + h + 1)
                        pool.wait_ge(mm_s, (i * HALVES + h) * W)
                        pool.sem_inc(passed, 1)
                        for b in range(W):
                            pool.indirect_dma_start(
                                out=rows[:, h, b], out_offset=None, in_=K.table,
                                in_offset=bass.IndirectOffsetOnAxis(ap=at[:, h, b:b + 1], axis=0)
                            ).then_inc(got[h], 16)

            @block.tensor
            def _(pe):
                pe.sem_inc(mm_s, W)
                with pe.Fori(0, rounds) as i:
                    for h in range(HALVES):
                        pe.wait_ge(hot_s, i * HALVES + h + 1)
                        pe.wait_ge(got[h], (i + 1) * (16 * W))
                        for b in range(W):
                            if b % 2 == 0:
                                pe.wait_ge(add_s, (i * HALVES + h) * W + b + 2)
                            pe.matmul(ps[0:TN, h, b], hot[:, h, b], rows[:, h, b], start=True, stop=True,
                                      skip_group_check=True).then_inc(mm_s, 1)

            @block.vector
            def _(dve):
                dve.sem_inc(add_s, HALVES * W)
                with dve.Fori(0, rounds) as i:
                    for h in range(HALVES):
                        dve.wait_ge(mm_s, (i * HALVES + h) * W)
                        shape = [P, W, TN]
                        dve.tensor_tensor(hot[:, h], K.iota[:, 0:TN].unsqueeze(1).to_broadcast(shape),
                                          K.gcn_dstT[:, bass.ds((i * HALVES + h) * W, W)].unsqueeze(2).to_broadcast(shape),
                                          ALU.is_equal).then_inc(hot_s, 1)
                        for b in range(W):
                            n = (i * HALVES + h) * W + b
                            t = dve.value_load(K.gcn_tiles[0:1, bass.ds(n, 1)], min_val=0, max_val=NT - 1)
                            a = K.acc[0:TN, bass.ds(t, 1), :].rearrange("p a f -> p (a f)")
                            if b % 2 == 0:
                                dve.wait_ge(mm_s, n + W + 2)
                            dve.wait_ge(add_s, n + HALVES * W)
                            dve.tensor_tensor(a, a, ps[0:TN, h, b], ALU.add).then_inc(add_s, 1)


def second_norm(nc, K, A):
    with ExitStack() as ctx:
        m = Mem(nc, ctx)
        wg = m.sb("wg", [P, KC, GW])
        att = m.sb("att", [P, 2, GW])
        pre = m.sb("c_pre", [P, 2, SUB, D])
        x1 = m.sb("c_x1", [P, 2, SUB, D])
        xf = m.sb("c_xf", [P, 2, SUB, D])
        xfT = m.sb("c_xfT", [P, 2, KC, BN])
        st6 = m.sb("c_st6", [P, SUB, 6])
        mv = m.sb("c_mv", [P, SUB, 2])
        rs = m.sb("c_rs", [P, SUB, 2])
        hg = m.sb("c_hg", [P, NT, GW])
        prod = m.sb("c_prod", [P, NT, GW])
        ptr = m.ps("c_ptr", [P, 2, KC, 512])
        ph = m.ps("c_ph", [P, 2, 512])
        S = {n: m.sem("c_" + n) for n in (
            "w", "x1", "st", "mv", "eps", "root", "rec", "xf", "turned", "xfT", "h", "h_sb", "prod", "row", "out", "pass")}
        l_in = [m.sem(f"c_in{s}") for s in range(2)]
        x1_s = [m.sem(f"c_x1s{s}") for s in range(2)]
        xf_s = [m.sem(f"c_xfs{s}") for s in range(2)]
        with nc.Block() as block:
            @block.sync
            def _(sp):
                sp.dma_start(wg[:], A.W_gat.rearrange("(c p) o -> p c o", p=P)).then_inc(S["w"], 16)
                for n, a in enumerate((A.att_src, A.att_dst)):
                    sp.dma_start(att[:, n], a.rearrange("(o h) e -> o (h e)", o=1).to_broadcast([P, GW])
                                 ).then_inc(S["w"], 16)

                def load(k, i, s):
                    sp.wait_ge(S["x1"], k * SUB + SUB)
                    for p0, p1 in ((0, 120), (120, TN)):
                        sp.dma_start(pre[p0:p1, s], K.pre_d[bass.ds(k, 1)].rearrange("a p j f -> p (a j) f")[p0:p1]
                                     ).then_inc(l_in[s], 16)

                def store(k, i, s):
                    sp.wait_ge(S["x1"], k * SUB + 3 * SUB)
                    for p0, p1 in ((0, 120), (120, TN)):
                        sp.dma_start(K.x1_d[bass.ds(k, 1)].rearrange("a p j f -> p (a j) f")[p0:p1], x1[p0:p1, s]
                                     ).then_inc(x1_s[s], 16)
                    sp.wait_ge(S["xfT"], k * KC + KC)
                    sp.dma_start(K.xfT_d[bass.ds(k, 1)].rearrange("a p c n -> p (a c) n"), xfT[:, s]
                                 ).then_inc(xf_s[s], 16)

                load(0, 0, 0)
                load(1, 0, 1)
                with sp.Fori(0, (NB - 3) // 2) as i:
                    for s in range(2):
                        load(i * 2 + 2 + s, i + 1, s)
                        store(i * 2 + s, i, s)
                load(NB - 1, 0, 0)
                store(NB - 3, 0, 0)
                store(NB - 2, 0, 1)
                store(NB - 1, 0, 0)
                for s in range(2):
                    sp.wait_ge(x1_s[s], 32 * ((NB + 1 - s) // 2))
                    sp.wait_ge(xf_s[s], 16 * ((NB + 1 - s) // 2))
                sp.wait_ge(S["row"], 3)
                sp.dma_start(K.gtab.rearrange("(t p) f -> p t f", p=TN), K.hrow[0:TN]).then_inc(S["out"], 16)
                sp.wait_ge(S["out"], 16)

            @block.vector
            def _(dve):
                dve.sem_inc(S["x1"], 2 * SUB)
                dve.wait_ge(S["w"], 16 * 3)

                def body(k, i, s):
                    dve.wait_ge(l_in[s], i * 32 + 32)
                    dve.wait_ge(x1_s[s], i * 32)
                    for j in range(SUB):
                        t = k * SUB + j
                        dve.scalar_tensor_tensor(x1[0:TN, s, j], K.acc[0:TN, bass.ds(t, 1), :].rearrange("p a f -> p (a f)"),
                                                 K.dinv[0:TN, bass.ds(t, 1)], pre[0:TN, s, j], ALU.mult, ALU.add
                                                 ).then_inc(S["x1"], 1)
                    dve.wait_ge(S["x1"], k * SUB + 3 * SUB)
                    for j in range(SUB):
                        dve.bn_stats(st6[0:TN, j], x1[0:TN, s, j]).then_inc(S["st"], 1)
                    dve.wait_ge(S["st"], k * SUB + SUB)
                    dve.sem_inc(S["pass"], 1)
                    for j in range(SUB):
                        dve.bn_aggr(mv[0:TN, j], st6[0:TN, j]).then_inc(S["mv"], 1)
                    dve.wait_ge(S["mv"], k * SUB + SUB)
                    dve.tensor_scalar(rs[0:TN, :, 0], mv[0:TN, :, 1], EPS, None, ALU.add).then_inc(S["eps"], 1)
                    dve.wait_ge(S["root"], k + 1)
                    dve.reciprocal(rs[0:TN, :, 0], rs[0:TN, :, 1]).then_inc(S["rec"], 1)
                    dve.wait_ge(S["rec"], k + 1)
                    dve.wait_ge(S["turned"], i * (2 * KC))
                    for j in range(SUB):
                        dve.tensor_scalar(xf[0:TN, s, j], x1[0:TN, s, j], mv[0:TN, j, 0:1], rs[0:TN, j, 0:1],
                                          ALU.subtract, ALU.mult).then_inc(S["xf"], 1)
                    dve.wait_ge(S["xf"], k * SUB + SUB)
                blocks(dve, body)
                dve.wait_ge(S["h_sb"], NB)
                v4 = "p t (h e) -> p t h e"
                n = 0
                shape = [TN, NT, GW]
                dve.tensor_copy(K.hrow[0:TN, :, 0:GW], hg[0:TN]).then_inc(S["row"], 1)
                for a, out in ((0, K.hrow[0:TN, :, GW:ROW]), (1, K.adst[0:TN])):
                    dve.tensor_tensor(prod[0:TN], hg[0:TN], att[0:TN, a].unsqueeze(1).to_broadcast(shape), ALU.mult
                                      ).then_inc(S["prod"], 1)
                    dve.wait_ge(S["prod"], a + 1)
                    dve.tensor_reduce(out, prod[0:TN].rearrange(v4, h=GH), AX.X, ALU.add).then_inc(S["row"], 1)
                    dve.wait_ge(S["row"], a + 2)

            @block.scalar
            def _(act):
                def body(k, i, s):
                    act.wait_ge(S["eps"], k + 1)
                    act.activation(rs[0:TN, :, 1], rs[0:TN, :, 0], ACT.Sqrt).then_inc(S["root"], 1)
                    act.wait_ge(xf_s[s], i * 16)
                    for c in range(KC):
                        act.wait_ge(S["turned"], k * KC + c + 1)
                        act.copy(xfT[:, s, c], ptr[:, s, c, 0:BN]).then_inc(S["xfT"], 1)
                    act.wait_ge(S["h"], k + 1)
                    act.copy(hg[0:TN, bass.ds(k * SUB, SUB), :], ph[0:TN, s, 0:SUB * GW].rearrange("p (j o) -> p j o", j=SUB)
                             ).then_inc(S["h_sb"], 1)
                blocks(act, body)

            @block.tensor
            def _(pe):
                pe.wait_ge(S["w"], 16 * 3)

                def body(k, i, s):
                    pe.wait_ge(S["xf"], k * SUB + SUB)
                    pe.wait_ge(S["xfT"], i * (2 * KC))
                    for c in range(KC):
                        for j in range(SUB):
                            mm = pe.transpose(ptr[:, s, c, j * TN:(j + 1) * TN], xf[0:TN, s, j, c * P:(c + 1) * P],
                                              K.ident[0:TN, 0:TN])
                        mm.then_inc(S["turned"], 1)
                    pe.wait_ge(S["xfT"], k * KC + KC)
                    pe.wait_ge(S["h_sb"], i * 2)
                    for j in range(SUB):
                        for c in range(KC):
                            mm = pe.matmul(ph[0:TN, s, j * GW:(j + 1) * GW], xfT[:, s, c, j * TN:(j + 1) * TN], wg[:, c],
                                           start=c == 0, stop=c == KC - 1, skip_group_check=True)
                    mm.then_inc(S["h"], 1)
                blocks(pe, body)


def gat_max(nc, K):
    W = BATCH
    rounds = S_GAT // (W * HALVES)
    BIG = 1e30
    with ExitStack() as ctx:
        m = Mem(nc, ctx)
        at = m.sb("x_at", [P, HALVES, W], U32)
        rows = m.sb("x_rows", [P, HALVES, W, ROW])
        other = m.sb("x_other", [P, HALVES, W, TN], BF16)
        neg = m.sb("x_neg", [P, P], BF16)
        aT = m.sb("x_aT", [W * GH, HALVES, P])
        asr = m.sb("x_asr", [P, HALVES, W * GH])
        mx = m.sb("x_mx", [P, HALVES, W, GH])
        RING = 4
        px = m.ps("x_px", [P, RING, GH, P])
        pt = m.ps("x_pt", [P, 512])
        S = {n: m.sem("x_" + n) for n in ("neg", "at", "pass", "other", "asr", "kept", "turned", "aT", "px", "mx", "m")}
        got = [m.sem(f"x_got{h}") for h in range(HALVES)]
        with nc.Block() as block:
            @block.gpsimd
            def _(pool):
                with pool.Fori(0, rounds) as i:
                    for h in range(HALVES):
                        pool.wait_ge(S["at"], i * HALVES + h + 1)
                        pool.wait_ge(S["kept"], i * HALVES + h + 1)
                        pool.sem_inc(S["pass"], 1)
                        for b in range(W):
                            pool.indirect_dma_start(
                                out=rows[:, h, b], out_offset=None, in_=K.gtab,
                                in_offset=bass.IndirectOffsetOnAxis(ap=at[:, h, b:b + 1], axis=0)
                            ).then_inc(got[h], 16)

            @block.scalar
            def _(act):
                act.sem_inc(S["kept"], 2)
                for h in range(HALVES):
                    act.copy(at[:, h], K.gat_srcT[:, h * W:(h + 1) * W]).then_inc(S["at"], 1)
                with act.Fori(0, rounds) as i:
                    for h in range(HALVES):
                        n = i * HALVES + h
                        act.wait_ge(got[h], (i + 1) * (16 * W))
                        act.wait_ge(S["turned"], i * HALVES)
                        act.copy(asr[:, h].rearrange("p (w g) -> p w g", w=W), rows[:, h, :, GW:ROW]).then_inc(S["asr"], 1)
                        act.copy(K.feat[:, bass.ds(n * W, W), :], rows[:, h]).then_inc(S["kept"], 1)
                        act.copy(at[:, h], K.gat_srcT[:, bass.ds((n + HALVES) * W, W)]).then_inc(S["at"], 1)
                        act.wait_ge(S["turned"], n + 1)
                        act.wait_ge(S["px"], i * (HALVES * W))
                        act.copy(aT[:, h], pt[0:W * GH, 0:P]).then_inc(S["aT"], 1)

            @block.tensor
            def _(pe):
                pe.wait_ge(S["neg"], 1)
                with pe.Fori(0, rounds) as i:
                    for h in range(HALVES):
                        n = i * HALVES + h
                        pe.wait_ge(S["asr"], n + 1)
                        pe.wait_ge(S["aT"], n)
                        pe.transpose(pt[0:W * GH, 0:P], asr[:, h], K.ident[:]).then_inc(S["turned"], 1)
                        pe.wait_ge(S["aT"], n + 1)
                        pe.wait_ge(S["other"], n + 1)
                        for b in range(W):
                            pe.wait_ge(S["mx"], n * W + b + 1)
                            pe.matmul(px[0:TN, b % RING], other[:, h, b], neg[:].unsqueeze(1).to_broadcast([P, GH, P]),
                                      start=True, stop=False, skip_group_check=True)
                            for g in range(GH):
                                r = b * GH + g
                                mm = pe.matmul(px[0:TN, b % RING, g],
                                               K.ident[0:W * GH, r:r + 1].to_broadcast([W * GH, TN]), aT[:, h],
                                               start=False, stop=g == GH - 1, skip_group_check=True)
                            mm.then_inc(S["px"], 1)

            @block.vector
            def _(dve):
                dve.tensor_scalar(neg[:], K.ident[:], -BIG, None, ALU.mult).then_inc(S["neg"], 1)
                dve.tensor_copy(K.amax[0:TN], K.hrow[0:TN, :, GW:ROW]).then_inc(S["m"], 1)
                dve.sem_inc(S["mx"], RING)
                with dve.Fori(0, rounds) as i:
                    for h in range(HALVES):
                        n = i * HALVES + h
                        dve.wait_ge(S["px"], i * (HALVES * W))
                        shape = [P, W, TN]
                        dve.tensor_tensor(other[:, h], K.iota[:, 0:TN].unsqueeze(1).to_broadcast(shape),
                                          K.gat_dstT[:, bass.ds(n * W, W)].unsqueeze(2).to_broadcast(shape),
                                          ALU.not_equal).then_inc(S["other"], 1)
                        for b in range(W):
                            dve.wait_ge(S["px"], n * W + b + 1)
                            dve.tensor_reduce(mx[0:TN, h, b], px[0:TN, b % RING], AX.X, ALU.max).then_inc(S["mx"], 1)
                        for b in range(W):
                            t = dve.value_load(K.gat_tiles[0:1, bass.ds(n * W + b, 1)], min_val=0, max_val=NT - 1)
                            a = K.amax[0:TN, bass.ds(t, 1), :].rearrange("p a f -> p (a f)")
                            dve.wait_ge(S["mx"], n * W + RING + b + 1)
                            dve.wait_ge(S["m"], n * W + b + 1)
                            dve.tensor_tensor(a, a, mx[0:TN, h, b], ALU.max).then_inc(S["m"], 1)


def gat_sum(nc, K):
    W = BATCH
    rounds = S_GAT // (W * HALVES)
    with ExitStack() as ctx:
        m = Mem(nc, ctx)
        am = m.sb("s_am", [P, NT, 2 * GH])
        own = m.sb("s_own", [P, NT, GH])
        hot = m.sb("s_hot", [P, HALVES, W, TN])
        hotT = m.sb("s_hotT", [P, HALVES, W, P])
        z = m.sb("s_z", [P, HALVES, W, GH])
        z2 = m.sb("s_z2", [P, HALVES, W, GH])
        msg = m.sb("s_msg", [P, HALVES, W, ROW])
        pt = m.ps("s_pt", [P, HALVES, 2, 512])
        pb = m.ps("s_pb", [P, HALVES, 512])
        po = m.ps("s_po", [P, HALVES, 512])
        S = {n: m.sem("s_" + n) for n in (
            "c", "exp0", "hot", "turned", "hotT", "pb", "z", "z2", "e", "msg", "po", "sum", "pass")}
        b4 = [TN, NT, GH, NE]
        with nc.Block() as block:
            @block.vector
            def _(dve):
                q = slice(0, TN)
                asrc = K.hrow[q, :, GW:ROW]
                M, ad = am[q, :, GH:2 * GH], am[q, :, 0:GH]
                dve.tensor_copy(ad, K.adst[q]).then_inc(S["c"], 1)
                dve.tensor_tensor(M, K.amax[q], K.adst[q], ALU.add).then_inc(S["c"], 1)
                dve.tensor_tensor(own[q], asrc, K.adst[q], ALU.add).then_inc(S["c"], 1)
                dve.wait_ge(S["c"], 3)
                dve.scalar_tensor_tensor(M, M, 0.2, M, ALU.mult, ALU.max).then_inc(S["c"], 1)
                dve.scalar_tensor_tensor(own[q], own[q], 0.2, own[q], ALU.mult, ALU.max).then_inc(S["c"], 1)
                dve.wait_ge(S["c"], 5)
                dve.tensor_tensor(own[q], own[q], M, ALU.subtract).then_inc(S["c"], 1)
                dve.wait_ge(S["exp0"], 1)
                dve.tensor_copy(K.gsum[q, :, GW:ROW], own[q]).then_inc(S["c"], 1)
                dve.tensor_tensor(K.gsum[q, :, 0:GW].rearrange("p t (h e) -> p t h e", h=GH),
                                  K.hrow[q, :, 0:GW].rearrange("p t (h e) -> p t h e", h=GH),
                                  own[q].unsqueeze(3).to_broadcast(b4), ALU.mult).then_inc(S["c"], 1)
                dve.wait_ge(S["c"], 8)

                def build(n, i, h):
                    dve.wait_ge(S["po"], i * HALVES)
                    shape = [P, W, TN]
                    dve.tensor_tensor(hot[:, h], K.iota[:, 0:TN].unsqueeze(1).to_broadcast(shape),
                                      K.gat_dstT[:, bass.ds(n * W, W)].unsqueeze(2).to_broadcast(shape),
                                      ALU.is_equal).then_inc(S["hot"], 1)

                with dve.Fori(0, rounds) as i:
                    for h in range(HALVES):
                        build(i * HALVES + h, i, h)
                    for h in range(HALVES):
                        n = i * HALVES + h
                        f = K.feat[:, bass.ds(n * W, W), :]
                        ps = pb[:, h, 0:W * 2 * GH].rearrange("p (w g) -> p w g", w=W)
                        dve.wait_ge(S["pb"], n + 1)
                        dve.tensor_tensor(z[:, h], f[:, :, GW:ROW], ps[:, :, 0:GH], ALU.add).then_inc(S["z"], 1)
                        dve.wait_ge(S["z"], n + 1)
                        dve.scalar_tensor_tensor(z[:, h], z[:, h], 0.2, z[:, h], ALU.mult, ALU.max).then_inc(S["z2"], 1)
                        dve.wait_ge(S["z2"], n * 3 + 1)
                        dve.tensor_tensor(z2[:, h], z[:, h], ps[:, :, GH:2 * GH], ALU.subtract).then_inc(S["z2"], 1)
                        dve.wait_ge(S["z2"], n * 3 + 2)
                        dve.tensor_scalar(z2[:, h], z2[:, h], 0.0, None, ALU.min).then_inc(S["z2"], 1)
                        dve.wait_ge(S["e"], n + 1)
                        w4 = msg[:, h, :, GW:ROW].unsqueeze(3).to_broadcast([P, W, GH, NE])
                        dve.tensor_tensor(msg[:, h, :, 0:GW].rearrange("p w (h e) -> p w h e", h=GH),
                                          f[:, :, 0:GW].rearrange("p w (h e) -> p w h e", h=GH), w4,
                                          ALU.mult).then_inc(S["msg"], 1)
                    for h in range(HALVES):
                        n = i * HALVES + h
                        dve.wait_ge(S["po"], n + 1)
                        for b in range(W):
                            t = dve.value_load(K.gat_tiles[0:1, bass.ds(n * W + b, 1)], min_val=0, max_val=NT - 1)
                            a = K.gsum[0:TN, bass.ds(t, 1), :].rearrange("p a f -> p (a f)")
                            dve.wait_ge(S["sum"], n * W + b)
                            dve.tensor_tensor(a, a, po[0:TN, h, b * ROW:(b + 1) * ROW], ALU.add).then_inc(S["sum"], 1)

            @block.scalar
            def _(act):
                act.wait_ge(S["c"], 6)
                act.activation(own[0:TN], own[0:TN], ACT.Exp).then_inc(S["exp0"], 1)
                with act.Fori(0, rounds) as i:
                    for h in range(HALVES):
                        n = i * HALVES + h
                        act.wait_ge(S["pb"], i * HALVES)
                        for v in range(2):
                            act.wait_ge(S["turned"], n * 2 + v + 1)
                            act.copy(hotT[0:TN, h, v * 4:(v + 1) * 4],
                                     pt[0:TN, h, v].rearrange("p (w e) -> p w e", w=4)).then_inc(S["hotT"], 1)
                    for h in range(HALVES):
                        n = i * HALVES + h
                        act.wait_ge(S["z2"], n * 3 + 3)
                        act.activation(msg[:, h, :, GW:ROW], z2[:, h], ACT.Exp).then_inc(S["e"], 1)

            @block.tensor
            def _(pe):
                pe.wait_ge(S["c"], 8)
                with pe.Fori(0, rounds) as i:
                    for h in range(HALVES):
                        n = i * HALVES + h
                        pe.wait_ge(S["hot"], n + 1)
                        pe.wait_ge(S["hotT"], i * (2 * HALVES))
                        for b in range(W):
                            mm = pe.transpose(pt[0:TN, h, b // 4, (b % 4) * P:(b % 4 + 1) * P], hot[:, h, b], K.ident[:])
                            if b % 4 == 3:
                                mm.then_inc(S["turned"], 1)
                    for h in range(HALVES):
                        n = i * HALVES + h
                        pe.wait_ge(S["hotT"], n * 2 + 2)
                        pe.wait_ge(S["z2"], i * (3 * HALVES))
                        for b in range(W):
                            t = pe.value_load(K.gat_tiles[0:1, bass.ds(n * W + b, 1)], min_val=0, max_val=NT - 1)
                            mm = pe.matmul(pb[:, h, b * 2 * GH:(b + 1) * 2 * GH], hotT[0:TN, h, b],
                                           am[0:TN, bass.ds(t, 1), :].rearrange("p a f -> p (a f)"),
                                           start=True, stop=True, skip_group_check=True)
                        mm.then_inc(S["pb"], 1)
                    for h in range(HALVES):
                        n = i * HALVES + h
                        pe.wait_ge(S["msg"], n + 1)
                        pe.wait_ge(S["sum"], i * (HALVES * W))
                        for b in range(W):
                            mm = pe.matmul(po[0:TN, h, b * ROW:(b + 1) * ROW], hot[:, h, b], msg[:, h, b],
                                           start=True, stop=True, skip_group_check=True)
                        mm.then_inc(S["po"], 1)


def gates(nc, K, A):
    with ExitStack() as ctx:
        m = Mem(nc, ctx)
        row = m.sb("e_row", [P, 3, GW])
        agg = m.sb("e_agg", [P, NT, GW])
        sq = m.sb("e_sq", [P, NT, GW])
        den = m.sb("e_den", [P, NT, GH])
        st = m.sb("e_st", [P, 4, NT])
        sc = m.sb("e_sc", [P, NT, NE])
        rank = m.sb("e_rank", [P, NT, NE])
        cmp_ = m.sb("e_cmp", [P, NT])
        w_s, v, root, ex = (m.sem("e_" + x) for x in ("w", "v", "root", "exp"))
        q = slice(0, TN)
        with nc.Block() as block:
            @block.sync
            def _(sp):
                for n, a in enumerate((A.b_gat, A.ln_gamma, A.ln_beta)):
                    sp.dma_start(row[:, n], a.rearrange("(a o) -> a o", a=1).to_broadcast([P, GW])).then_inc(w_s, 16)

            @block.scalar
            def _(act):
                act.wait_ge(v, 10)
                act.activation(st[q, 1], st[q, 1], ACT.Sqrt).then_inc(root, 1)
                act.wait_ge(root, 2)
                act.activation(sc[q], sc[q], ACT.Exp).then_inc(ex, 1)

            @block.vector
            def _(dve):
                n = [0]

                def step(ins):
                    n[0] += 1
                    ins.then_inc(v, 1)
                    dve.wait_ge(v, n[0])

                def wide(ap, width=GW):
                    return ap.unsqueeze(2).to_broadcast([TN, NT, width])

                def param(r):
                    return row[q, r].unsqueeze(1).to_broadcast([TN, NT, GW])

                dve.wait_ge(w_s, 48)
                step(dve.tensor_scalar(den[q], K.gsum[q, :, GW:ROW], 1e-16, None, ALU.add))
                step(dve.reciprocal(den[q], den[q]))
                step(dve.tensor_tensor(agg[q].rearrange("p t (h e) -> p t h e", h=GH),
                                       K.gsum[q, :, 0:GW].rearrange("p t (h e) -> p t h e", h=GH),
                                       den[q].unsqueeze(3).to_broadcast([TN, NT, GH, NE]), ALU.mult))
                step(dve.tensor_tensor(agg[q], agg[q], param(0), ALU.add))
                step(dve.tensor_reduce(st[q, 0], agg[q], AX.X, ALU.add))
                step(dve.tensor_scalar(st[q, 0], st[q, 0], 1.0 / GW, None, ALU.mult))
                step(dve.tensor_tensor(agg[q], agg[q], wide(st[q, 0]), ALU.subtract))
                step(dve.tensor_tensor(sq[q], agg[q], agg[q], ALU.mult))
                step(dve.tensor_reduce(st[q, 1], sq[q], AX.X, ALU.add))
                step(dve.tensor_scalar(st[q, 1], st[q, 1], 1.0 / GW, EPS, ALU.mult, ALU.add))
                dve.wait_ge(root, 1)
                step(dve.reciprocal(st[q, 1], st[q, 1]))
                step(dve.tensor_tensor(agg[q], agg[q], wide(st[q, 1]), ALU.mult))
                step(dve.tensor_tensor(agg[q], agg[q], param(1), ALU.mult))
                step(dve.tensor_tensor(agg[q], agg[q], param(2), ALU.add))
                step(dve.tensor_reduce(sc[q], agg[q].rearrange("p t (h e) -> p t e h", h=GH), AX.X, ALU.add))
                step(dve.tensor_scalar(sc[q], sc[q], 1.0 / GH, None, ALU.mult))
                step(dve.tensor_reduce(st[q, 2], sc[q], AX.X, ALU.max))
                for e in range(NE):
                    first = True
                    for f in range(NE):
                        if f == e:
                            continue
                        out = rank[q, :, e] if first else cmp_[q]
                        step(dve.tensor_tensor(out, sc[q, :, f], sc[q, :, e], ALU.is_ge if f < e else ALU.is_gt))
                        if not first:
                            step(dve.tensor_tensor(rank[q, :, e], rank[q, :, e], cmp_[q], ALU.add))
                        first = False
                step(dve.tensor_scalar(rank[q], rank[q], 1.5, None, ALU.is_lt))
                step(dve.tensor_tensor(sc[q], sc[q], wide(st[q, 2], NE), ALU.subtract))
                dve.sem_inc(root, 1)
                dve.wait_ge(ex, 1)
                step(dve.tensor_tensor(sc[q], sc[q], rank[q], ALU.mult))
                step(dve.tensor_reduce(st[q, 3], sc[q], AX.X, ALU.add))
                step(dve.reciprocal(st[q, 3], st[q, 3]))
                step(dve.tensor_tensor(K.gate[q], sc[q], wide(st[q, 3], NE), ALU.mult))


def experts(nc, K, A):
    MC = FF // P
    with ExitStack() as ctx:
        m = Mem(nc, ctx)
        w1 = m.sb("f_w1", [P, NE, KC, FF])
        w2 = m.sb("f_w2", [P, NE, MC, D])
        b1 = m.sb("f_b1", [P, NE, MC])
        b2 = m.sb("f_b2", [P, NE, D])
        xfT = m.sb("f_xfT", [P, 2, KC, BN])
        hh = m.sb("f_hh", [P, 2, MC, BN])
        y = m.sb("f_y", [P, 2, SUB, D])
        ph = m.ps("f_ph", [P, 4, 512])
        py = m.ps("f_py", [P, 2, 2, 512])
        S = {n: m.sem("f_" + n) for n in ("w", "free", "ph", "hh", "py", "y", "yb")}
        l_x = [m.sem(f"f_lx{s}") for s in range(2)]
        l_y = [m.sem(f"f_ly{s}") for s in range(2)]
        out_s = [m.sem(f"f_out{s}") for s in range(2)]
        NY = NE * SUB * 2
        with nc.Block() as block:
            @block.sync
            def _(sp):
                for e in range(NE):
                    sp.dma_start(w1[:, e], A.W1[e].rearrange("(c p) o -> p c o", p=P)).then_inc(S["w"], 16)
                    sp.dma_start(w2[:, e], A.W2[e].rearrange("(c p) o -> p c o", p=P)).then_inc(S["w"], 16)
                    sp.dma_start(b2[:, e], A.b2f[e:e + 1].to_broadcast([P, D])).then_inc(S["w"], 16)
                    with nc.allow_non_contiguous_dma(reason="biases"):
                        sp.dma_start(b1[:, e], A.b1f[e].rearrange("(c p) -> p c", p=P)).then_inc(S["w"], 16)

                def load(k, i, s):
                    sp.wait_ge(S["ph"], k * (NE * MC) + NE * MC)
                    sp.dma_start(xfT[:, s], K.xfT_d[bass.ds(k, 1)].rearrange("a p c n -> p (a c) n")).then_inc(l_x[s], 16)
                    sp.wait_ge(out_s[s], i * 32)
                    for p0, p1 in ((0, 120), (120, TN)):
                        sp.dma_start(y[p0:p1, s], K.x1_d[bass.ds(k, 1)].rearrange("a p j f -> p (a j) f")[p0:p1]
                                     ).then_inc(l_y[s], 16)

                def store(k, i, s):
                    sp.wait_ge(S["y"], k * NY + NY)
                    for p0, p1 in ((0, 120), (120, TN)):
                        sp.dma_start(A.out[bass.ds(k * BN, BN)].rearrange("(j p) f -> p j f", p=TN)[p0:p1], y[p0:p1, s]
                                     ).then_inc(out_s[s], 16)

                load(0, 0, 0)
                load(1, 0, 1)
                with sp.Fori(0, (NB - 3) // 2) as i:
                    for s in range(2):
                        store(i * 2 + s, i, s)
                        load(i * 2 + 2 + s, i + 1, s)
                store(NB - 3, 0, 0)
                load(NB - 1, NB // 2, 0)
                store(NB - 2, 0, 1)
                store(NB - 1, 0, 0)
                for s in range(2):
                    sp.wait_ge(out_s[s], 32 * ((NB + 1 - s) // 2))

            @block.tensor
            def _(pe):
                pe.sem_inc(S["ph"], 2 * NE * MC)
                pe.wait_ge(S["w"], 64 * NE)

                def up(k, s, e):
                    for o in range(MC):
                        n = k * (NE * MC) + e * MC + o
                        pe.wait_ge(S["hh"], n + 1)
                        for c in range(KC):
                            mm = pe.matmul(ph[:, o, 0:BN], w1[:, e, c, o * P:(o + 1) * P], xfT[:, s, c],
                                           start=c == 0, stop=c == KC - 1)
                        mm.then_inc(S["ph"], 1)

                def down(k, s, e):
                    pe.wait_ge(S["hh"], k * (NE * MC) + (e + 1) * MC + MC)
                    pe.wait_ge(S["yb"], k * NE + e + 1)
                    for j in range(SUB):
                        for c in range(MC):
                            mm = pe.matmul(py[0:TN, e % 2, j // 2, (j % 2) * D:(j % 2 + 1) * D],
                                           hh[:, e % 2, c, j * TN:(j + 1) * TN], w2[:, e, c],
                                           start=c == 0, stop=c == MC - 1, skip_group_check=True)
                        mm.then_inc(S["py"], 1)

                def body(k, i, s):
                    pe.wait_ge(l_x[s], i * 16 + 16)
                    up(k, s, 0)
                    for e in range(NE):
                        if e + 1 < NE:
                            up(k, s, e + 1)
                        down(k, s, e)
                blocks(pe, body)

            @block.scalar
            def _(act):
                act.wait_ge(S["w"], 64 * NE)
                act.sem_inc(S["hh"], MC)

                def body(k, i, s):
                    for e in range(NE):
                        if e < 2:
                            act.wait_ge(S["py"], k * (NE * SUB))
                        else:
                            act.wait_ge(S["py"], k * (NE * SUB) + (e - 1) * SUB)
                        for o in range(MC):
                            n = k * (NE * MC) + e * MC + o
                            act.wait_ge(S["ph"], n + 2 * NE * MC + 1)
                            act.activation(hh[:, e % 2, o], ph[:, o, 0:BN], ACT.Gelu, bias=b1[:, e, o:o + 1]
                                           ).then_inc(S["hh"], 1)
                blocks(act, body)

            @block.vector
            def _(dve):
                dve.sem_inc(S["yb"], 2)
                dve.wait_ge(S["w"], 64 * NE)

                def body(k, i, s):
                    dve.wait_ge(l_y[s], i * 32 + 32)
                    for e in range(NE):
                        n0 = k * NY + e * (2 * SUB)
                        for j in range(SUB):
                            dve.wait_ge(S["y"], n0 + (j if e == 0 else j - 0))
                            g = K.gate[0:TN, bass.ds(k * SUB + j, 1), e]
                            dve.scalar_tensor_tensor(y[0:TN, s, j], b2[0:TN, e], g, y[0:TN, s, j], ALU.mult, ALU.add
                                                     ).then_inc(S["y"], 1)
                        for j in range(SUB):
                            if j % 2 == 0:
                                dve.wait_ge(S["py"], k * (NE * SUB) + e * SUB + j + 2)
                            dve.wait_ge(S["y"], n0 + SUB + j)
                            g = K.gate[0:TN, bass.ds(k * SUB + j, 1), e]
                            dve.scalar_tensor_tensor(y[0:TN, s, j], py[0:TN, e % 2, j // 2, (j % 2) * D:(j % 2 + 1) * D],
                                                     g, y[0:TN, s, j], ALU.mult, ALU.add).then_inc(S["y"], 1)
                        dve.wait_ge(S["y"], n0 + 2 * SUB)
                        dve.sem_inc(S["yb"], 1)
                blocks(dve, body)


def program(nc, A):
    with ExitStack() as ctx:
        m = Mem(nc, ctx)

        class K:
            pass
        K.gcn_pairs = m.dram("gcn_pairs", [E_GCN + P, 2], I32)
        K.gat_pairs = m.dram("gat_pairs", [E_GAT + P, 2], I32)
        K.hT_d = m.dram("hT_d", [NB, P, KC, BN])
        K.qT_d = m.dram("qT_d", [NB, P, KC, BN])
        K.xfT_d = m.dram("xfT_d", [NB, P, KC, BN])
        K.pre_d = m.dram("pre_d", [NB, TN, SUB, D])
        K.x1_d = m.dram("x1_d", [NB, TN, SUB, D])
        K.table = m.dram("table", [N, D])
        K.gtab = m.dram("gtab", [N, ROW])
        gcn_td, gat_td = m.dram("gcn_td", [G_GCN * P], I32), m.dram("gat_td", [G_GAT * P], I32)
        constants(nc, m, K)
        K.dinv = m.sb("dinv", [P, NT])
        K.gat_srcT = m.sb("gat_srcT", [P, G_GAT * P], U32)
        K.gat_dstT = m.sb("gat_dstT", [P, G_GAT * P])
        K.gat_tiles = m.sb("gat_tiles", [1, G_GAT * P], I32)
        K.hrow = m.sb("hrow", [P, NT, ROW])
        K.adst = m.sb("adst", [P, NT, GH])
        with ExitStack() as c1:
            m1 = Mem(nc, c1)
            K.gcn_srcT = m1.sb("gcn_srcT", [P, G_GCN * P], U32)
            K.gcn_dstT = m1.sb("gcn_dstT", [P, G_GCN * P])
            K.gcn_tiles = m1.sb("gcn_tiles", [1, G_GCN * P], I32)
            K.xmv = m1.sb("xmv", [P, NT, 2])
            K.xrs = m1.sb("xrs", [P, NT])
            K.hmv = m1.sb("hmv", [P, KC, 2])
            K.kv = m1.sb("kv", [P, KC, P + 1])
            K.cnt = m1.sb("cnt", [P, NT])
            K.base = m1.sb("base", [P, NT])
            with ExitStack() as c2:
                m2 = Mem(nc, c2)
                load_edges(nc, m2, K, A)
                degrees(nc, K, A)
                sort_edges(nc, K, "ga", K.gat_pairs, GAT_P, GAT_C, K.gat_tile, K.gat_pay)
                step_tables(nc, K, "ga", K.gat_pairs, E_GAT, G_GAT, K.gat_srcT, K.gat_dstT, K.gat_tiles, gat_td)
                sort_edges(nc, K, "gc", K.gcn_pairs, GCN_P, GCN_C, K.gcn_tile, K.gcn_pay)
            step_tables(nc, K, "gc", K.gcn_pairs, E_GCN, G_GCN, K.gcn_srcT, K.gcn_dstT, K.gcn_tiles, gcn_td)
            dense_first(nc, K, A)
            K.acc = m1.sb("acc", [P, NT, D])
            dense_second(nc, K, A)
            gather_sum(nc, K)
            second_norm(nc, K, A)
        K.gsum = m.sb("gsum", [P, NT, ROW])
        K.gate = m.sb("gate", [P, NT, NE])
        with ExitStack() as c3:
            m3 = Mem(nc, c3)
            K.feat = m3.sb("feat", [P, S_GAT, ROW])
            K.amax = m3.sb("amax", [P, NT, GH])
            gat_max(nc, K)
            gat_sum(nc, K)
        gates(nc, K, A)
        experts(nc, K, A)


_ARGS = {
    "x": "x", "src": "src", "dst": "dst", "L0_ffn_edge_index": "edge_index",
    "L0_gnn_b1": "b1", "L0_gnn_gamma": "gamma", "L0_gnn_beta": "beta", "L0_gnn_w2": "w2", "L0_gnn_b2": "b2",
    "L0_gnn_b_gcn": "b_gcn", "L0_mix_wq": "wq", "L0_mix_bq": "bq", "L0_mix_wk": "wk", "L0_mix_bk": "bk",
    "L0_mix_wv": "wv", "L0_mix_bv": "bv", "L0_mix_wo": "wo", "L0_mix_bo": "bo", "L0_ffn_W_gat": "W_gat",
    "L0_ffn_att_src": "att_src", "L0_ffn_att_dst": "att_dst", "L0_ffn_b_gat": "b_gat",
    "L0_ffn_ln_gamma": "ln_gamma", "L0_ffn_ln_beta": "ln_beta", "L0_ffn_W1": "W1", "L0_ffn_b1": "b1f",
    "L0_ffn_W2": "W2", "L0_ffn_b2": "b2f",
}
_TURNED = {"L0_gnn_w1": "w1T", "L0_gnn_w_gcn": "wgT"}


def kernel(**inputs):
    import types

    import numpy as _np
    import concourse.bacc as _bacc
    from concourse import mybir as _mybir
    from concourse.bass_utils import run_bass_kernel_spmd as _run

    nc = _bacc.Bacc("TRN2", target_bir_lowering=False, num_devices=1)
    A = types.SimpleNamespace()
    arrays = {}
    given = [(v, _np.ascontiguousarray(inputs[k])) for k, v in _ARGS.items()]
    given += [(v, _np.ascontiguousarray(_np.transpose(inputs[k]))) for k, v in _TURNED.items()]
    for name, a in given:
        arrays[f"in_{name}"] = a
        A.__dict__[name] = nc.dram_tensor(f"in_{name}", a.shape, _mybir.dt.from_np(a.dtype), kind="ExternalInput").ap()
    A.out = nc.dram_tensor("out_x", (N, D), _mybir.dt.float32, kind="ExternalOutput").ap()
    program(nc, A)
    r = _run(nc, [arrays], core_ids=[0])
    return r.results[0]["out_x"]
```

```python
from contextlib import ExitStack, nullcontext

import concourse.bass as bass
from concourse import mybir

F32 = mybir.dt.float32
I32 = mybir.dt.int32
U32 = mybir.dt.uint32
U16 = mybir.dt.uint16
BF16 = mybir.dt.bfloat16
ALU = mybir.AluOpType
ACT = mybir.ActivationFunctionType
AX = mybir.AxisListType

N = 12500
D = 256
P = 128
TN = 125
NT = N // TN
SUB = 4
BN = SUB * TN
NB = N // BN
KC = D // P
HD = 32
EPS = 1e-5
E_GCN, GCN_P = 200000, 125
E_GAT, GAT_P = 131072, 128
GCN_C, GAT_C = E_GCN // GCN_P, E_GAT // GAT_P
BATCH = 8
HALVES = 2


ROUND = BATCH * HALVES


def steps_for(edges, unit):
    most = (edges + NT * P * unit) // P
    return -(-most // ROUND) * ROUND


UNIT_GCN, UNIT_GAT = 2, 1
S_GCN, S_GAT = steps_for(E_GCN, UNIT_GCN), steps_for(E_GAT, UNIT_GAT)
G_GCN, G_GAT = -(-S_GCN // P), -(-S_GAT // P)
NE, FF = 4, 512
GH = 4
BIG = 1e30
GW = GH * NE
ROW = GW + GH
PARTS = 3
TROW = ROW + PARTS * GH // 2


def blocks(eng, body):
    with eng.Fori(0, NB // 2) as i:
        body(i * 2, i, 0)
        body(i * 2 + 1, i, 1)
    if NB % 2:
        body(NB - 1, NB // 2, 0)


class Mem:

    def __init__(self, nc, ctx):
        self.nc, self.ctx, self.sems, self.kept = nc, ctx, [], []
        ctx.callback(self.clear)

    def clear(self):
        if not self.sems + self.kept:
            return
        with self.nc.Block() as block:
            @block.gpsimd
            def _(pool):
                for s in self.sems + self.kept:
                    pool.sem_clear(s)
        for s in self.sems:
            self.nc.release_semaphore(s)

    def sb(self, name, shape, dt=F32):
        return self.ctx.enter_context(self.nc.sbuf_tensor(name, shape, dt))

    def ps(self, name, shape, dt=F32):
        return self.ctx.enter_context(self.nc.psum_tensor(name, shape, dt))

    def sem(self, name):
        self.sems.append(self.nc.alloc_semaphore(name))
        return self.sems[-1]

    def gather_sem(self, name):
        self.kept.append(self.nc.alloc_semaphore(name))
        return self.kept[-1]

    def dram(self, name, shape, dt=F32):
        return self.nc.dram_tensor(name, shape, dt).ap()


def constants(nc, m, K):
    K.ident = m.sb("ident", [P, P])
    K.ones = m.sb("ones", [P, P])
    K.before = m.sb("before", [P, P])
    K.iota = m.sb("iota", [P, P])
    K.iota_h = m.sb("iota_h", [P, P], BF16)
    K.head = m.sb("head", [P, P])
    K.part = m.sb("part", [P, 1])
    iota_i = m.sb("iota_i", [P, P], I32)
    part_i = m.sb("part_i", [P, 1], I32)
    q_s, j_s, v_s = m.sem("c_set"), m.sem("c_sel"), m.sem("c_copied")
    with nc.Block() as block:
        @block.gpsimd
        def _(pool):
            pool.memset(K.ident[:], 0.0).then_inc(q_s, 1)
            pool.memset(K.ones[:], 1.0).then_inc(q_s, 1)
            pool.memset(K.before[:], 0.0).then_inc(q_s, 1)
            pool.iota(iota_i[:], [[1, P]], base=0, channel_multiplier=0).then_inc(q_s, 1)
            pool.iota(part_i[:], [[1, 1]], base=0, channel_multiplier=1).then_inc(q_s, 1)
            pool.wait_ge(q_s, 5)
            pool.affine_select(out=K.ident[:], in_=K.ident[:], compare_op=ALU.not_equal, fill=1.0, base=0,
                               pattern=[[-1, P]], channel_multiplier=1).then_inc(j_s, 1)
            pool.affine_select(out=K.before[:], in_=K.before[:], compare_op=ALU.is_ge, fill=1.0, base=0,
                               pattern=[[-1, P]], channel_multiplier=1).then_inc(j_s, 1)
            hv = K.head[:].rearrange("p (g j) -> p g j", j=HD)
            pool.affine_select(out=hv, in_=K.ones[:].rearrange("p (g j) -> p g j", j=HD), compare_op=ALU.is_ge,
                               fill=0.0, base=0, pattern=[[-HD, P // HD], [0, HD]],
                               channel_multiplier=1).then_inc(j_s, 1)
            pool.wait_ge(j_s, 3)
            pool.affine_select(out=hv, in_=hv, compare_op=ALU.is_ge, fill=0.0, base=HD - 1,
                               pattern=[[HD, P // HD], [0, HD]], channel_multiplier=-1).then_inc(j_s, 1)

        @block.vector
        def _(dve):
            dve.wait_ge(q_s, 5)
            dve.tensor_copy(K.iota[:], iota_i[:]).then_inc(v_s, 1)
            dve.tensor_copy(K.iota_h[:], iota_i[:]).then_inc(v_s, 1)
            dve.tensor_copy(K.part[:], part_i[:]).then_inc(v_s, 1)
            dve.wait_ge(v_s, 3)


def sort_edges(nc, K, tag, pairs, n_part, cols, tile_h, pay, unsorted=None):

    def where_needed(eng):
        return eng.If(eng.value_load(unsorted[:], min_val=0, max_val=1)) if unsorted is not None else nullcontext()

    with ExitStack() as ctx:
        m = Mem(nc, ctx)
        passed = m.sem(tag + "_passed")
        cnt = m.sb(tag + "_cnt", [P, NT])
        eq = m.sb(tag + "_eq", [P, cols], U16)
        run = m.sb(tag + "_run", [P, cols])
        place_f = m.sb(tag + "_place_f", [P, cols])
        place = m.sb(tag + "_place", [P, cols], U32)
        incl = m.sb(tag + "_incl", [P, NT])
        off = m.sb(tag + "_off", [P, NT])
        ptot = m.ps(tag + "_ptot", [P, NT])
        ppre = m.ps(tag + "_ppre", [P, NT])
        counted, summed, chain, placed = (m.sem(tag + x) for x in ("_counted", "_summed", "_chain", "_placed"))
        q = slice(0, n_part)
        with nc.Block() as block:
            @block.vector
            def _(dve):
                with where_needed(dve):
                    dve.sem_inc(counted, 1)
                    with dve.Fori(0, NT) as t:
                        dve.wait_ge(counted, t + 1)
                        dve.tensor_scalar(eq[q], tile_h[q], K.iota[q, bass.ds(t, 1)], None, ALU.is_equal, ALU.add,
                                          accum_out=cnt[q, bass.ds(t, 1)]).then_inc(counted, 1)
                    dve.wait_ge(summed, 2)
                    dve.tensor_copy(K.cnt[:], ptot[:]).then_inc(chain, 1)
                    dve.wait_ge(chain, 1)
                    dve.tensor_tensor_scan(incl[:], K.cnt[:], K.cnt[:], 0.0, ALU.add, ALU.bypass).then_inc(chain, 1)
                    dve.wait_ge(chain, 2)
                    dve.tensor_tensor(K.base[:], incl[:], K.cnt[:], ALU.subtract).then_inc(chain, 1)
                    dve.wait_ge(chain, 3)
                    dve.scalar_tensor_tensor(off[q], ppre[q], -1.0, K.base[q], ALU.add, ALU.add).then_inc(chain, 1)
                    dve.wait_ge(chain, 4)
                    dve.wait_ge(placed, 1)
                    with dve.Fori(0, NT) as t:
                        dve.tensor_scalar(eq[q], tile_h[q], K.iota[q, bass.ds(t, 1)], None,
                                          ALU.is_equal).then_inc(chain, 1)
                        dve.wait_ge(chain, t * 3 + 5)
                        dve.tensor_tensor_scan(run[q], eq[q], eq[q], off[q, bass.ds(t, 1)], ALU.add,
                                               ALU.bypass).then_inc(chain, 1)
                        dve.wait_ge(chain, t * 3 + 6)
                        dve.sem_inc(passed, 1)
                        dve.copy_predicated(place_f[q], eq[q], run[q]).then_inc(chain, 1)
                        dve.wait_ge(chain, t * 3 + 7)
                    dve.tensor_copy(place[q], place_f[q]).then_inc(placed, 1)

            @block.gpsimd
            def _(pool):
                with where_needed(pool):
                    pool.memset(place_f[:], 0.0).then_inc(placed, 1)

            @block.tensor
            def _(pe):
                with where_needed(pe):
                    pe.wait_ge(counted, NT + 1)
                    pe.matmul(ptot[:], K.ones[q, :], cnt[q], start=True, stop=True).then_inc(summed, 1)
                    pe.matmul(ppre[q], K.before[q, q], cnt[q], start=True, stop=True).then_inc(summed, 1)
        at = m.sb(tag + "_at", [P, HALVES, BATCH], U32)
        row = m.sb(tag + "_row", [P, HALVES, BATCH, 2], I32)
        staged = m.sem(tag + "_staged")
        sent = [m.gather_sem(f"{tag}_sent{h}") for h in range(HALVES)]
        nq = n_part
        with nc.Block() as block:
            @block.gpsimd
            def _(pool):
                with where_needed(pool):
                    with pool.Fori(0, cols // (BATCH * HALVES)) as i:
                        for h in range(HALVES):
                            c = i * (BATCH * HALVES) + h * BATCH
                            pool.wait_ge(sent[h], i * (16 * BATCH))
                            pool.tensor_copy(at[0:nq, h], place[0:nq, bass.ds(c, BATCH)]).then_inc(staged, 1)
                            pool.tensor_copy(row[0:nq, h], pay[0:nq, bass.ds(c, BATCH), :]).then_inc(staged, 1)
                            pool.wait_ge(staged, i * 4 + 2 * h + 2)
                            pool.sem_inc(passed, 1)
                            for b in range(BATCH):
                                pool.indirect_dma_start(
                                    out=pairs, out_offset=bass.IndirectOffsetOnAxis(ap=at[0:nq, h, b:b + 1], axis=0),
                                    in_=row[0:nq, h, b, :], in_offset=None).then_inc(sent[h], 16)
                    for h in range(HALVES):
                        pool.wait_ge(sent[h], 16 * BATCH * (cols // (BATCH * HALVES)))


def step_tables(nc, K, tag, pairs, edges, unit, groups, src_T, dst_T, ch_start, ch_end, tile_row=None, tile_dram=None):
    with ExitStack() as ctx:
        m = Mem(nc, ctx)
        nch = m.sb(tag + "_nch", [P, NT])
        nch_i = m.sb(tag + "_nch_i", [P, NT], I32)
        shift = m.sb(tag + "_shift", [P, NT])
        ended = m.sb(tag + "_ended", [P, groups, NT])
        mine = m.sb(tag + "_mine", [P, groups, NT])
        step = m.sb(tag + "_step", [P, groups])
        tile = m.sb(tag + "_tile", [P, groups])
        tile_i = m.sb(tag + "_tile_i", [P, groups], I32)
        first = m.sb(tag + "_first", [P, groups])
        first_i = m.sb(tag + "_first_i", [P, groups], U32)
        node0 = m.sb(tag + "_node0", [P, groups])
        rows = m.sb(tag + "_rows", [P, 2, P, 2], I32)
        cols = m.sb(tag + "_cols", [P, 2, 2, P])
        ptr = m.ps(tag + "_ptr", [P, 2, 2, P])
        c, fetched, split, turned, used, out_s = (m.sem(tag + x) for x in (
            "_st", "_fetched", "_split", "_turned", "_used", "_outs"))
        fetch = [m.gather_sem(f"{tag}_fetch{h}") for h in range(2)]
        with nc.Block() as block:
            @block.vector
            def _(dve):
                n = [0]

                def done(ins):
                    n[0] += 1
                    ins.then_inc(c, 1)
                    dve.wait_ge(c, n[0])

                wide = P * unit
                done(dve.tensor_scalar(nch_i[:], K.cnt[:], 1.0 / wide, (wide - 1) / (2.0 * wide), ALU.mult, ALU.add))
                done(dve.tensor_scalar(nch[:], nch_i[:], 1.0, float(unit), ALU.max, ALU.mult))
                done(dve.tensor_tensor_scan(ch_end[:], nch[:], nch[:], 0.0, ALU.add, ALU.bypass))
                done(dve.tensor_tensor(ch_start[:], ch_end[:], nch[:], ALU.subtract))
                done(dve.scalar_tensor_tensor(shift[:], ch_start[:], -float(P), K.base[:], ALU.mult, ALU.add))
                for g in range(groups):
                    dve.tensor_scalar(step[:, g:g + 1], K.part[:], float(P * g), None, ALU.add).then_inc(c, 1)
                n[0] += groups
                dve.wait_ge(c, n[0])
                both = [P, groups, NT]
                st = step[:].unsqueeze(2).to_broadcast(both)
                done(dve.tensor_tensor(ended[:], ch_end[:].unsqueeze(1).to_broadcast(both), st, ALU.is_le))
                done(dve.tensor_tensor(mine[:], ch_start[:].unsqueeze(1).to_broadcast(both), st, ALU.is_le))
                done(dve.tensor_tensor(mine[:], mine[:], ended[:], ALU.subtract))
                done(dve.tensor_tensor(mine[:], mine[:], shift[:].unsqueeze(1).to_broadcast(both), ALU.mult))
                done(dve.tensor_reduce(first[:], mine[:], AX.X, ALU.add))
                done(dve.scalar_tensor_tensor(first[:], step[:], float(P), first[:], ALU.mult, ALU.add))
                done(dve.tensor_scalar(first_i[:], first[:], float(edges), None, ALU.min))
                done(dve.tensor_reduce(tile[:], ended[:], AX.X, ALU.add))
                done(dve.tensor_scalar(tile[:], tile[:], float(NT - 1), None, ALU.min))
                done(dve.tensor_copy(tile_i[:], tile[:]))
                done(dve.tensor_scalar(node0[:], tile[:], float(TN), None, ALU.mult))
                dve.sem_inc(fetched, 1)
                for g in range(groups):
                    s = g % 2
                    dve.wait_ge(fetch[s], 16 * (g // 2 + 1))
                    if g >= 2:
                        dve.wait_ge(turned, 2 * (g - 1))
                    dve.tensor_copy(cols[:, s, 0], rows[:, s, :, 0]).then_inc(split, 1)
                    dve.tensor_scalar(cols[:, s, 1], rows[:, s, :, 1], node0[:, g:g + 1], None,
                                      ALU.subtract).then_inc(split, 1)
                    dve.wait_ge(turned, 2 * (g + 1))
                    dve.tensor_copy(src_T[:, g * P:(g + 1) * P], ptr[:, s, 0]).then_inc(used, 1)
                    dve.tensor_copy(dst_T[:, g * P:(g + 1) * P], ptr[:, s, 1]).then_inc(used, 1)

            @block.gpsimd
            def _(pool):
                pool.wait_ge(fetched, 1)
                for g in range(groups):
                    s = g % 2
                    if g >= 2:
                        pool.wait_ge(split, 2 * (g - 1))
                    pool.indirect_dma_start(out=rows[:, s].rearrange("p a b -> p (a b)"), out_offset=None, in_=pairs,
                                            in_offset=bass.IndirectOffsetOnAxis(ap=first_i[:, g:g + 1], axis=0)
                                            ).then_inc(fetch[s], 16)

            @block.tensor
            def _(pe):
                for g in range(groups):
                    s = g % 2
                    pe.wait_ge(split, 2 * (g + 1))
                    if g >= 2:
                        pe.wait_ge(used, 2 * (g - 1))
                    for a in range(2):
                        pe.transpose(ptr[:, s, a], cols[:, s, a], K.ident[:]).then_inc(turned, 1)

            if tile_row is None:
                return

            @block.sync
            def _(sp):
                sp.wait_ge(fetched, 1)
                with nc.allow_non_contiguous_dma(reason="a small table"):
                    sp.dma_start(tile_dram.rearrange("(g p) -> p g", p=P), tile_i[:]).then_inc(out_s, 16)
                sp.wait_ge(out_s, 16)
                sp.dma_start(tile_row[:], tile_dram.rearrange("(a s) -> a s", a=1)).then_inc(out_s, 16)
                sp.wait_ge(out_s, 32)


def load_edges(nc, m, K, A):
    K.unsorted = m.sb("unsorted", [1, 1], I32)
    K.gat_pay = m.sb("gat_pay", [P, GAT_C, 2], I32)
    K.gat_tile = m.sb("gat_tile", [P, GAT_C], BF16)
    K.gcn_pay = m.sb("gcn_pay", [P, GCN_C, 2], I32)
    K.gcn_tile = m.sb("gcn_tile", [P, GCN_C], BF16)
    K.gcn_node = m.sb("gcn_node", [P, GCN_C], BF16)
    with ExitStack() as ctx:
        m = Mem(nc, ctx)
        raw = m.sb("raw", [P, 2, GCN_C], I32)
        raw2 = m.sb("raw2", [P, 2, GAT_C], I32)
        ti = m.sb("ti", [P, GCN_C], I32)
        tail = m.sb("tail", [P, 2], I32)
        after = m.sb("after", [P, 1], I32)
        falls = m.sb("falls", [P, GCN_C], BF16)
        fall = m.sb("fall", [P, 2])
        pfall = m.ps("pfall", [P, 1])
        fell = m.sem("le_fell")
        copied = m.sem("le_copied")
        loaded, chain, out_s, pad = m.sem("le_loaded"), m.sem("le_chain"), m.sem("le_out"), m.sem("le_pad")
        c = GCN_P
        with nc.Block() as block:
            @block.sync
            def _(sp):
                sp.dma_start(raw[0:c, 0], A.src.rearrange("(p c) -> p c", p=c)).then_inc(loaded, 16)
                sp.dma_start(raw[0:c, 1], A.dst.rearrange("(p c) -> p c", p=c)).then_inc(loaded, 16)
                sp.dma_start(raw2[:, 0], A.edge_index[0].rearrange("(p c) -> p c", p=P)).then_inc(loaded, 16)
                sp.dma_start(raw2[:, 1], A.edge_index[1].rearrange("(p c) -> p c", p=P)).then_inc(loaded, 16)
                with nc.allow_non_contiguous_dma(reason="one value per partition"):
                    sp.dma_start(after[0:c - 1], A.dst.rearrange("(p c) -> p c", p=c)[1:c, 0:1]).then_inc(loaded, 16)
                sp.wait_ge(copied, 2)
                sp.dma_start(K.gcn_pairs[0:E_GCN].rearrange("(p c) a -> p c a", p=c), K.gcn_pay[0:c]).then_inc(out_s, 16)
                sp.wait_ge(pad, 1)
                sp.dma_start(K.gcn_pairs[E_GCN:E_GCN + P], tail[:]).then_inc(out_s, 16)
                sp.dma_start(K.gat_pairs[E_GAT:E_GAT + P], tail[:]).then_inc(out_s, 16)
                sp.wait_ge(out_s, 48)

            @block.gpsimd
            def _(pool):
                pool.memset(tail[:, 0:1], 0).then_inc(chain, 1)
                pool.memset(tail[:, 1:2], -1).then_inc(chain, 1)
                pool.wait_ge(chain, 2)
                pool.sem_inc(pad, 1)
                pool.wait_ge(loaded, 80)
                for a in range(2):
                    pool.tensor_copy(K.gat_pay[:, :, a], raw2[:, a]).then_inc(chain, 1)

            @block.scalar
            def _(act):
                act.wait_ge(loaded, 80)
                for a in range(2):
                    act.copy(K.gcn_pay[0:c, :, a], raw[0:c, a]).then_inc(copied, 1)

            @block.vector
            def _(dve):
                n = [0]
                dv = m.sem("le_dve")

                def done(ins):
                    n[0] += 1
                    ins.then_inc(dv, 1)
                    dve.wait_ge(dv, n[0])

                dve.wait_ge(loaded, 80)
                scale, bias = 1.0 / TN, 0.5 / TN - 0.5
                done(dve.tensor_scalar(ti[0:c], raw[0:c, 1], scale, bias, ALU.mult, ALU.add))
                done(dve.tensor_copy(K.gcn_tile[0:c], ti[0:c]))
                done(dve.scalar_tensor_tensor(K.gcn_node[0:c], ti[0:c], -float(TN), raw[0:c, 1], ALU.mult, ALU.add))
                done(dve.tensor_scalar(ti[:, 0:GAT_C], raw2[:, 1], scale, bias, ALU.mult, ALU.add))
                done(dve.tensor_copy(K.gat_tile[:], ti[:, 0:GAT_C]))
                done(dve.memset(fall[:], 0.0))
                done(dve.tensor_tensor(falls[0:c, 1:GCN_C], raw[0:c, 1, 1:GCN_C], raw[0:c, 1, 0:GCN_C - 1], ALU.is_lt))
                done(dve.tensor_reduce(fall[0:c, 0:1], falls[0:c, 1:GCN_C], AX.X, ALU.max))
                done(dve.tensor_tensor(fall[0:c - 1, 1:2], after[0:c - 1], raw[0:c - 1, 1, GCN_C - 1:GCN_C], ALU.is_lt))
                done(dve.tensor_tensor(fall[:, 0:1], fall[:, 0:1], fall[:, 1:2], ALU.add))
                dve.sem_inc(fell, 1)
                dve.wait_ge(fell, 2)
                done(dve.tensor_scalar(K.unsorted[:], pfall[0:1], 1.0, None, ALU.min))

            @block.tensor
            def _(pe):
                pe.wait_ge(fell, 1)
                pe.matmul(pfall[:], K.ones[:], fall[:, 0:1], start=True, stop=True).then_inc(fell, 1)


def degrees(nc, K, A):
    HB = 16
    rounds = GCN_C // HB
    with ExitStack() as ctx:
        m = Mem(nc, ctx)
        on = m.sb("on", [P, 2, HB, TN], BF16)
        ot = m.sb("ot", [P, 2, HB, NT], BF16)
        pdeg = m.ps("pdeg", [P, NT])
        xin = m.sb("dx_in", [P, 2, SUB, D])
        st6 = m.sb("dx_st", [P, SUB, 6])
        mv = m.sb("dx_mv", [P, SUB, 2])
        var = m.sb("dx_var", [P, NT, 2])
        node_s, tile_s, used, done_s, chain, root, x_free, kept = (m.sem("dg_" + x) for x in (
            "node", "tile", "used", "done", "chain", "root", "x_free", "kept"))
        xl = [m.sem(f"dg_xl{s}") for s in range(2)]
        c = GCN_P
        with nc.Block() as block:
            def onehot(eng, out, ids, width, i, s, sem):
                k = i * 2 + s
                eng.wait_ge(used, i * 2 + s)
                shape = [c, HB, width]
                eng.tensor_tensor(out[0:c, s], K.iota_h[0:c, 0:width].unsqueeze(1).to_broadcast(shape),
                                  ids[0:c, bass.ds(k * HB, HB)].unsqueeze(2).to_broadcast(shape),
                                  ALU.is_equal).then_inc(sem, 1)

            @block.sync
            def _(sp):
                def body(k, i, s):
                    sp.wait_ge(x_free, k + 1)
                    for p0, p1 in ((0, 120), (120, TN)):
                        sp.dma_start(xin[p0:p1, s],
                                     A.x[bass.ds(k * BN, BN)].rearrange("(j p) f -> p j f", p=TN)[p0:p1]
                                     ).then_inc(xl[s], 16)
                blocks(sp, body)

            @block.tensor
            def _(pe):
                def body(i, s, first, last):
                    pe.wait_ge(node_s, i * 2 + s + 1)
                    pe.wait_ge(tile_s, i * 2 + s + 1)
                    for b in range(HB):
                        mm = pe.matmul(pdeg[0:TN], on[0:c, s, b], ot[0:c, s, b],
                                       start=first and b == 0, stop=last and b == HB - 1)
                    mm.then_inc(used, 1)
                pe.sem_inc(used, 1)
                body(0, 0, True, False)
                body(0, 1, False, False)
                with pe.Fori(1, rounds // 2 - 1) as i:
                    body(i, 0, False, False)
                    body(i, 1, False, False)
                body(rounds // 2 - 1, 0, False, False)
                body(rounds // 2 - 1, 1, False, True)

            @block.vector
            def _(dve):
                def stats(k, i, s):
                    dve.wait_ge(xl[s], i * 32 + 32)
                    for j in range(SUB):
                        dve.bn_stats(st6[0:TN, j], xin[0:TN, s, j]).then_inc(chain, 1)
                    dve.wait_ge(chain, k * (2 * SUB) + SUB)
                    dve.sem_inc(x_free, 1)
                    for j in range(SUB):
                        dve.bn_aggr(mv[0:TN, j], st6[0:TN, j]).then_inc(chain, 1)
                    dve.wait_ge(chain, k * (2 * SUB) + 2 * SUB)
                    dve.tensor_copy(K.xmv[0:TN, bass.ds(k * SUB, SUB), :], mv[0:TN]).then_inc(kept, 1)
                dve.sem_inc(x_free, 2)
                blocks(dve, stats)
                with dve.Fori(0, rounds // 2) as i:
                    for s in range(2):
                        onehot(dve, on, K.gcn_node, TN, i, s, node_s)
                        onehot(dve, ot, K.gcn_tile, NT, i, s, tile_s)
                dve.wait_ge(kept, NB)
                dve.wait_ge(used, rounds + 1)
                dve.tensor_scalar(var[0:TN, :, 0], K.xmv[0:TN, :, 1], EPS, None, ALU.add).then_inc(done_s, 1)
                dve.tensor_scalar(var[0:TN, :, 1], pdeg[0:TN], 1.0, None, ALU.add).then_inc(done_s, 1)
                dve.tensor_copy(K.degree[0:TN], pdeg[0:TN]).then_inc(kept, 1)
                dve.wait_ge(root, 1)
                dve.reciprocal(var[0:TN], var[0:TN]).then_inc(done_s, 1)
                dve.wait_ge(done_s, 3)
                dve.tensor_copy(K.xrs[0:TN], var[0:TN, :, 0]).then_inc(done_s, 1)
                dve.tensor_copy(K.dinv[0:TN], var[0:TN, :, 1]).then_inc(done_s, 1)

            @block.scalar
            def _(act):
                act.wait_ge(done_s, 2)
                act.activation(var[0:TN], var[0:TN], ACT.Sqrt).then_inc(root, 1)


def counts_of_tiles(nc, K):
    with ExitStack() as ctx:
        m = Mem(nc, ctx)
        upto = m.sb("ct_upto", [P, NT])
        total = m.ps("ct_total", [P, NT])
        summed, chain = m.sem("ct_summed"), m.sem("ct_chain")
        with nc.Block() as block:
            @block.tensor
            def _(pe):
                pe.matmul(total[:], K.ones[0:TN], K.degree[0:TN], start=True, stop=True).then_inc(summed, 1)

            @block.vector
            def _(dve):
                dve.wait_ge(summed, 1)
                dve.tensor_copy(K.cnt[:], total[:]).then_inc(chain, 1)
                dve.wait_ge(chain, 1)
                dve.tensor_tensor_scan(upto[:], K.cnt[:], K.cnt[:], 0.0, ALU.add, ALU.bypass).then_inc(chain, 1)
                dve.wait_ge(chain, 2)
                dve.tensor_tensor(K.base[:], upto[:], K.cnt[:], ALU.subtract).then_inc(chain, 1)


def dense_first(nc, K, A):
    with ExitStack() as ctx:
        m = Mem(nc, ctx)
        w1T = m.sb("w1T", [P, KC, D])
        wq = m.sb("wq", [P, KC, D])
        wkv = m.sb("wkv", [P, KC, 2, D])
        b1c = m.sb("b1c", [P, KC])
        bqc = m.sb("bqc", [P, KC])
        bkv = m.sb("bkv", [P, 2, D])
        xin = m.sb("a_xin", [P, 2, SUB, D])
        xn = m.sb("a_xn", [P, 2, SUB, D])
        xnT = m.sb("a_xnT", [P, 2, KC, BN])
        hT = m.sb("a_hT", [P, 2, KC, BN])
        qT = m.sb("a_qT", [P, 2, KC, BN])
        qm = m.sb("a_qm", [P, KC, BN])
        kb = m.sb("a_kb", [P, 2, D])
        km = m.sb("a_km", [P, 2, D])
        ve = m.sb("a_ve", [P, 2, KC, P + 1])
        stats = m.sb("a_stats", [P, KC, NB, 6])
        hst = m.sb("a_hst", [P, KC, 6])
        ptr = m.ps("a_ptr", [P, KC, 512])
        pqh = m.ps("a_pqh", [P, KC, 512])
        pkv = m.ps("a_pkv", [P, 2, 512])
        pacc = m.ps("a_pacc", [P, KC, 512])
        S = {n: m.sem("a_" + n) for n in (
            "w", "ones", "x_free", "xn", "turned", "xnT", "q", "q_min", "q_sb", "q_exp", "q_sum", "h", "h_sb",
            "h_stat", "kv", "kb", "v", "k_min", "k_exp", "k_sum", "acc", "agg", "mean")}
        x_in = [m.sem(f"a_x_in{s}") for s in range(2)]
        stored = [m.sem(f"a_stored{s}") for s in range(2)]
        with nc.Block() as block:
            @block.sync
            def _(sp):
                sp.dma_start(w1T[:], A.w1T.rearrange("(c p) o -> p c o", p=P)).then_inc(S["w"], 16)
                sp.dma_start(wq[:], A.wq.rearrange("(c p) o -> p c o", p=P)).then_inc(S["w"], 16)
                sp.dma_start(wkv[:, :, 0], A.wk.rearrange("(c p) o -> p c o", p=P)).then_inc(S["w"], 16)
                sp.dma_start(wkv[:, :, 1], A.wv.rearrange("(c p) o -> p c o", p=P)).then_inc(S["w"], 16)
                with nc.allow_non_contiguous_dma(reason="biases"):
                    sp.dma_start(b1c[:], A.b1.rearrange("(c p) -> p c", p=P)).then_inc(S["w"], 16)
                    sp.dma_start(bqc[:], A.bq.rearrange("(c p) -> p c", p=P)).then_inc(S["w"], 16)
                sp.dma_start(bkv[:, 0], A.bk.rearrange("(a o) -> a o", a=1).to_broadcast([P, D])).then_inc(S["w"], 16)
                sp.dma_start(bkv[:, 1], A.bv.rearrange("(a o) -> a o", a=1).to_broadcast([P, D])).then_inc(S["w"], 16)

                def load(k, i, s):
                    sp.wait_ge(S["x_free"], k + 1)
                    for p0, p1 in ((0, 120), (120, TN)):
                        sp.dma_start(xin[p0:p1, s], A.x[bass.ds(k * BN, BN)].rearrange("(j p) f -> p j f", p=TN)[p0:p1]
                                     ).then_inc(x_in[s], 16)

                def store(k, i, s):
                    sp.wait_ge(S["h_sb"], k * 2 + 2)
                    sp.dma_start(K.hT_d[bass.ds(k, 1)].rearrange("a p c n -> p (a c) n"), hT[:, s]
                                 ).then_inc(stored[s], 16)
                    sp.wait_ge(S["q_sum"], k * 2 + 2)
                    sp.dma_start(K.qT_d[bass.ds(k, 1)].rearrange("a p c n -> p (a c) n"), qT[:, s]
                                 ).then_inc(stored[s], 16)

                load(0, 0, 0)
                load(1, 0, 1)
                with sp.Fori(0, (NB - 3) // 2) as i:
                    for s in range(2):
                        load(i * 2 + 2 + s, i + 1, s)
                        store(i * 2 + s, i, s)
                load(NB - 1, 0, 0)
                store(NB - 3, 0, 0)
                store(NB - 2, 0, 1)
                store(NB - 1, 0, 0)
                sp.wait_ge(stored[0], 32 * (NB // 2 + 1))
                sp.wait_ge(stored[1], 32 * (NB // 2))

            @block.tensor
            def _(pe):
                def project(w, s, sem):
                    for o in range(KC):
                        for c in range(KC):
                            mm = pe.matmul(pqh[:, o, 0:BN], w[:, c, o * P:(o + 1) * P], xnT[:, s, c],
                                           start=c == 0, stop=c == KC - 1)
                        mm.then_inc(sem, 1)

                def kv(k, s, j):
                    pe.wait_ge(S["v"], k * SUB + j)
                    for c in range(KC):
                        mm = pe.matmul(pkv[0:TN, j % 2], xnT[:, s, c, j * TN:(j + 1) * TN],
                                       wkv[:, c].rearrange("p a o -> p (a o)"), start=c == 0, stop=c == KC - 1)
                    mm.then_inc(S["kv"], 1)

                def accumulate(k, j, first, last):
                    pe.wait_ge(S["k_sum"], k * SUB + j + 1)
                    for c in range(KC):
                        mm = pe.matmul(pacc[:, c, 0:P + 1], km[0:TN, j % 2, c * P:(c + 1) * P], ve[0:TN, j % 2, c],
                                       start=first and j == 0, stop=last and j == SUB - 1)
                    mm.then_inc(S["acc"], 1)

                def body(k, s, first=False, last=False):
                    pe.wait_ge(S["xnT"], k * KC + KC)
                    pe.wait_ge(S["h_sb"], k * KC)
                    project(wq, s, S["q"])
                    kv(k, s, 0)
                    kv(k, s, 1)
                    pe.wait_ge(S["q_sb"], k * KC + KC)
                    project(w1T, s, S["h"])
                    if not last:
                        transposes_next(k, s)
                    accumulate(k, 0, first, last)
                    kv(k, s, 2)
                    accumulate(k, 1, first, last)
                    kv(k, s, 3)
                    accumulate(k, 2, first, last)
                    accumulate(k, 3, first, last)

                def transposes_next(k, s):
                    pe.wait_ge(S["xn"], k * SUB + 2 * SUB)
                    pe.wait_ge(S["xnT"], k * KC + KC)
                    turn(1 - s)

                def turn(s):
                    for c in range(KC):
                        for j in range(SUB):
                            mm = pe.transpose(ptr[:, c, j * TN:(j + 1) * TN], xn[0:TN, s, j, c * P:(c + 1) * P],
                                              K.ident[0:TN, 0:TN])
                        mm.then_inc(S["turned"], 1)

                pe.wait_ge(S["w"], 16 * 8)
                pe.wait_ge(S["ones"], 1)
                pe.wait_ge(S["xn"], SUB)
                turn(0)
                body(0, 0, first=True)
                body(1, 1)
                with pe.Fori(1, NB // 2) as i:
                    body(i * 2, 0)
                    body(i * 2 + 1, 1)
                body(NB - 1, 0, last=True)

            @block.scalar
            def _(act):
                def turned(k, s):
                    act.wait_ge(S["turned"], k * KC + KC)
                    for c in range(KC):
                        act.copy(xnT[:, s, c], ptr[:, c, 0:BN]).then_inc(S["xnT"], 1)

                def body(k, i, s, last=False):
                    act.wait_ge(stored[s], i * 32)
                    for c in range(KC):
                        act.wait_ge(S["q"], k * KC + c + 1)
                        act.activation(qT[:, s, c], pqh[:, c, 0:BN], ACT.Identity, bias=bqc[:, c:c + 1]
                                       ).then_inc(S["q_sb"], 1)
                    for c in range(KC):
                        act.wait_ge(S["q_min"], k * KC + c + 1)
                        act.activation(qm[:, c], qm[:, c], ACT.Exp).then_inc(S["q_exp"], 1)
                    k_exp(k, 0)
                    k_exp(k, 1)
                    for c in range(KC):
                        act.wait_ge(S["h"], k * KC + c + 1)
                        act.activation(hT[:, s, c], pqh[:, c, 0:BN], ACT.Identity, bias=b1c[:, c:c + 1]
                                       ).then_inc(S["h_sb"], 1)
                    if not last:
                        turned(k + 1, 1 - s)
                    k_exp(k, 2)
                    k_exp(k, 3)

                def k_exp(k, j):
                    act.wait_ge(S["k_min"], k * SUB + j + 1)
                    act.activation(km[0:TN, j % 2], km[0:TN, j % 2], ACT.Exp).then_inc(S["k_exp"], 1)

                act.wait_ge(S["w"], 16 * 8)
                turned(0, 0)
                with act.Fori(0, NB // 2) as i:
                    body(i * 2, i, 0)
                    body(i * 2 + 1, i, 1)
                body(NB - 1, NB // 2, 0, last=True)

            @block.vector
            def _(dve):
                def normalise(k, i, s):
                    dve.wait_ge(x_in[s], i * 32 + 32)
                    dve.wait_ge(S["turned"], i * (2 * KC))
                    for j in range(SUB):
                        t = k * SUB + j
                        ins = dve.tensor_scalar(xn[0:TN, s, j], xin[0:TN, s, j], K.xmv[0:TN, bass.ds(t, 1), 0],
                                                K.xrs[0:TN, bass.ds(t, 1)], ALU.subtract, ALU.mult)
                        ins.then_inc(S["xn"], 1)
                    dve.wait_ge(S["xn"], k * SUB + SUB)
                    dve.sem_inc(S["x_free"], 1)

                def k_part(k, j):
                    s = j % 2
                    dve.wait_ge(S["kv"], k * SUB + j + 1)
                    if j >= 2:
                        dve.wait_ge(S["acc"], k * SUB + j - 1)
                    else:
                        dve.wait_ge(S["acc"], k * SUB)
                    dve.tensor_tensor(kb[0:TN, s], pkv[0:TN, s, 0:D], bkv[0:TN, 0], ALU.add).then_inc(S["kb"], 1)
                    dve.tensor_tensor(ve[0:TN, s, :, 0:P], pkv[0:TN, s, D:2 * D].rearrange("p (c e) -> p c e", c=KC),
                                      bkv[0:TN, 1].rearrange("p (c e) -> p c e", c=KC), ALU.add).then_inc(S["v"], 1)
                    dve.wait_ge(S["kb"], k * SUB + j + 1)
                    dve.tensor_scalar(km[0:TN, s], kb[0:TN, s], 0.0, None, ALU.min).then_inc(S["k_min"], 1)

                def k_sum(k, j):
                    s = j % 2
                    dve.wait_ge(S["k_exp"], k * SUB + j + 1)
                    dve.scalar_tensor_tensor(km[0:TN, s], kb[0:TN, s], 0.0, km[0:TN, s], ALU.max, ALU.add
                                             ).then_inc(S["k_sum"], 1)

                def body(k, i, s, last=False):
                    dve.wait_ge(S["q_sum"], k * KC)
                    for c in range(KC):
                        dve.wait_ge(S["q_sb"], k * KC + c + 1)
                        dve.tensor_scalar(qm[:, c], qT[:, s, c], 0.0, None, ALU.min).then_inc(S["q_min"], 1)
                    if not last:
                        normalise(k + 1, *((i, 1) if s == 0 else (i + 1, 0)))
                    k_part(k, 0)
                    k_part(k, 1)
                    for c in range(KC):
                        dve.wait_ge(S["q_exp"], k * KC + c + 1)
                        dve.scalar_tensor_tensor(qT[:, s, c], qT[:, s, c], 0.0, qm[:, c], ALU.max, ALU.add
                                                 ).then_inc(S["q_sum"], 1)
                    k_sum(k, 0)
                    k_sum(k, 1)
                    for c in range(KC):
                        dve.wait_ge(S["h_sb"], k * KC + c + 1)
                        dve.bn_stats(hst[:, c], hT[:, s, c]).then_inc(S["h_stat"], 1)
                    dve.wait_ge(S["h_stat"], k * KC + KC)
                    dve.tensor_copy(stats[:, :, bass.ds(k, 1), :].rearrange("p c a b -> p c (a b)"), hst[:]).then_inc(S["agg"], 1)
                    dve.wait_ge(S["agg"], k + 1)
                    k_part(k, 2)
                    k_sum(k, 2)
                    k_part(k, 3)
                    k_sum(k, 3)

                dve.memset(ve[:, :, :, P:P + 1], 1.0).then_inc(S["ones"], 1)
                dve.sem_inc(S["x_free"], 2)
                dve.sem_inc(S["v"], 1)
                dve.wait_ge(S["w"], 16 * 8)
                dve.wait_ge(S["ones"], 1)
                normalise(0, 0, 0)
                with dve.Fori(0, NB // 2) as i:
                    body(i * 2, i, 0)
                    body(i * 2 + 1, i, 1)
                body(NB - 1, NB // 2, 0, last=True)
                for c in range(KC):
                    dve.bn_aggr(K.hmv[:, c], stats[:, c].rearrange("p n s -> p (n s)")).then_inc(S["mean"], 1)
                dve.wait_ge(S["acc"], NT)
                dve.tensor_copy(K.kv[:], pacc[:, :, 0:P + 1]).then_inc(S["mean"], 1)
                dve.wait_ge(S["mean"], 3)


def dense_second(nc, K, A):
    with ExitStack() as ctx:
        m = Mem(nc, ctx)
        w2 = m.sb("w2", [P, KC, D])
        wgT = m.sb("wgT", [P, KC, D])
        wo = m.sb("wo", [P, KC, D])
        gb = m.sb("gb", [P, 2, KC])
        b2c = m.sb("b2c", [P, KC])
        rows_b = m.sb("rows_b", [P, 2, D])
        W = m.sb("w_both", [P, KC, D])
        bW = m.sb("b_both", [P, D])
        kvm = m.sb("kvm", [P, KC, P])
        kvT = m.sb("kvT", [P, KC, P])
        kvw = m.sb("kvw", [P, KC, D])
        Z = m.sb("zmat", [P, KC, P])
        b2r = m.sb("b2r", [P, KC, P])
        bn = m.sb("bn", [P, KC, 4])
        scale, shift = m.sb("bn_scale", [P, KC]), m.sb("bn_shift", [P, KC])
        hT = m.sb("b_hT", [P, 2, KC, BN])
        qT = m.sb("b_qT", [P, 2, KC, BN])
        xin = m.sb("b_xin", [P, 2, SUB, D])
        pre = m.sb("b_pre", [P, 2, SUB, D])
        tmp = m.sb("b_tmp", [P, SUB, D])
        rz = m.sb("b_rz", [P, KC, BN])
        pz = m.ps("b_pz", [P, KC, 512])
        px = m.ps("b_px", [P, SUB, D])
        pm = m.ps("b_pm", [P, SUB, D])
        pw = m.ps("b_pw", [P, 512])
        S = {n: m.sem("b_" + n) for n in (
            "w", "v", "root", "p", "z", "rz", "qs", "relu", "px", "tmp", "acc", "pm", "pre", "in_free")}
        l_in = [m.sem(f"b_in{s}") for s in range(2)]
        tab_s = [m.sem(f"b_tab{s}") for s in range(2)]
        pre_s = [m.sem(f"b_pre_s{s}") for s in range(2)]
        with nc.Block() as block:
            @block.sync
            def _(sp):
                for t, a in ((w2, A.w2), (wgT, A.wgT), (wo, A.wo)):
                    sp.dma_start(t[:], a.rearrange("(c p) o -> p c o", p=P)).then_inc(S["w"], 16)
                with nc.allow_non_contiguous_dma(reason="biases"):
                    for t, a in ((gb[:, 0], A.gamma), (gb[:, 1], A.beta), (b2c[:], A.b2)):
                        sp.dma_start(t, a.rearrange("(c p) -> p c", p=P)).then_inc(S["w"], 16)
                for n, a in enumerate((A.bo, A.b_gcn)):
                    sp.dma_start(rows_b[:, n], a.rearrange("(a o) -> a o", a=1).to_broadcast([P, D])
                                 ).then_inc(S["w"], 16)

                def load(k, i, s):
                    sp.wait_ge(S["in_free"], k + 1)
                    sp.dma_start(hT[:, s], K.hT_d[bass.ds(k, 1)].rearrange("a p c n -> p (a c) n")).then_inc(l_in[s], 16)
                    sp.dma_start(qT[:, s], K.qT_d[bass.ds(k, 1)].rearrange("a p c n -> p (a c) n")).then_inc(l_in[s], 16)
                    for p0, p1 in ((0, 120), (120, TN)):
                        sp.dma_start(xin[p0:p1, s], A.x[bass.ds(k * BN, BN)].rearrange("(j p) f -> p j f", p=TN)[p0:p1]
                                     ).then_inc(l_in[s], 16)

                def store(k, i, s):
                    sp.wait_ge(S["acc"], k * SUB + SUB)
                    for p0, p1 in ((0, 120), (120, TN)):
                        sp.dma_start(K.table[bass.ds(k * BN, BN)].rearrange("(j p) f -> p j f", p=TN)[p0:p1],
                                     K.acc[p0:p1, bass.ds(k * SUB, SUB), :]).then_inc(tab_s[s], 16)
                    sp.wait_ge(S["pre"], k * (2 * SUB) + 2 * SUB)
                    for p0, p1 in ((0, 120), (120, TN)):
                        sp.dma_start(K.pre_d[bass.ds(k, 1)].rearrange("a p j f -> p (a j) f")[p0:p1],
                                     pre[p0:p1, s]).then_inc(pre_s[s], 16)

                load(0, 0, 0)
                load(1, 0, 1)
                with sp.Fori(0, (NB - 3) // 2) as i:
                    for s in range(2):
                        load(i * 2 + 2 + s, i + 1, s)
                        store(i * 2 + s, i, s)
                load(NB - 1, 0, 0)
                store(NB - 3, 0, 0)
                store(NB - 2, 0, 1)
                store(NB - 1, 0, 0)
                for s in range(2):
                    sp.wait_ge(tab_s[s], 32 * ((NB + 1 - s) // 2))
                    sp.wait_ge(pre_s[s], 32 * ((NB + 1 - s) // 2))

            @block.tensor
            def _(pe):
                pe.wait_ge(S["w"], 16 * 8)
                for b in range(KC):
                    for a in range(KC):
                        mm = pe.matmul(pw[:, b * D:(b + 1) * D], w2[:, a, b * P:(b + 1) * P], wgT[:, a],
                                       start=a == 0, stop=a == KC - 1, skip_group_check=True)
                mm.then_inc(S["p"], 1)
                pe.wait_ge(S["v"], 4)
                for c in range(KC):
                    mm = pe.transpose(pz[:, 0, c * P:(c + 1) * P], kvm[:, c], K.ident[:])
                mm.then_inc(S["p"], 1)
                for a in range(KC):
                    mm = pe.matmul(pz[:, 1, 0:D], b2r[:, a], wgT[:, a], start=a == 0, stop=a == KC - 1)
                mm.then_inc(S["p"], 1)
                pe.wait_ge(S["v"], 7)
                for c in range(KC):
                    mm = pe.matmul(pw[:, c * D:(c + 1) * D], kvT[:, c], wo[:, c], start=True, stop=True,
                                   skip_group_check=True)
                mm.then_inc(S["p"], 1)
                pe.wait_ge(S["v"], 8)

                def body(k, i, s):
                    pe.wait_ge(l_in[s], i * 64 + 64)
                    pe.wait_ge(S["rz"], k * KC)
                    for c in range(KC):
                        pe.matmul(pz[:, c, 0:BN], Z[:, c], qT[:, s, c], start=True, stop=True).then_inc(S["z"], 1)
                    pe.wait_ge(S["relu"], k * KC + KC)
                    pe.wait_ge(S["tmp"], k * SUB)
                    for j in range(SUB):
                        for c in range(KC):
                            mm = pe.matmul(px[0:TN, j], hT[:, s, c, j * TN:(j + 1) * TN], W[:, c],
                                           start=c == 0, stop=c == KC - 1, skip_group_check=True)
                        mm.then_inc(S["px"], 1)
                    pe.wait_ge(S["qs"], k * KC + KC)
                    pe.wait_ge(S["pre"], k * (2 * SUB))
                    for j in range(SUB):
                        for c in range(KC):
                            mm = pe.matmul(pm[0:TN, j], qT[:, s, c, j * TN:(j + 1) * TN], kvw[:, c],
                                           start=c == 0, stop=c == KC - 1, skip_group_check=True)
                        mm.then_inc(S["pm"], 1)
                blocks(pe, body)

            @block.scalar
            def _(act):
                act.wait_ge(S["v"], 5)
                act.activation(bn[:, :, 1], bn[:, :, 0], ACT.Sqrt).then_inc(S["root"], 1)
                act.wait_ge(S["v"], 8)

                def body(k, i, s):
                    act.wait_ge(l_in[s], i * 64 + 64)
                    for c in range(KC):
                        act.activation(hT[:, s, c], hT[:, s, c], ACT.Relu, bias=shift[:, c:c + 1],
                                       scale=scale[:, c:c + 1]).then_inc(S["relu"], 1)
                    for j in range(SUB):
                        t = k * SUB + j
                        act.wait_ge(S["tmp"], k * SUB + j + 1)
                        act.activation(K.acc[0:TN, bass.ds(t, 1), :].rearrange("p a f -> p (a f)"), tmp[0:TN, j],
                                       ACT.Copy, scale=K.dinv[0:TN, bass.ds(t, 1)]).then_inc(S["acc"], 1)
                blocks(act, body)

            @block.vector
            def _(dve):
                dve.wait_ge(S["w"], 16 * 8)
                for c in range(KC):
                    dve.tensor_tensor(kvm[:, c], K.kv[:, c, 0:P], K.head[:], ALU.mult).then_inc(S["v"], 1)
                for c in range(KC):
                    dve.tensor_scalar(b2r[:, c], K.ones[:], b2c[:, c:c + 1], None, ALU.mult).then_inc(S["v"], 1)
                dve.tensor_scalar(bn[:, :, 0], K.hmv[:, :, 1], EPS, None, ALU.add).then_inc(S["v"], 1)
                dve.wait_ge(S["p"], 3)
                dve.tensor_copy(W[:].rearrange("p c f -> p (c f)"), pw[:]).then_inc(S["v"], 1)
                dve.tensor_copy(kvT[:].rearrange("p c f -> p (c f)"), pz[:, 0, 0:KC * P]).then_inc(S["v"], 1)
                u = m.sem("b_u")
                for c in range(KC):
                    dve.tensor_scalar(Z[:, c], K.head[:], K.kv[:, c, P:P + 1], None, ALU.mult).then_inc(u, 1)
                dve.tensor_copy(bW[:], pz[:, 1, 0:D]).then_inc(u, 1)
                dve.tensor_tensor(rows_b[:, 0], rows_b[:, 0], rows_b[:, 1], ALU.add).then_inc(u, 1)
                dve.wait_ge(S["root"], 1)
                dve.reciprocal(bn[:, :, 2], bn[:, :, 1]).then_inc(u, 1)
                dve.wait_ge(u, 5)
                dve.tensor_tensor(scale[:], bn[:, :, 2], gb[:, 0], ALU.mult).then_inc(u, 1)
                dve.wait_ge(u, 6)
                dve.tensor_tensor(bn[:, :, 3], K.hmv[:, :, 0], scale[:], ALU.mult).then_inc(u, 1)
                dve.wait_ge(u, 7)
                dve.tensor_tensor(shift[:], gb[:, 1], bn[:, :, 3], ALU.subtract).then_inc(u, 1)
                dve.wait_ge(u, 8)
                dve.wait_ge(S["p"], 4)
                dve.tensor_copy(kvw[:].rearrange("p c f -> p (c f)"), pw[:]).then_inc(S["v"], 1)
                dve.sem_inc(S["in_free"], 2)
                dve.wait_ge(S["v"], 8)

                def body(k, i, s):
                    for c in range(KC):
                        dve.wait_ge(S["z"], k * KC + c + 1)
                        dve.tensor_scalar(rz[:, c], pz[:, c, 0:BN], 1e-6, None, ALU.add).then_inc(S["rz"], 1)
                    dve.wait_ge(S["rz"], k * KC + KC)
                    for c in range(KC):
                        dve.reciprocal(rz[:, c], rz[:, c]).then_inc(r2, 1)
                    dve.wait_ge(r2, k * KC + KC)
                    for c in range(KC):
                        dve.tensor_tensor(qT[:, s, c], qT[:, s, c], rz[:, c], ALU.mult).then_inc(S["qs"], 1)
                    dve.wait_ge(S["acc"], k * SUB)
                    for j in range(SUB):
                        if j % 2 == 0:
                            dve.wait_ge(S["px"], k * SUB + j + 2)
                        dve.tensor_tensor(tmp[0:TN, j], px[0:TN, j], bW[0:TN], ALU.add).then_inc(S["tmp"], 1)
                    dve.wait_ge(pre_s[s], i * 32)
                    for j in range(SUB):
                        dve.tensor_tensor(pre[0:TN, s, j], xin[0:TN, s, j], rows_b[0:TN, 0], ALU.add
                                          ).then_inc(S["pre"], 1)
                    dve.wait_ge(S["pre"], k * (2 * SUB) + SUB)
                    for j in range(SUB):
                        if j % 2 == 0:
                            dve.wait_ge(S["pm"], k * SUB + j + 2)
                        dve.tensor_tensor(pre[0:TN, s, j], pre[0:TN, s, j], pm[0:TN, j], ALU.add
                                          ).then_inc(S["pre"], 1)
                    dve.wait_ge(S["pre"], k * (2 * SUB) + 2 * SUB)
                    dve.sem_inc(S["in_free"], 1)
                r2 = m.sem("b_r2")
                blocks(dve, body)


def gather_sum(nc, K):
    W, PAIRS = BATCH, BATCH // 2
    rounds = S_GCN // (W * HALVES)
    with ExitStack() as ctx:
        m = Mem(nc, ctx)
        at = m.sb("g_at", [P, HALVES, W], U32)
        rows = m.sb("g_rows", [P, HALVES, W, D])
        hot = m.sb("g_hot", [P, HALVES, W, TN])
        ps = m.ps("g_ps", [P, HALVES, PAIRS, 512])
        at_s, hot_s, mm_s, add_s, passed = (m.sem("g_" + x) for x in ("at", "hot", "mm", "add", "passed"))
        got = [m.gather_sem(f"g_got{h}") for h in range(HALVES)]
        with nc.Block() as block:
            @block.scalar
            def _(act):
                for h in range(HALVES):
                    act.copy(at[:, h], K.gcn_srcT[:, h * W:(h + 1) * W]).then_inc(at_s, 1)
                with act.Fori(1, rounds) as i:
                    for h in range(HALVES):
                        act.wait_ge(got[h], i * (16 * W))
                        act.copy(at[:, h], K.gcn_srcT[:, bass.ds((i * HALVES + h) * W, W)]).then_inc(at_s, 1)

            @block.gpsimd
            def _(pool):
                with pool.Fori(0, rounds) as i:
                    for h in range(HALVES):
                        pool.wait_ge(at_s, i * HALVES + h + 1)
                        pool.wait_ge(mm_s, (i * HALVES + h) * PAIRS + PAIRS)
                        pool.sem_inc(passed, 1)
                        for b in range(W):
                            pool.indirect_dma_start(
                                out=rows[:, h, b], out_offset=None, in_=K.table,
                                in_offset=bass.IndirectOffsetOnAxis(ap=at[:, h, b:b + 1], axis=0)
                            ).then_inc(got[h], 16)

            @block.tensor
            def _(pe):
                pe.sem_inc(mm_s, HALVES * PAIRS)
                with pe.Fori(0, rounds) as i:
                    for h in range(HALVES):
                        pe.wait_ge(hot_s, i * HALVES + h + 1)
                        pe.wait_ge(got[h], (i + 1) * (16 * W))
                        for j in range(PAIRS):
                            pe.wait_ge(add_s, (i * HALVES + h) * PAIRS + j + 1)
                            for b in (2 * j, 2 * j + 1):
                                mm = pe.matmul(ps[0:TN, h, j, 0:D], hot[:, h, b], rows[:, h, b], start=b == 2 * j,
                                               stop=b == 2 * j + 1)
                            mm.then_inc(mm_s, 1)

            @block.vector
            def _(dve):
                dve.sem_inc(add_s, HALVES * PAIRS)

                def build(n, h):
                    dve.wait_ge(mm_s, n * PAIRS + PAIRS)
                    shape = [P, W, TN]
                    dve.tensor_tensor(hot[:, h], K.iota[:, 0:TN].unsqueeze(1).to_broadcast(shape),
                                      K.gcn_dstT[:, bass.ds(n * W, W)].unsqueeze(2).to_broadcast(shape),
                                      ALU.is_equal).then_inc(hot_s, 1)

                def add(n, h):
                    for j in range(PAIRS):
                        t = dve.value_load(K.gcn_tiles[0:1, bass.ds(n * W + 2 * j, 1)], min_val=0, max_val=NT - 1)
                        a = K.acc[0:TN, bass.ds(t, 1), :].rearrange("p a f -> p (a f)")
                        dve.wait_ge(mm_s, n * PAIRS + HALVES * PAIRS + j + 1)
                        dve.wait_ge(add_s, n * PAIRS + HALVES * PAIRS + j)
                        dve.tensor_tensor(a, a, ps[0:TN, h, j, 0:D], ALU.add).then_inc(add_s, 1)

                build(0, 0)
                with dve.Fori(0, rounds - 1) as i:
                    for h in range(HALVES):
                        n = i * HALVES + h
                        build(n + 1, 1 - h)
                        add(n, h)
                n = (rounds - 1) * HALVES
                build(n + 1, 1)
                add(n, 0)
                add(n + 1, 1)


def second_norm(nc, K, A):
    with ExitStack() as ctx:
        m = Mem(nc, ctx)
        wg = m.sb("wg", [P, KC, GW])
        att = m.sb("att", [P, 2, GW])
        pre = m.sb("c_pre", [P, 2, SUB, D])
        x1 = m.sb("c_x1", [P, 2, SUB, D])
        xf = m.sb("c_xf", [P, 2, SUB, D])
        xfT = m.sb("c_xfT", [P, 2, KC, BN])
        st6 = m.sb("c_st6", [P, SUB, 6])
        mv = m.sb("c_mv", [P, SUB, 2])
        rs = m.sb("c_rs", [P, SUB, 2])
        hg = m.sb("c_hg", [P, NT, GW])
        prod = m.sb("c_prod", [P, NT, GW])
        trow = m.sb("c_trow", [P, NT, TROW])
        ptr = m.ps("c_ptr", [P, 2, KC, 512])
        ph = m.ps("c_ph", [P, 2, 512])
        S = {n: m.sem("c_" + n) for n in (
            "w", "x1", "st", "mv", "eps", "root", "rec", "xf", "turned", "xfT", "h", "h_sb", "prod", "row", "part", "trow", "out", "pass")}
        l_in = [m.sem(f"c_in{s}") for s in range(2)]
        x1_s = [m.sem(f"c_x1s{s}") for s in range(2)]
        xf_s = [m.sem(f"c_xfs{s}") for s in range(2)]
        with nc.Block() as block:
            @block.sync
            def _(sp):
                sp.dma_start(wg[:], A.W_gat.rearrange("(c p) o -> p c o", p=P)).then_inc(S["w"], 16)
                for n, a in enumerate((A.att_src, A.att_dst)):
                    sp.dma_start(att[:, n], a.rearrange("(o h) e -> o (h e)", o=1).to_broadcast([P, GW])
                                 ).then_inc(S["w"], 16)

                def load(k, i, s):
                    sp.wait_ge(S["x1"], k * SUB + SUB)
                    for p0, p1 in ((0, 120), (120, TN)):
                        sp.dma_start(pre[p0:p1, s], K.pre_d[bass.ds(k, 1)].rearrange("a p j f -> p (a j) f")[p0:p1]
                                     ).then_inc(l_in[s], 16)

                def store(k, i, s):
                    sp.wait_ge(S["x1"], k * SUB + 3 * SUB)
                    for p0, p1 in ((0, 120), (120, TN)):
                        sp.dma_start(K.x1_d[bass.ds(k, 1)].rearrange("a p j f -> p (a j) f")[p0:p1], x1[p0:p1, s]
                                     ).then_inc(x1_s[s], 16)
                    sp.wait_ge(S["xfT"], k * KC + KC)
                    sp.dma_start(K.xfT_d[bass.ds(k, 1)].rearrange("a p c n -> p (a c) n"), xfT[:, s]
                                 ).then_inc(xf_s[s], 16)

                load(0, 0, 0)
                load(1, 0, 1)
                with sp.Fori(0, (NB - 3) // 2) as i:
                    for s in range(2):
                        load(i * 2 + 2 + s, i + 1, s)
                        store(i * 2 + s, i, s)
                load(NB - 1, 0, 0)
                store(NB - 3, 0, 0)
                store(NB - 2, 0, 1)
                store(NB - 1, 0, 0)
                for s in range(2):
                    sp.wait_ge(x1_s[s], 32 * ((NB + 1 - s) // 2))
                    sp.wait_ge(xf_s[s], 16 * ((NB + 1 - s) // 2))
                sp.wait_ge(S["trow"], 2)
                sp.dma_start(K.gtab.rearrange("(t p) f -> p t f", p=TN), trow[0:TN]).then_inc(S["out"], 16)
                sp.wait_ge(S["out"], 16)

            @block.vector
            def _(dve):
                dve.sem_inc(S["x1"], 2 * SUB)
                dve.wait_ge(S["w"], 16 * 3)

                def body(k, i, s):
                    dve.wait_ge(l_in[s], i * 32 + 32)
                    dve.wait_ge(x1_s[s], i * 32)
                    for j in range(SUB):
                        t = k * SUB + j
                        dve.scalar_tensor_tensor(x1[0:TN, s, j], K.acc[0:TN, bass.ds(t, 1), :].rearrange("p a f -> p (a f)"),
                                                 K.dinv[0:TN, bass.ds(t, 1)], pre[0:TN, s, j], ALU.mult, ALU.add
                                                 ).then_inc(S["x1"], 1)
                    dve.wait_ge(S["x1"], k * SUB + 3 * SUB)
                    for j in range(SUB):
                        dve.bn_stats(st6[0:TN, j], x1[0:TN, s, j]).then_inc(S["st"], 1)
                    dve.wait_ge(S["st"], k * SUB + SUB)
                    dve.sem_inc(S["pass"], 1)
                    for j in range(SUB):
                        dve.bn_aggr(mv[0:TN, j], st6[0:TN, j]).then_inc(S["mv"], 1)
                    dve.wait_ge(S["mv"], k * SUB + SUB)
                    dve.tensor_scalar(rs[0:TN, :, 0], mv[0:TN, :, 1], EPS, None, ALU.add).then_inc(S["eps"], 1)
                    dve.wait_ge(S["root"], k + 1)
                    dve.reciprocal(rs[0:TN, :, 0], rs[0:TN, :, 1]).then_inc(S["rec"], 1)
                    dve.wait_ge(S["rec"], k + 1)
                    dve.wait_ge(S["turned"], i * (2 * KC))
                    for j in range(SUB):
                        dve.tensor_scalar(xf[0:TN, s, j], x1[0:TN, s, j], mv[0:TN, j, 0:1], rs[0:TN, j, 0:1],
                                          ALU.subtract, ALU.mult).then_inc(S["xf"], 1)
                    dve.wait_ge(S["xf"], k * SUB + SUB)
                blocks(dve, body)
                dve.wait_ge(S["h_sb"], NB)
                v4 = "p t (h e) -> p t h e"
                n = 0
                shape = [TN, NT, GW]
                dve.tensor_copy(K.hrow[0:TN, :, 0:GW], hg[0:TN]).then_inc(S["row"], 1)
                for a, out in ((0, K.hrow[0:TN, :, GW:ROW]), (1, K.adst[0:TN])):
                    dve.tensor_tensor(prod[0:TN], hg[0:TN], att[0:TN, a].unsqueeze(1).to_broadcast(shape), ALU.mult
                                      ).then_inc(S["prod"], 1)
                    dve.wait_ge(S["prod"], a + 1)
                    dve.tensor_reduce(out, prod[0:TN].rearrange(v4, h=GH), AX.X, ALU.add).then_inc(S["row"], 1)
                    dve.wait_ge(S["row"], a + 2)
                q = slice(0, TN)
                left = K.hrow[q, :, GW:ROW]
                for v in range(PARTS):
                    part = trow[q, :, ROW:TROW].bitcast(BF16)[:, :, v * GH:(v + 1) * GH]
                    dve.tensor_copy(part, left).then_inc(S["part"], 1)
                    dve.wait_ge(S["part"], 2 * v + 1)
                    if v < PARTS - 1:
                        rest = prod[q, :, v * GH:(v + 1) * GH]
                        dve.tensor_tensor(rest, left, part, ALU.subtract).then_inc(S["part"], 1)
                        dve.wait_ge(S["part"], 2 * v + 2)
                        left = rest
                dve.tensor_copy(trow[q, :, 0:ROW], K.hrow[q]).then_inc(S["trow"], 1)
                dve.sem_inc(S["trow"], 1)

            @block.scalar
            def _(act):
                def body(k, i, s):
                    act.wait_ge(S["eps"], k + 1)
                    act.activation(rs[0:TN, :, 1], rs[0:TN, :, 0], ACT.Sqrt).then_inc(S["root"], 1)
                    act.wait_ge(xf_s[s], i * 16)
                    for c in range(KC):
                        act.wait_ge(S["turned"], k * KC + c + 1)
                        act.copy(xfT[:, s, c], ptr[:, s, c, 0:BN]).then_inc(S["xfT"], 1)
                    act.wait_ge(S["h"], k + 1)
                    act.copy(hg[0:TN, bass.ds(k * SUB, SUB), :], ph[0:TN, s, 0:SUB * GW].rearrange("p (j o) -> p j o", j=SUB)
                             ).then_inc(S["h_sb"], 1)
                blocks(act, body)

            @block.tensor
            def _(pe):
                pe.wait_ge(S["w"], 16 * 3)

                def body(k, i, s):
                    pe.wait_ge(S["xf"], k * SUB + SUB)
                    pe.wait_ge(S["xfT"], i * (2 * KC))
                    for c in range(KC):
                        for j in range(SUB):
                            mm = pe.transpose(ptr[:, s, c, j * TN:(j + 1) * TN], xf[0:TN, s, j, c * P:(c + 1) * P],
                                              K.ident[0:TN, 0:TN])
                        mm.then_inc(S["turned"], 1)
                    pe.wait_ge(S["xfT"], k * KC + KC)
                    pe.wait_ge(S["h_sb"], i * 2)
                    for j in range(SUB):
                        for c in range(KC):
                            mm = pe.matmul(ph[0:TN, s, j * GW:(j + 1) * GW], xfT[:, s, c, j * TN:(j + 1) * TN], wg[:, c],
                                           start=c == 0, stop=c == KC - 1, skip_group_check=True)
                    mm.then_inc(S["h"], 1)
                blocks(pe, body)


def gat_tables(nc, K):
    G, T = G_GAT, G_GAT * P
    with ExitStack() as ctx:
        m = Mem(nc, ctx)
        step = m.sb("n_step", [P, G])
        at = m.sb("n_at", [P, G, NT])
        first = m.sb("n_first", [P, G])
        diag = m.sb("n_diag", [P, 2, P])
        pt = m.ps("n_pt", [P, 2, 512])
        pc = m.ps("n_pc", [P, 2, 512])
        c, tables, diag_s, spread, turned, used = (m.sem("n_" + x) for x in (
            "c", "tables", "diag", "spread", "turned", "used"))
        with nc.Block() as block:
            @block.vector
            def _(dve):
                n = [0]

                def done(ins):
                    n[0] += 1
                    ins.then_inc(c, 1)
                    dve.wait_ge(c, n[0])

                both = [P, G, NT]
                for g in range(G):
                    done(dve.tensor_scalar(step[:, g:g + 1], K.part[:], float(P * g), None, ALU.add))
                st = step[:].unsqueeze(2).to_broadcast(both)
                starts = K.gat_start[:].unsqueeze(1).to_broadcast(both)
                ends = K.gat_end[:].unsqueeze(1).to_broadcast(both)
                done(dve.tensor_tensor(at[:], ends, st, ALU.is_le))
                done(dve.tensor_tensor(K.step_tile[:], starts, st, ALU.is_le))
                done(dve.tensor_tensor(K.step_tile[:], K.step_tile[:], at[:], ALU.subtract))
                dve.sem_inc(tables, 1)
                done(dve.tensor_tensor(at[:], starts, st, ALU.is_equal))
                done(dve.tensor_reduce(first[:], at[:], AX.X, ALU.add))
                done(dve.scalar_tensor_tensor(K.last[:], ends, -1.0, st, ALU.add, ALU.is_equal))
                for g in range(G):
                    if g >= 2:
                        dve.wait_ge(spread, g - 1)
                    dve.tensor_scalar(diag[:, g % 2], K.ident[:], first[:, g:g + 1], -BIG, ALU.mult, ALU.mult
                                      ).then_inc(diag_s, 1)
                    dve.wait_ge(spread, g + 1)
                    dve.tensor_copy(K.cut[:, g * P:(g + 1) * P], pc[:, g % 2, 0:P]).then_inc(used, 1)
                    dve.wait_ge(turned, g + 1)
                    dve.tensor_copy(K.tile_step[0:NT, g * P:(g + 1) * P], pt[0:NT, g % 2, 0:P]).then_inc(used, 1)

            @block.tensor
            def _(pe):
                pe.wait_ge(tables, 1)
                for g in range(G):
                    if g >= 2:
                        pe.wait_ge(used, 2 * (g - 1))
                    pe.wait_ge(diag_s, g + 1)
                    pe.matmul(pc[:, g % 2, 0:P], K.ones[:], diag[:, g % 2], start=True, stop=True).then_inc(spread, 1)
                    pe.transpose(pt[0:NT, g % 2, 0:P], K.step_tile[:, g], K.ident[:]).then_inc(turned, 1)


def gat_max(nc, K):
    W = BATCH
    rounds = S_GAT // (W * HALVES)
    HW = W * GH
    with ExitStack() as ctx:
        m = Mem(nc, ctx)
        at = m.sb("x_at", [P, HALVES, W], U32)
        rows = m.sb("x_rows", [P, HALVES, W, TROW])
        other = m.sb("x_other", [P, HALVES, W, TN], BF16)
        neg = m.sb("x_neg", [P, P], BF16)
        ident_h = m.sb("x_ident", [P, P], BF16)
        pick_f = m.sb("x_pick_f", [P, HW])
        pick = m.sb("x_pick", [P, HW], BF16)
        aT = m.sb("x_aT", [P, HALVES, P], BF16)
        asr = m.sb("x_asr", [P, HALVES, PARTS, W, GH], BF16)
        px = m.ps("x_px", [P, 2, 2, GH, P])
        pt = m.ps("x_pt", [P, HALVES, 1024], BF16)
        S = {n: m.sem("x_" + n) for n in ("set", "neg", "at", "pass", "other", "asr", "kept", "turned", "aT", "px", "mx")}
        got = [m.gather_sem(f"x_got{h}") for h in range(HALVES)]
        with nc.Block() as block:
            @block.gpsimd
            def _(pool):
                with pool.Fori(0, rounds) as i:
                    for h in range(HALVES):
                        pool.wait_ge(S["at"], i * HALVES + h + 1)
                        pool.wait_ge(S["kept"], i * HALVES + h + 1)
                        pool.sem_inc(S["pass"], 1)
                        for b in range(W):
                            pool.indirect_dma_start(
                                out=rows[:, h, b], out_offset=None, in_=K.gtab,
                                in_offset=bass.IndirectOffsetOnAxis(ap=at[:, h, b:b + 1], axis=0)
                            ).then_inc(got[h], 16)

            @block.scalar
            def _(act):
                act.sem_inc(S["kept"], 2)
                for h in range(HALVES):
                    act.copy(at[:, h], K.gat_srcT[:, h * W:(h + 1) * W]).then_inc(S["at"], 1)
                with act.Fori(0, rounds) as i:
                    for h in range(HALVES):
                        n = i * HALVES + h
                        act.wait_ge(got[h], (i + 1) * (16 * W))
                        act.wait_ge(S["turned"], i * HALVES)
                        act.copy(asr[:, h], rows[:, h, :, ROW:TROW].bitcast(BF16).rearrange("p w (v g) -> p v w g", v=PARTS)
                                 ).then_inc(S["asr"], 1)
                        act.copy(K.feat[:, bass.ds(n * W, W), :], rows[:, h, :, 0:ROW]).then_inc(S["kept"], 1)
                        act.copy(at[:, h], K.gat_srcT[:, bass.ds((n + HALVES) * W, W)]).then_inc(S["at"], 1)
                        act.wait_ge(S["turned"], n + 1)
                        act.wait_ge(S["px"], i * (HALVES * W // 2))
                        act.copy(aT[0:PARTS * HW, h], pt[0:PARTS * HW, h, 0:P]).then_inc(S["aT"], 1)

            @block.tensor
            def _(pe):
                pe.wait_ge(S["neg"], 3)
                with pe.Fori(0, rounds) as i:
                    for h in range(HALVES):
                        n = i * HALVES + h
                        pe.wait_ge(S["asr"], n + 1)
                        pe.wait_ge(S["aT"], i * HALVES)
                        pe.transpose(pt[0:PARTS * HW, h, 0:P], asr[:, h].rearrange("p v w g -> p (v w g)"), ident_h[:]
                                     ).then_inc(S["turned"], 1)
                        pe.wait_ge(S["aT"], n + 1)
                        pe.wait_ge(S["other"], n + 1)
                        for b in range(W):
                            pair, slot = b // 2, (b // 2) % 2
                            if b % 2 == 0:
                                pe.wait_ge(S["mx"], n * (W // 2) + pair + 1)
                            pe.matmul(px[0:TN, slot, b % 2], other[:, h, b], neg[:].unsqueeze(1).to_broadcast([P, GH, P]),
                                      start=True, stop=False, skip_group_check=True)
                            for g in range(GH):
                                r = b * GH + g
                                mm = pe.matmul(px[0:TN, slot, b % 2, g],
                                               pick[0:PARTS * HW, r:r + 1].to_broadcast([PARTS * HW, TN]),
                                               aT[0:PARTS * HW, h], start=False, stop=g == GH - 1, skip_group_check=True)
                            if b % 2 == 1:
                                mm.then_inc(S["px"], 1)

            @block.vector
            def _(dve):
                dve.tensor_scalar(neg[:], K.ident[:], -BIG, None, ALU.mult).then_inc(S["neg"], 1)
                dve.tensor_copy(ident_h[:], K.ident[:]).then_inc(S["neg"], 1)
                dve.tensor_tensor(pick_f[:], K.ident[:, 0:HW], K.ident[:, HW:2 * HW], ALU.add).then_inc(S["set"], 1)
                dve.wait_ge(S["set"], 1)
                dve.tensor_tensor(pick[:], pick_f[:], K.ident[:, 2 * HW:3 * HW], ALU.add).then_inc(S["neg"], 1)
                dve.memset(K.feat[:, S_GAT:G_GAT * P, :], 0.0).then_inc(S["set"], 1)
                dve.memset(K.mx[:, :, S_GAT:G_GAT * P], 0.0).then_inc(S["set"], 1)
                dve.sem_inc(S["mx"], 2)
                with dve.Fori(0, rounds) as i:
                    for h in range(HALVES):
                        n = i * HALVES + h
                        dve.wait_ge(S["px"], i * (HALVES * W // 2))
                        shape = [P, W, TN]
                        dve.tensor_tensor(other[:, h], K.iota[:, 0:TN].unsqueeze(1).to_broadcast(shape),
                                          K.gat_dstT[:, bass.ds(n * W, W)].unsqueeze(2).to_broadcast(shape),
                                          ALU.not_equal).then_inc(S["other"], 1)
                    for h in range(HALVES):
                        n = i * HALVES + h
                        for j in range(W // 2):
                            dve.wait_ge(S["px"], n * (W // 2) + j + 1)
                            dve.tensor_reduce(K.mx[0:TN, :, bass.ds(n * W + 2 * j, 2)].rearrange("p g w -> p w g"),
                                              px[0:TN, j % 2], AX.X, ALU.max).then_inc(S["mx"], 1)


def by_tile(nc, K, tag, values, columns_last, n_cols, select, out):
    G, B = G_GAT, 3
    banks = -(-G // B)
    with ExitStack() as ctx:
        m = Mem(nc, ctx)
        col = m.sb(tag + "_col", [P, 2, G * P])
        turned_sb = m.sb(tag + "_turned_sb", [P, banks, B, P])
        pt = m.ps(tag + "_pt", [P, banks, 512])
        po = m.ps(tag + "_po", [P, 2, 512])
        passed, ready, turned, copied, summed, taken = (m.sem(tag + x) for x in (
            "_passed", "_ready", "_turned", "_copied", "_summed", "_taken"))
        with nc.Block() as block:
            @block.gpsimd
            def _(pool):
                pool.sem_inc(turned, 2 * banks)
                with pool.Fori(0, n_cols // 2) as i:
                    for s in range(2):
                        c = i * 2 + s
                        if columns_last:
                            column = values[0:TN, :, bass.ds(c, 1)].rearrange("p s c -> p (s c)")
                        else:
                            column = values[0:TN, bass.ds(c, 1), :].rearrange("p c s -> p (c s)")
                        pool.wait_ge(turned, c * banks + banks)
                        pool.tensor_copy(col[0:TN, s], column).then_inc(ready, 1)

            @block.tensor
            def _(pe):
                pe.sem_inc(taken, 2)
                with pe.Fori(0, n_cols // 2) as i:
                    for s in range(2):
                        c = i * 2 + s
                        pe.wait_ge(ready, c + 1)
                        pe.wait_ge(copied, c * banks)
                        for g in range(G):
                            b = g // B
                            mm = pe.transpose(pt[:, b, (g % B) * P:(g % B) * P + TN], col[0:TN, s, g * P:(g + 1) * P],
                                              K.ident[0:TN, 0:TN])
                            if g % B == B - 1 or g == G - 1:
                                mm.then_inc(turned, 1)
                        pe.wait_ge(taken, c + 1)
                        for g in range(G):
                            if g % B == 0:
                                pe.wait_ge(copied, c * banks + g // B + 1)
                            mm = pe.matmul(po[0:TN, s, 0:NT], turned_sb[:, g // B, g % B, 0:TN], select[:, g],
                                           start=g == 0, stop=g == G - 1)
                        mm.then_inc(summed, 1)

            @block.scalar
            def _(act):
                with act.Fori(0, n_cols) as c:
                    act.wait_ge(summed, c)
                    for b in range(banks):
                        w = min(B, G - b * B)
                        act.wait_ge(turned, c * banks + 2 * banks + b + 1)
                        act.copy(turned_sb[:, b, 0:w, 0:TN], pt[:, b, 0:w * P].rearrange("p (g n) -> p g n", n=P)[:, :, 0:TN]
                                 ).then_inc(copied, 1)

            @block.vector
            def _(dve):
                with dve.Fori(0, n_cols // 2) as i:
                    for s in range(2):
                        c = i * 2 + s
                        dve.wait_ge(summed, c + 1)
                        dve.sem_inc(passed, 1)
                        dve.tensor_copy(out[0:TN, :, bass.ds(c, 1)].rearrange("p t c -> p (t c)"), po[0:TN, s, 0:NT]
                                        ).then_inc(taken, 1)


def scan_max(nc, K):
    with ExitStack() as ctx:
        m = Mem(nc, ctx)
        scanned = m.sem("y_scanned")
        with nc.Block() as block:
            @block.vector
            def _(dve):
                for g in range(GH):
                    dve.tensor_tensor_scan(K.mx[0:TN, g], K.cut[0:TN], K.mx[0:TN, g], -BIG, ALU.add, ALU.max
                                           ).then_inc(scanned, 1)


def gat_spread(nc, K, peak, own):
    C, G3 = 2 * GH, 3
    PART = G_GAT * P // G3
    with ExitStack() as ctx:
        m = Mem(nc, ctx)
        am = m.sb("e_am", [P, C, NT])
        amT = m.sb("e_amT", [P, C, P])
        pt = m.ps("e_pt", [P, 2, 4, P])
        pe_s = m.ps("e_ps", [P, G3, 512])
        passed, c, turned, amT_s, spread, taken, ex = (m.sem("e_" + x) for x in (
            "passed", "c", "turned", "amT", "spread", "taken", "ex"))
        q = slice(0, TN)
        with nc.Block() as block:
            @block.vector
            def _(dve):
                n = [0]

                def done(ins):
                    n[0] += 1
                    ins.then_inc(c, 1)
                    dve.wait_ge(c, n[0])

                asrc = K.hrow[q, :, GW:ROW]
                ad, M = am[q, 0:GH].rearrange("p g t -> p t g"), am[q, GH:C].rearrange("p g t -> p t g")
                done(dve.tensor_tensor(M, peak[q], asrc, ALU.max))
                done(dve.tensor_copy(ad, K.adst[q]))
                done(dve.tensor_tensor(M, M, ad, ALU.add))
                done(dve.tensor_tensor(own[q], asrc, K.adst[q], ALU.add))
                done(dve.scalar_tensor_tensor(M, M, 0.2, M, ALU.mult, ALU.max))
                done(dve.scalar_tensor_tensor(own[q], own[q], 0.2, own[q], ALU.mult, ALU.max))
                done(dve.tensor_tensor(own[q], own[q], M, ALU.subtract))
                dve.wait_ge(turned, 2)
                for b in range(2):
                    dve.tensor_copy(amT[0:NT, b * 4:(b + 1) * 4, 0:TN], pt[0:NT, b, :, 0:TN]).then_inc(amT_s, 1)
                with dve.Fori(0, C) as i:
                    for b in range(G3):
                        dve.wait_ge(spread, i * G3 + b + 1)
                        dve.sem_inc(passed, 1)
                        dve.tensor_copy(K.spread[q, bass.ds(i, 1), b * PART:(b + 1) * PART].rearrange("p c s -> p (c s)"),
                                        pe_s[q, b, 0:PART]).then_inc(taken, 1)

            @block.scalar
            def _(act):
                act.wait_ge(c, 7)
                act.activation(own[q], own[q], ACT.Exp).then_inc(ex, 1)

            @block.tensor
            def _(pe):
                pe.sem_inc(taken, G3)
                pe.wait_ge(c, 7)
                for b in range(2):
                    for k in range(4):
                        mm = pe.transpose(pt[0:NT, b, k, 0:TN], am[q, b * 4 + k], K.ident[q, q])
                    mm.then_inc(turned, 1)
                pe.wait_ge(amT_s, 2)
                for k in range(C):
                    for b in range(G3):
                        pe.wait_ge(taken, k * G3 + b + 1)
                        pe.matmul(pe_s[q, b, 0:PART], amT[0:NT, k, 0:TN], K.tile_step[0:NT, b * PART:(b + 1) * PART],
                                  start=True, stop=True).then_inc(spread, 1)


def gat_sum(nc, K):
    W = BATCH
    rounds = S_GAT // (W * HALVES)
    R = rounds * HALVES
    with ExitStack() as ctx:
        m = Mem(nc, ctx)
        hot = m.sb("s_hot", [P, HALVES, W, TN])
        hotT = m.sb("s_hotT", [P, HALVES, W, P])
        z = m.sb("s_z", [P, HALVES, W, GH])
        z2 = m.sb("s_z2", [P, HALVES, W, GH])
        msg = m.sb("s_msg", [P, HALVES, W, ROW])
        pt = m.ps("s_pt", [P, HALVES, 2, 512])
        pb = m.ps("s_pb", [P, HALVES, 512])
        po = m.ps("s_po", [P, HALVES, 512])
        S = {n: m.sem("s_" + n) for n in ("hot", "turned", "hotT", "pb", "z", "e", "msg", "po", "sum", "pass")}
        with nc.Block() as block:
            @block.vector
            def _(dve):
                def build(n, h):
                    if not (isinstance(n, int) and n < 2):
                        dve.wait_ge(S["po"], n - 1)
                    shape = [P, W, TN]
                    dve.tensor_tensor(hot[:, h], K.iota[:, 0:TN].unsqueeze(1).to_broadcast(shape),
                                      K.gat_dstT[:, bass.ds(n * W, W)].unsqueeze(2).to_broadcast(shape),
                                      ALU.is_equal).then_inc(S["hot"], 1)

                def weigh(n, h):
                    f = K.feat[:, bass.ds(n * W, W), :]
                    ps = pb[:, h, 0:W * 2 * GH].rearrange("p (w g) -> p w g", w=W)
                    dve.wait_ge(S["pb"], n + 1)
                    dve.tensor_tensor(z[:, h], f[:, :, GW:ROW], ps[:, :, 0:GH], ALU.add).then_inc(S["z"], 1)
                    dve.wait_ge(S["z"], n * 4 + 1)
                    dve.scalar_tensor_tensor(z[:, h], z[:, h], 0.2, z[:, h], ALU.mult, ALU.max).then_inc(S["z"], 1)
                    dve.wait_ge(S["z"], n * 4 + 2)
                    dve.tensor_tensor(z2[:, h], z[:, h], ps[:, :, GH:2 * GH], ALU.subtract).then_inc(S["z"], 1)
                    dve.wait_ge(S["z"], n * 4 + 3)
                    dve.tensor_scalar(z2[:, h], z2[:, h], 0.0, None, ALU.min).then_inc(S["z"], 1)
                    dve.wait_ge(S["e"], n + 1)
                    w4 = msg[:, h, :, GW:ROW].unsqueeze(3).to_broadcast([P, W, GH, NE])
                    dve.tensor_tensor(msg[:, h, :, 0:GW].rearrange("p w (h e) -> p w h e", h=GH),
                                      f[:, :, 0:GW].rearrange("p w (h e) -> p w h e", h=GH), w4,
                                      ALU.mult).then_inc(S["msg"], 1)

                def take(n, h):
                    dve.wait_ge(S["po"], n + 1)
                    dve.sem_inc(S["pass"], 1)
                    dve.tensor_copy(K.feat[0:TN, bass.ds(n * W, W), :],
                                    po[0:TN, h, 0:W * ROW].rearrange("p (w c) -> p w c", w=W)).then_inc(S["sum"], 1)

                build(0, 0)
                build(1, 1)
                weigh(0, 0)
                with dve.Fori(1, rounds) as i:
                    for h in range(HALVES):
                        n = i * HALVES + h
                        build(n, h)
                        weigh(n - 1, 1 - h)
                        take(n - 2, h)
                weigh(R - 1, 1)
                take(R - 2, 0)
                take(R - 1, 1)

            @block.scalar
            def _(act):
                def copies(n, h):
                    if not (isinstance(n, int) and n < 2):
                        act.wait_ge(S["pb"], n - 1)
                    for v in range(2):
                        act.wait_ge(S["turned"], n * 2 + v + 1)
                        act.copy(hotT[0:TN, h, v * 4:(v + 1) * 4],
                                 pt[0:TN, h, v].rearrange("p (w e) -> p w e", w=4)).then_inc(S["hotT"], 1)

                def exps(n, h):
                    act.wait_ge(S["z"], n * 4 + 4)
                    if not (isinstance(n, int) and n < 2):
                        act.wait_ge(S["po"], n - 1)
                    act.activation(msg[:, h, :, GW:ROW], z2[:, h], ACT.Exp).then_inc(S["e"], 1)

                copies(0, 0)
                copies(1, 1)
                exps(0, 0)
                with act.Fori(1, rounds) as i:
                    for h in range(HALVES):
                        n = i * HALVES + h
                        copies(n, h)
                        exps(n - 1, 1 - h)
                exps(R - 1, 1)

            @block.tensor
            def _(pe):
                def turn(n, h):
                    pe.wait_ge(S["hot"], n + 1)
                    if not (isinstance(n, int) and n < 2):
                        pe.wait_ge(S["hotT"], n * 2 - 2)
                    for b in range(W):
                        mm = pe.transpose(pt[0:TN, h, b // 4, (b % 4) * P:(b % 4 + 1) * P], hot[:, h, b], K.ident[:])
                        if b % 4 == 3:
                            mm.then_inc(S["turned"], 1)

                def spread(n, h):
                    pe.wait_ge(S["hotT"], n * 2 + 2)
                    if not (isinstance(n, int) and n < 2):
                        pe.wait_ge(S["z"], n * 4 - 5)
                    for b in range(W):
                        mm = pe.matmul(pb[:, h, b * 2 * GH:(b + 1) * 2 * GH], hotT[0:TN, h, b],
                                       K.spread[0:TN, :, bass.ds(n * W + b, 1)].rearrange("p c s -> p (c s)"),
                                       start=True, stop=True, skip_group_check=True)
                    mm.then_inc(S["pb"], 1)

                def add_up(n, h):
                    pe.wait_ge(S["msg"], n + 1)
                    if not (isinstance(n, int) and n < 2):
                        pe.wait_ge(S["sum"], n - 1)
                    for b in range(W):
                        mm = pe.matmul(po[0:TN, h, b * ROW:(b + 1) * ROW], hot[:, h, b], msg[:, h, b],
                                       start=True, stop=True, skip_group_check=True)
                    mm.then_inc(S["po"], 1)

                turn(0, 0)
                spread(0, 0)
                turn(1, 1)
                spread(1, 1)
                add_up(0, 0)
                with pe.Fori(1, rounds) as i:
                    for h in range(HALVES):
                        n = i * HALVES + h
                        turn(n, h)
                        spread(n, h)
                        add_up(n - 1, 1 - h)
                add_up(R - 1, 1)


def gat_own(nc, K, own, sums):
    with ExitStack() as ctx:
        m = Mem(nc, ctx)
        c = m.sem("o_c")
        q = slice(0, TN)
        v4 = "p t (h e) -> p t h e"
        with nc.Block() as block:
            @block.vector
            def _(dve):
                dve.tensor_tensor(K.gsum[q, :, 0:GW].rearrange(v4, h=GH), K.hrow[q, :, 0:GW].rearrange(v4, h=GH),
                                  own[q].unsqueeze(3).to_broadcast([TN, NT, GH, NE]), ALU.mult).then_inc(c, 1)
                dve.tensor_tensor(K.gsum[q, :, GW:ROW], sums[q, :, GW:ROW], own[q], ALU.add).then_inc(c, 1)
                dve.wait_ge(c, 1)
                dve.tensor_tensor(K.gsum[q, :, 0:GW], K.gsum[q, :, 0:GW], sums[q, :, 0:GW], ALU.add).then_inc(c, 1)


def gates(nc, K, A):
    with ExitStack() as ctx:
        m = Mem(nc, ctx)
        row = m.sb("e_row", [P, 3, GW])
        agg = m.sb("e_agg", [P, NT, GW])
        sq = m.sb("e_sq", [P, NT, GW])
        den = m.sb("e_den", [P, NT, GH])
        st = m.sb("e_st", [P, 4, NT])
        sc = m.sb("e_sc", [P, NT, NE])
        rank = m.sb("e_rank", [P, NT, NE])
        cmp_ = m.sb("e_cmp", [P, NT])
        w_s, v, root, ex = (m.sem("e_" + x) for x in ("w", "v", "root", "exp"))
        q = slice(0, TN)
        with nc.Block() as block:
            @block.sync
            def _(sp):
                for n, a in enumerate((A.b_gat, A.ln_gamma, A.ln_beta)):
                    sp.dma_start(row[:, n], a.rearrange("(a o) -> a o", a=1).to_broadcast([P, GW])).then_inc(w_s, 16)

            @block.scalar
            def _(act):
                act.wait_ge(v, 10)
                act.activation(st[q, 1], st[q, 1], ACT.Sqrt).then_inc(root, 1)
                act.wait_ge(root, 2)
                act.activation(sc[q], sc[q], ACT.Exp).then_inc(ex, 1)

            @block.vector
            def _(dve):
                n = [0]

                def step(ins):
                    n[0] += 1
                    ins.then_inc(v, 1)
                    dve.wait_ge(v, n[0])

                def wide(ap, width=GW):
                    return ap.unsqueeze(2).to_broadcast([TN, NT, width])

                def param(r):
                    return row[q, r].unsqueeze(1).to_broadcast([TN, NT, GW])

                dve.wait_ge(w_s, 48)
                step(dve.tensor_scalar(den[q], K.gsum[q, :, GW:ROW], 1e-16, None, ALU.add))
                step(dve.reciprocal(den[q], den[q]))
                step(dve.tensor_tensor(agg[q].rearrange("p t (h e) -> p t h e", h=GH),
                                       K.gsum[q, :, 0:GW].rearrange("p t (h e) -> p t h e", h=GH),
                                       den[q].unsqueeze(3).to_broadcast([TN, NT, GH, NE]), ALU.mult))
                step(dve.tensor_tensor(agg[q], agg[q], param(0), ALU.add))
                step(dve.tensor_reduce(st[q, 0], agg[q], AX.X, ALU.add))
                step(dve.tensor_scalar(st[q, 0], st[q, 0], 1.0 / GW, None, ALU.mult))
                step(dve.tensor_tensor(agg[q], agg[q], wide(st[q, 0]), ALU.subtract))
                step(dve.tensor_tensor(sq[q], agg[q], agg[q], ALU.mult))
                step(dve.tensor_reduce(st[q, 1], sq[q], AX.X, ALU.add))
                step(dve.tensor_scalar(st[q, 1], st[q, 1], 1.0 / GW, EPS, ALU.mult, ALU.add))
                dve.wait_ge(root, 1)
                step(dve.reciprocal(st[q, 1], st[q, 1]))
                step(dve.tensor_tensor(agg[q], agg[q], wide(st[q, 1]), ALU.mult))
                step(dve.tensor_tensor(agg[q], agg[q], param(1), ALU.mult))
                step(dve.tensor_tensor(agg[q], agg[q], param(2), ALU.add))
                step(dve.tensor_reduce(sc[q], agg[q].rearrange("p t (h e) -> p t e h", h=GH), AX.X, ALU.add))
                step(dve.tensor_scalar(sc[q], sc[q], 1.0 / GH, None, ALU.mult))
                step(dve.tensor_reduce(st[q, 2], sc[q], AX.X, ALU.max))
                for e in range(NE):
                    first = True
                    for f in range(NE):
                        if f == e:
                            continue
                        out = rank[q, :, e] if first else cmp_[q]
                        step(dve.tensor_tensor(out, sc[q, :, f], sc[q, :, e], ALU.is_ge if f < e else ALU.is_gt))
                        if not first:
                            step(dve.tensor_tensor(rank[q, :, e], rank[q, :, e], cmp_[q], ALU.add))
                        first = False
                step(dve.tensor_scalar(rank[q], rank[q], 1.5, None, ALU.is_lt))
                step(dve.tensor_tensor(sc[q], sc[q], wide(st[q, 2], NE), ALU.subtract))
                dve.sem_inc(root, 1)
                dve.wait_ge(ex, 1)
                step(dve.tensor_tensor(sc[q], sc[q], rank[q], ALU.mult))
                step(dve.tensor_reduce(st[q, 3], sc[q], AX.X, ALU.add))
                step(dve.reciprocal(st[q, 3], st[q, 3]))
                step(dve.tensor_tensor(K.gate[q], sc[q], wide(st[q, 3], NE), ALU.mult))


def experts(nc, K, A):
    MC = FF // P
    with ExitStack() as ctx:
        m = Mem(nc, ctx)
        w1 = m.sb("f_w1", [P, NE, KC, FF])
        w2 = m.sb("f_w2", [P, NE, MC, D])
        b1 = m.sb("f_b1", [P, NE, MC])
        b2 = m.sb("f_b2", [P, NE, D])
        xfT = m.sb("f_xfT", [P, 2, KC, BN])
        hh = m.sb("f_hh", [P, 2, MC, BN])
        y = m.sb("f_y", [P, 2, SUB, D])
        ph = m.ps("f_ph", [P, 4, 512])
        py = m.ps("f_py", [P, 2, 2, 512])
        S = {n: m.sem("f_" + n) for n in ("w", "free", "ph", "hh", "py", "y", "yb")}
        l_x = [m.sem(f"f_lx{s}") for s in range(2)]
        l_y = [m.sem(f"f_ly{s}") for s in range(2)]
        out_s = [m.sem(f"f_out{s}") for s in range(2)]
        NY = NE * SUB * 2
        with nc.Block() as block:
            @block.sync
            def _(sp):
                for e in range(NE):
                    sp.dma_start(w1[:, e], A.W1[e].rearrange("(c p) o -> p c o", p=P)).then_inc(S["w"], 16)
                    sp.dma_start(w2[:, e], A.W2[e].rearrange("(c p) o -> p c o", p=P)).then_inc(S["w"], 16)
                    sp.dma_start(b2[:, e], A.b2f[e:e + 1].to_broadcast([P, D])).then_inc(S["w"], 16)
                    with nc.allow_non_contiguous_dma(reason="biases"):
                        sp.dma_start(b1[:, e], A.b1f[e].rearrange("(c p) -> p c", p=P)).then_inc(S["w"], 16)

                def load(k, i, s):
                    sp.wait_ge(S["ph"], k * (NE * MC) + NE * MC)
                    sp.dma_start(xfT[:, s], K.xfT_d[bass.ds(k, 1)].rearrange("a p c n -> p (a c) n")).then_inc(l_x[s], 16)
                    sp.wait_ge(out_s[s], i * 32)
                    for p0, p1 in ((0, 120), (120, TN)):
                        sp.dma_start(y[p0:p1, s], K.x1_d[bass.ds(k, 1)].rearrange("a p j f -> p (a j) f")[p0:p1]
                                     ).then_inc(l_y[s], 16)

                def store(k, i, s):
                    sp.wait_ge(S["y"], k * NY + NY)
                    for p0, p1 in ((0, 120), (120, TN)):
                        sp.dma_start(A.out[bass.ds(k * BN, BN)].rearrange("(j p) f -> p j f", p=TN)[p0:p1], y[p0:p1, s]
                                     ).then_inc(out_s[s], 16)

                load(0, 0, 0)
                load(1, 0, 1)
                with sp.Fori(0, (NB - 3) // 2) as i:
                    for s in range(2):
                        store(i * 2 + s, i, s)
                        load(i * 2 + 2 + s, i + 1, s)
                store(NB - 3, 0, 0)
                load(NB - 1, NB // 2, 0)
                store(NB - 2, 0, 1)
                store(NB - 1, 0, 0)
                for s in range(2):
                    sp.wait_ge(out_s[s], 32 * ((NB + 1 - s) // 2))

            @block.tensor
            def _(pe):
                pe.sem_inc(S["ph"], 2 * NE * MC)
                pe.wait_ge(S["w"], 64 * NE)

                def up(k, s, e):
                    for o in range(MC):
                        n = k * (NE * MC) + e * MC + o
                        pe.wait_ge(S["hh"], n + 1)
                        for c in range(KC):
                            mm = pe.matmul(ph[:, o, 0:BN], w1[:, e, c, o * P:(o + 1) * P], xfT[:, s, c],
                                           start=c == 0, stop=c == KC - 1)
                        mm.then_inc(S["ph"], 1)

                def down(k, s, e):
                    pe.wait_ge(S["hh"], k * (NE * MC) + (e + 1) * MC + MC)
                    pe.wait_ge(S["yb"], k * NE + e + 1)
                    for j in range(SUB):
                        for c in range(MC):
                            mm = pe.matmul(py[0:TN, e % 2, j // 2, (j % 2) * D:(j % 2 + 1) * D],
                                           hh[:, e % 2, c, j * TN:(j + 1) * TN], w2[:, e, c],
                                           start=c == 0, stop=c == MC - 1, skip_group_check=True)
                        mm.then_inc(S["py"], 1)

                def body(k, i, s):
                    pe.wait_ge(l_x[s], i * 16 + 16)
                    up(k, s, 0)
                    for e in range(NE):
                        if e + 1 < NE:
                            up(k, s, e + 1)
                        down(k, s, e)
                blocks(pe, body)

            @block.scalar
            def _(act):
                act.wait_ge(S["w"], 64 * NE)
                act.sem_inc(S["hh"], MC)

                def body(k, i, s):
                    for e in range(NE):
                        if e < 2:
                            act.wait_ge(S["py"], k * (NE * SUB))
                        else:
                            act.wait_ge(S["py"], k * (NE * SUB) + (e - 1) * SUB)
                        for o in range(MC):
                            n = k * (NE * MC) + e * MC + o
                            act.wait_ge(S["ph"], n + 2 * NE * MC + 1)
                            act.activation(hh[:, e % 2, o], ph[:, o, 0:BN], ACT.Gelu, bias=b1[:, e, o:o + 1]
                                           ).then_inc(S["hh"], 1)
                blocks(act, body)

            @block.vector
            def _(dve):
                dve.sem_inc(S["yb"], 2)
                dve.wait_ge(S["w"], 64 * NE)

                def body(k, i, s):
                    dve.wait_ge(l_y[s], i * 32 + 32)
                    for e in range(NE):
                        n0 = k * NY + e * (2 * SUB)
                        for j in range(SUB):
                            dve.wait_ge(S["y"], n0 + (j if e == 0 else j - 0))
                            g = K.gate[0:TN, bass.ds(k * SUB + j, 1), e]
                            dve.scalar_tensor_tensor(y[0:TN, s, j], b2[0:TN, e], g, y[0:TN, s, j], ALU.mult, ALU.add
                                                     ).then_inc(S["y"], 1)
                        for j in range(SUB):
                            if j % 2 == 0:
                                dve.wait_ge(S["py"], k * (NE * SUB) + e * SUB + j + 2)
                            dve.wait_ge(S["y"], n0 + SUB + j)
                            g = K.gate[0:TN, bass.ds(k * SUB + j, 1), e]
                            dve.scalar_tensor_tensor(y[0:TN, s, j], py[0:TN, e % 2, j // 2, (j % 2) * D:(j % 2 + 1) * D],
                                                     g, y[0:TN, s, j], ALU.mult, ALU.add).then_inc(S["y"], 1)
                        dve.wait_ge(S["y"], n0 + 2 * SUB)
                        dve.sem_inc(S["yb"], 1)
                blocks(dve, body)


def program(nc, A):
    with ExitStack() as ctx:
        m = Mem(nc, ctx)

        class K:
            pass
        K.gcn_pairs = m.dram("gcn_pairs", [E_GCN + P, 2], I32)
        K.gat_pairs = m.dram("gat_pairs", [E_GAT + P, 2], I32)
        K.hT_d = m.dram("hT_d", [NB, P, KC, BN])
        K.qT_d = m.dram("qT_d", [NB, P, KC, BN])
        K.xfT_d = m.dram("xfT_d", [NB, P, KC, BN])
        K.pre_d = m.dram("pre_d", [NB, TN, SUB, D])
        K.x1_d = m.dram("x1_d", [NB, TN, SUB, D])
        K.table = m.dram("table", [N, D])
        K.gtab = m.dram("gtab", [N, TROW])
        gcn_td = m.dram("gcn_td", [G_GCN * P], I32)
        constants(nc, m, K)
        K.dinv = m.sb("dinv", [P, NT])
        K.gat_srcT = m.sb("gat_srcT", [P, G_GAT * P], U32)
        K.gat_dstT = m.sb("gat_dstT", [P, G_GAT * P])
        K.gat_start = m.sb("gat_start", [P, NT])
        K.gat_end = m.sb("gat_end", [P, NT])
        K.hrow = m.sb("hrow", [P, NT, ROW])
        K.adst = m.sb("adst", [P, NT, GH])
        with ExitStack() as c1:
            m1 = Mem(nc, c1)
            K.gcn_srcT = m1.sb("gcn_srcT", [P, G_GCN * P], U32)
            K.gcn_dstT = m1.sb("gcn_dstT", [P, G_GCN * P])
            K.gcn_start = m1.sb("gcn_start", [P, NT])
            K.gcn_end = m1.sb("gcn_end", [P, NT])
            K.gcn_tiles = m1.sb("gcn_tiles", [1, G_GCN * P], I32)
            K.xmv = m1.sb("xmv", [P, NT, 2])
            K.xrs = m1.sb("xrs", [P, NT])
            K.hmv = m1.sb("hmv", [P, KC, 2])
            K.kv = m1.sb("kv", [P, KC, P + 1])
            K.degree = m1.sb("degree", [P, NT])
            K.cnt = m1.sb("cnt", [P, NT])
            K.base = m1.sb("base", [P, NT])
            with ExitStack() as c2:
                m2 = Mem(nc, c2)
                load_edges(nc, m2, K, A)
                degrees(nc, K, A)
                sort_edges(nc, K, "ga", K.gat_pairs, GAT_P, GAT_C, K.gat_tile, K.gat_pay)
                step_tables(nc, K, "ga", K.gat_pairs, E_GAT, UNIT_GAT, G_GAT, K.gat_srcT, K.gat_dstT, K.gat_start,
                            K.gat_end)
                counts_of_tiles(nc, K)
                sort_edges(nc, K, "gc", K.gcn_pairs, GCN_P, GCN_C, K.gcn_tile, K.gcn_pay, K.unsorted)
            step_tables(nc, K, "gc", K.gcn_pairs, E_GCN, UNIT_GCN, G_GCN, K.gcn_srcT, K.gcn_dstT, K.gcn_start,
                        K.gcn_end, K.gcn_tiles, gcn_td)
            dense_first(nc, K, A)
            K.acc = m1.sb("acc", [P, NT, D])
            dense_second(nc, K, A)
            gather_sum(nc, K)
            second_norm(nc, K, A)
        K.gsum = m.sb("gsum", [P, NT, ROW])
        K.gate = m.sb("gate", [P, NT, NE])
        with ExitStack() as c3:
            m3 = Mem(nc, c3)
            K.amax = m3.sb("amax", [P, NT, GH])
            K.feat = m3.sb("feat", [P, G_GAT * P, ROW])
            K.step_tile = m3.sb("step_tile", [P, G_GAT, NT])
            K.tile_step = m3.sb("tile_step", [P, G_GAT * P])
            with ExitStack() as c4:
                m4 = Mem(nc, c4)
                K.last = m4.sb("last", [P, G_GAT, NT])
                K.cut = m4.sb("cut", [P, G_GAT * P])
                K.mx = m4.sb("mx", [P, GH, G_GAT * P])
                gat_tables(nc, K)
                gat_max(nc, K)
                scan_max(nc, K)
                by_tile(nc, K, "pk", K.mx, False, GH, K.last, K.amax)
            own = m3.sb("own", [P, NT, GH])
            K.spread = m3.sb("spread", [P, 2 * GH, G_GAT * P])
            gat_spread(nc, K, K.amax, own)
            gat_sum(nc, K)
            sums = m3.sb("sums", [P, NT, ROW])
            by_tile(nc, K, "sm", K.feat, True, ROW, K.step_tile, sums)
            gat_own(nc, K, own, sums)
        gates(nc, K, A)
        experts(nc, K, A)


_ARGS = {
    "x": "x", "src": "src", "dst": "dst", "L0_ffn_edge_index": "edge_index",
    "L0_gnn_b1": "b1", "L0_gnn_gamma": "gamma", "L0_gnn_beta": "beta", "L0_gnn_w2": "w2", "L0_gnn_b2": "b2",
    "L0_gnn_b_gcn": "b_gcn", "L0_mix_wq": "wq", "L0_mix_bq": "bq", "L0_mix_wk": "wk", "L0_mix_bk": "bk",
    "L0_mix_wv": "wv", "L0_mix_bv": "bv", "L0_mix_wo": "wo", "L0_mix_bo": "bo", "L0_ffn_W_gat": "W_gat",
    "L0_ffn_att_src": "att_src", "L0_ffn_att_dst": "att_dst", "L0_ffn_b_gat": "b_gat",
    "L0_ffn_ln_gamma": "ln_gamma", "L0_ffn_ln_beta": "ln_beta", "L0_ffn_W1": "W1", "L0_ffn_b1": "b1f",
    "L0_ffn_W2": "W2", "L0_ffn_b2": "b2f",
}
_TURNED = {"L0_gnn_w1": "w1T", "L0_gnn_w_gcn": "wgT"}


def kernel(**inputs):
    import types

    import numpy as _np
    import concourse.bacc as _bacc
    from concourse import mybir as _mybir
    from concourse.bass_utils import run_bass_kernel_spmd as _run

    nc = _bacc.Bacc("TRN2", target_bir_lowering=False, num_devices=1)
    A = types.SimpleNamespace()
    arrays = {}
    given = [(v, _np.ascontiguousarray(inputs[k])) for k, v in _ARGS.items()]
    given += [(v, _np.ascontiguousarray(_np.transpose(inputs[k]))) for k, v in _TURNED.items()]
    for name, a in given:
        arrays[f"in_{name}"] = a
        A.__dict__[name] = nc.dram_tensor(f"in_{name}", a.shape, _mybir.dt.from_np(a.dtype), kind="ExternalInput").ap()
    A.out = nc.dram_tensor("out_x", (N, D), _mybir.dt.float32, kind="ExternalOutput").ap()
    program(nc, A)
    r = _run(nc, [arrays], core_ids=[0])
    return r.results[0]["out_x"]
```

```python
from contextlib import ExitStack, nullcontext

import concourse.bass as bass
from concourse import mybir

F32 = mybir.dt.float32
I32 = mybir.dt.int32
U32 = mybir.dt.uint32
U16 = mybir.dt.uint16
BF16 = mybir.dt.bfloat16
ALU = mybir.AluOpType
ACT = mybir.ActivationFunctionType
AX = mybir.AxisListType

N = 12500
D = 256
P = 128
TN = 125
NT = N // TN
SUB = 4
BN = SUB * TN
NB = N // BN
KC = D // P
HD = 32
EPS = 1e-5
E_GCN, GCN_P = 200000, 125
E_GAT, GAT_P = 131072, 128
GCN_C, GAT_C = E_GCN // GCN_P, E_GAT // GAT_P
BATCH = 8
HALVES = 2


ROUND = BATCH * HALVES


def steps_for(edges, unit):
    most = (edges + NT * P * unit) // P
    return -(-most // ROUND) * ROUND


UNIT_GCN, UNIT_GAT = 2, 1
S_GCN, S_GAT = steps_for(E_GCN, UNIT_GCN), steps_for(E_GAT, UNIT_GAT)
G_GCN, G_GAT = -(-S_GCN // P), -(-S_GAT // P)
NE, FF = 4, 512
GH = 4
BIG = 1e30
GW = GH * NE
ROW = GW + GH
PARTS = 3
TROW = ROW + PARTS * GH // 2


def blocks(eng, body):
    with eng.Fori(0, NB // 2) as i:
        body(i * 2, i, 0)
        body(i * 2 + 1, i, 1)
    if NB % 2:
        body(NB - 1, NB // 2, 0)


class Mem:

    def __init__(self, nc, ctx):
        self.nc, self.ctx, self.sems, self.kept = nc, ctx, [], []
        ctx.callback(self.clear)

    def clear(self):
        if not self.sems + self.kept:
            return
        with self.nc.Block() as block:
            @block.gpsimd
            def _(pool):
                for s in self.sems + self.kept:
                    pool.sem_clear(s)
        for s in self.sems:
            self.nc.release_semaphore(s)

    def sb(self, name, shape, dt=F32):
        return self.ctx.enter_context(self.nc.sbuf_tensor(name, shape, dt))

    def ps(self, name, shape, dt=F32):
        return self.ctx.enter_context(self.nc.psum_tensor(name, shape, dt))

    def sem(self, name):
        self.sems.append(self.nc.alloc_semaphore(name))
        return self.sems[-1]

    def gather_sem(self, name):
        self.kept.append(self.nc.alloc_semaphore(name))
        return self.kept[-1]

    def dram(self, name, shape, dt=F32):
        return self.nc.dram_tensor(name, shape, dt).ap()


def constants(nc, m, K):
    K.ident = m.sb("ident", [P, P])
    K.ones = m.sb("ones", [P, P])
    K.before = m.sb("before", [P, P])
    K.iota = m.sb("iota", [P, P])
    K.iota_h = m.sb("iota_h", [P, P], BF16)
    K.head = m.sb("head", [P, P])
    K.part = m.sb("part", [P, 1])
    iota_i = m.sb("iota_i", [P, P], I32)
    part_i = m.sb("part_i", [P, 1], I32)
    q_s, j_s, v_s = m.sem("c_set"), m.sem("c_sel"), m.sem("c_copied")
    with nc.Block() as block:
        @block.gpsimd
        def _(pool):
            pool.memset(K.ident[:], 0.0).then_inc(q_s, 1)
            pool.memset(K.ones[:], 1.0).then_inc(q_s, 1)
            pool.memset(K.before[:], 0.0).then_inc(q_s, 1)
            pool.iota(iota_i[:], [[1, P]], base=0, channel_multiplier=0).then_inc(q_s, 1)
            pool.iota(part_i[:], [[1, 1]], base=0, channel_multiplier=1).then_inc(q_s, 1)
            pool.wait_ge(q_s, 5)
            pool.affine_select(out=K.ident[:], in_=K.ident[:], compare_op=ALU.not_equal, fill=1.0, base=0,
                               pattern=[[-1, P]], channel_multiplier=1).then_inc(j_s, 1)
            pool.affine_select(out=K.before[:], in_=K.before[:], compare_op=ALU.is_ge, fill=1.0, base=0,
                               pattern=[[-1, P]], channel_multiplier=1).then_inc(j_s, 1)
            hv = K.head[:].rearrange("p (g j) -> p g j", j=HD)
            pool.affine_select(out=hv, in_=K.ones[:].rearrange("p (g j) -> p g j", j=HD), compare_op=ALU.is_ge,
                               fill=0.0, base=0, pattern=[[-HD, P // HD], [0, HD]],
                               channel_multiplier=1).then_inc(j_s, 1)
            pool.wait_ge(j_s, 3)
            pool.affine_select(out=hv, in_=hv, compare_op=ALU.is_ge, fill=0.0, base=HD - 1,
                               pattern=[[HD, P // HD], [0, HD]], channel_multiplier=-1).then_inc(j_s, 1)

        @block.vector
        def _(dve):
            dve.wait_ge(q_s, 5)
            dve.tensor_copy(K.iota[:], iota_i[:]).then_inc(v_s, 1)
            dve.tensor_copy(K.iota_h[:], iota_i[:]).then_inc(v_s, 1)
            dve.tensor_copy(K.part[:], part_i[:]).then_inc(v_s, 1)
            dve.wait_ge(v_s, 3)


def where(eng, flag):
    return nullcontext() if flag is None else eng.If(eng.value_load(flag[:], min_val=0, max_val=1))


def places(nc, K, tag, n_part, cols, tile_h, cnt_all, base, place, unsorted=None):


    with ExitStack() as ctx:
        m = Mem(nc, ctx)
        passed = m.sem(tag + "_passed")
        cnt = m.sb(tag + "_cnt", [P, NT])
        eq = m.sb(tag + "_eq", [P, 3, cols], U16)
        run = K.acc[:].rearrange("p t f -> p (t f)")[:, 0:2 * cols].rearrange("p (r c) -> p r c", r=2)
        place_f = m.sb(tag + "_place_f", [P, cols])
        incl = m.sb(tag + "_incl", [P, NT])
        off = m.sb(tag + "_off", [P, NT])
        ptot = m.ps(tag + "_ptot", [P, NT])
        ppre = m.ps(tag + "_ppre", [P, NT])
        counted, summed, chain, placed, marked, ranked, kept = (m.sem(tag + x) for x in (
            "_counted", "_summed", "_chain", "_placed", "_marked", "_ranked", "_kept"))
        q = slice(0, n_part)
        with nc.Block() as block:
            @block.vector
            def _(dve):
                with where(dve, unsorted):
                    dve.sem_inc(counted, 1)
                    with dve.Fori(0, NT) as t:
                        dve.wait_ge(counted, t + 1)
                        dve.tensor_scalar(eq[q, 0], tile_h[q], K.iota[q, bass.ds(t, 1)], None, ALU.is_equal, ALU.add,
                                          accum_out=cnt[q, bass.ds(t, 1)]).then_inc(counted, 1)
                    dve.wait_ge(summed, 2)
                    dve.tensor_copy(cnt_all[:], ptot[:]).then_inc(chain, 1)
                    dve.wait_ge(chain, 1)
                    dve.tensor_tensor_scan(incl[:], cnt_all[:], cnt_all[:], 0.0, ALU.add, ALU.bypass).then_inc(chain, 1)
                    dve.wait_ge(chain, 2)
                    dve.tensor_tensor(base[:], incl[:], cnt_all[:], ALU.subtract).then_inc(chain, 1)
                    dve.wait_ge(chain, 3)
                    dve.scalar_tensor_tensor(off[q], ppre[q], -1.0, base[q], ALU.add, ALU.add).then_inc(chain, 1)
                    dve.wait_ge(chain, 4)
                    dve.wait_ge(placed, 1)

                    def mark(t, e):
                        dve.tensor_scalar(eq[q, e], tile_h[q], K.iota[q, bass.ds(t, 1)], None,
                                          ALU.is_equal).then_inc(marked, 1)

                    def sum_up(t, e, r):
                        dve.wait_ge(marked, t + 1)
                        dve.tensor_tensor_scan(run[q, r], eq[q, e], eq[q, e], off[q, bass.ds(t, 1)], ALU.add,
                                               ALU.bypass).then_inc(ranked, 1)

                    def keep(t, e, r):
                        dve.wait_ge(ranked, t + 1)
                        dve.wait_ge(kept, t + 1)
                        dve.sem_inc(passed, 1)
                        dve.copy_predicated(place_f[q], eq[q, e], run[q, r]).then_inc(kept, 1)

                    dve.sem_inc(kept, 1)
                    mark(0, 0)
                    mark(1, 1)
                    sum_up(0, 0, 0)
                    with dve.Fori(0, (NT - 4) // 6) as i:
                        for j in range(6):
                            t = i * 6 + j
                            dve.wait_ge(kept, t + 1)
                            mark(t + 2, (j + 2) % 3)
                            sum_up(t + 1, (j + 1) % 3, (j + 1) % 2)
                            keep(t, j % 3, j % 2)
                    for t in range((NT - 4) // 6 * 6, NT):
                        dve.wait_ge(kept, t + 1)
                        if t + 2 < NT:
                            mark(t + 2, (t + 2) % 3)
                        if t + 1 < NT:
                            sum_up(t + 1, (t + 1) % 3, (t + 1) % 2)
                        keep(t, t % 3, t % 2)
                    dve.wait_ge(kept, NT + 1)
                    dve.tensor_copy(place[q], place_f[q]).then_inc(placed, 1)

            @block.gpsimd
            def _(pool):
                with where(pool, unsorted):
                    pool.memset(place_f[:], 0.0).then_inc(placed, 1)

            @block.tensor
            def _(pe):
                with where(pe, unsorted):
                    pe.wait_ge(counted, NT + 1)
                    pe.matmul(ptot[:], K.ones[q, :], cnt[q], start=True, stop=True).then_inc(summed, 1)
                    pe.matmul(ppre[q], K.before[q, q], cnt[q], start=True, stop=True).then_inc(summed, 1)


class Scatter:

    def __init__(self, m, tag, pairs, n_part, place, pay):
        self.pairs, self.q, self.place, self.pay = pairs, slice(0, n_part), place, pay
        self.at = m.sb(tag + "_at", [P, HALVES, BATCH], U32)
        self.row = m.sb(tag + "_row", [P, HALVES, BATCH, 2], I32)
        self.staged, self.passed = m.sem(tag + "_staged"), m.sem(tag + "_passed")
        self.sent = [m.gather_sem(f"{tag}_sent{h}") for h in range(HALVES)]

    def run(self, pool, first, rounds):
        q = self.q

        def one(i, h):
            c = (i + first) * (BATCH * HALVES) + h * BATCH
            pool.tensor_copy(self.at[q, h], self.place[q, bass.ds(c, BATCH)]).then_inc(self.staged, 1)
            pool.tensor_copy(self.row[q, h], self.pay[q, bass.ds(c, BATCH), :]).then_inc(self.staged, 1)
            pool.wait_ge(self.staged, i * 4 + 2 * h + 2)
            pool.sem_inc(self.passed, 1)
            for b in range(BATCH):
                pool.indirect_dma_start(
                    out=self.pairs, out_offset=bass.IndirectOffsetOnAxis(ap=self.at[q, h, b:b + 1], axis=0),
                    in_=self.row[q, h, b, :], in_offset=None).then_inc(self.sent[h], 16)

        one(0, 0)
        one(0, 1)
        with pool.Fori(1, rounds) as i:
            for h in range(HALVES):
                pool.wait_ge(self.sent[h], i * (16 * BATCH))
                one(i, h)
        for h in range(HALVES):
            pool.wait_ge(self.sent[h], 16 * BATCH * rounds)


def scatter_unsorted(nc, K):
    with ExitStack() as ctx:
        scatter = Scatter(Mem(nc, ctx), "gc", K.gcn_pairs, GCN_P, K.gcn_place, K.gcn_pay)
        with nc.Block() as block:
            @block.gpsimd
            def _(pool):
                with where(pool, K.unsorted):
                    scatter.run(pool, 0, GCN_C // ROUND)


def step_tables(nc, K, tag, pairs, edges, cnt, base, unit, groups, src_T, dst_T, ch_start, ch_end, tile_row=None, tile_dram=None):
    with ExitStack() as ctx:
        m = Mem(nc, ctx)
        nch = m.sb(tag + "_nch", [P, NT])
        nch_i = m.sb(tag + "_nch_i", [P, NT], I32)
        shift = m.sb(tag + "_shift", [P, NT])
        ended = m.sb(tag + "_ended", [P, groups, NT])
        mine = m.sb(tag + "_mine", [P, groups, NT])
        step = m.sb(tag + "_step", [P, groups])
        tile = m.sb(tag + "_tile", [P, groups])
        tile_i = m.sb(tag + "_tile_i", [P, groups], I32)
        first = m.sb(tag + "_first", [P, groups])
        first_i = m.sb(tag + "_first_i", [P, groups], U32)
        node0 = m.sb(tag + "_node0", [P, groups])
        rows = m.sb(tag + "_rows", [P, 2, P, 2], I32)
        cols = m.sb(tag + "_cols", [P, 2, 2, P])
        ptr = m.ps(tag + "_ptr", [P, 2, 2, P])
        c, fetched, split, turned, used, out_s = (m.sem(tag + x) for x in (
            "_st", "_fetched", "_split", "_turned", "_used", "_outs"))
        fetch = [m.gather_sem(f"{tag}_fetch{h}") for h in range(2)]
        with nc.Block() as block:
            @block.vector
            def _(dve):
                n = [0]

                def done(ins):
                    n[0] += 1
                    ins.then_inc(c, 1)
                    dve.wait_ge(c, n[0])

                wide = P * unit
                done(dve.tensor_scalar(nch_i[:], cnt[:], 1.0 / wide, (wide - 1) / (2.0 * wide), ALU.mult, ALU.add))
                done(dve.tensor_scalar(nch[:], nch_i[:], 1.0, float(unit), ALU.max, ALU.mult))
                done(dve.tensor_tensor_scan(ch_end[:], nch[:], nch[:], 0.0, ALU.add, ALU.bypass))
                done(dve.tensor_tensor(ch_start[:], ch_end[:], nch[:], ALU.subtract))
                done(dve.scalar_tensor_tensor(shift[:], ch_start[:], -float(P), base[:], ALU.mult, ALU.add))
                for g in range(groups):
                    dve.tensor_scalar(step[:, g:g + 1], K.part[:], float(P * g), None, ALU.add).then_inc(c, 1)
                n[0] += groups
                dve.wait_ge(c, n[0])
                both = [P, groups, NT]
                st = step[:].unsqueeze(2).to_broadcast(both)
                done(dve.tensor_tensor(ended[:], ch_end[:].unsqueeze(1).to_broadcast(both), st, ALU.is_le))
                done(dve.tensor_tensor(mine[:], ch_start[:].unsqueeze(1).to_broadcast(both), st, ALU.is_le))
                done(dve.tensor_tensor(mine[:], mine[:], ended[:], ALU.subtract))
                done(dve.tensor_tensor(mine[:], mine[:], shift[:].unsqueeze(1).to_broadcast(both), ALU.mult))
                done(dve.tensor_reduce(first[:], mine[:], AX.X, ALU.add))
                done(dve.scalar_tensor_tensor(first[:], step[:], float(P), first[:], ALU.mult, ALU.add))
                done(dve.tensor_scalar(first_i[:], first[:], float(edges), None, ALU.min))
                done(dve.tensor_reduce(tile[:], ended[:], AX.X, ALU.add))
                done(dve.tensor_scalar(tile[:], tile[:], float(NT - 1), None, ALU.min))
                done(dve.tensor_copy(tile_i[:], tile[:]))
                done(dve.tensor_scalar(node0[:], tile[:], float(TN), None, ALU.mult))
                dve.sem_inc(fetched, 1)
                for g in range(groups):
                    s = g % 2
                    dve.wait_ge(fetch[s], 16 * (g // 2 + 1))
                    if g >= 2:
                        dve.wait_ge(turned, 2 * (g - 1))
                    dve.tensor_copy(cols[:, s, 0], rows[:, s, :, 0]).then_inc(split, 1)
                    dve.tensor_scalar(cols[:, s, 1], rows[:, s, :, 1], node0[:, g:g + 1], None,
                                      ALU.subtract).then_inc(split, 1)
                    dve.wait_ge(turned, 2 * (g + 1))
                    dve.tensor_copy(src_T[:, g * P:(g + 1) * P], ptr[:, s, 0]).then_inc(used, 1)
                    dve.tensor_copy(dst_T[:, g * P:(g + 1) * P], ptr[:, s, 1]).then_inc(used, 1)

            @block.gpsimd
            def _(pool):
                pool.wait_ge(fetched, 1)
                for g in range(groups):
                    s = g % 2
                    if g >= 2:
                        pool.wait_ge(split, 2 * (g - 1))
                    pool.indirect_dma_start(out=rows[:, s].rearrange("p a b -> p (a b)"), out_offset=None, in_=pairs,
                                            in_offset=bass.IndirectOffsetOnAxis(ap=first_i[:, g:g + 1], axis=0)
                                            ).then_inc(fetch[s], 16)

            @block.tensor
            def _(pe):
                for g in range(groups):
                    s = g % 2
                    pe.wait_ge(split, 2 * (g + 1))
                    if g >= 2:
                        pe.wait_ge(used, 2 * (g - 1))
                    for a in range(2):
                        pe.transpose(ptr[:, s, a], cols[:, s, a], K.ident[:]).then_inc(turned, 1)

            if tile_row is None:
                return

            @block.sync
            def _(sp):
                sp.wait_ge(fetched, 1)
                with nc.allow_non_contiguous_dma(reason="a small table"):
                    sp.dma_start(tile_dram.rearrange("(g p) -> p g", p=P), tile_i[:]).then_inc(out_s, 16)
                sp.wait_ge(out_s, 16)
                sp.dma_start(tile_row[:], tile_dram.rearrange("(a s) -> a s", a=1)).then_inc(out_s, 16)
                sp.wait_ge(out_s, 32)


def load_edges(nc, m, K, A):
    K.unsorted = m.sb("unsorted", [1, 1], I32)
    K.gat_tile = m.sb("gat_tile", [P, GAT_C], BF16)
    K.gcn_pay = m.sb("gcn_pay", [P, GCN_C, 2], I32)
    K.gcn_tile = m.sb("gcn_tile", [P, GCN_C], BF16)
    K.gcn_node = m.sb("gcn_node", [P, GCN_C], BF16)
    with ExitStack() as ctx:
        m = Mem(nc, ctx)
        scratch = K.acc[:].rearrange("p t f -> p (t f)").bitcast(I32)
        raw = scratch[:, 0:2 * GCN_C].rearrange("p (a c) -> p a c", a=2)
        ti = scratch[:, 2 * GCN_C:3 * GCN_C]
        raw2 = m.sb("raw2", [P, 2, GAT_C], I32)
        tail = m.sb("tail", [P, 2], I32)
        after = m.sb("after", [P, 1], I32)
        falls = m.sb("falls", [P, GCN_C], BF16)
        fall = m.sb("fall", [P, 2])
        pfall = m.ps("pfall", [P, 1])
        fell = m.sem("le_fell")
        copied = m.sem("le_copied")
        loaded, chain, out_s, pad = m.sem("le_loaded"), m.sem("le_chain"), m.sem("le_out"), m.sem("le_pad")
        c = GCN_P
        with nc.Block() as block:
            @block.sync
            def _(sp):
                sp.dma_start(raw[0:c, 0], A.src.rearrange("(p c) -> p c", p=c)).then_inc(loaded, 16)
                sp.dma_start(raw[0:c, 1], A.dst.rearrange("(p c) -> p c", p=c)).then_inc(loaded, 16)
                sp.dma_start(raw2[:, 0], A.edge_index[0].rearrange("(p c) -> p c", p=P)).then_inc(loaded, 16)
                sp.dma_start(raw2[:, 1], A.edge_index[1].rearrange("(p c) -> p c", p=P)).then_inc(loaded, 16)
                with nc.allow_non_contiguous_dma(reason="one value per partition"):
                    sp.dma_start(after[0:c - 1], A.dst.rearrange("(p c) -> p c", p=c)[1:c, 0:1]).then_inc(loaded, 16)
                sp.wait_ge(copied, 2)
                sp.dma_start(K.gcn_pairs[0:E_GCN].rearrange("(p c) a -> p c a", p=c), K.gcn_pay[0:c]).then_inc(out_s, 16)
                sp.wait_ge(pad, 1)
                sp.dma_start(K.gcn_pairs[E_GCN:E_GCN + P], tail[:]).then_inc(out_s, 16)
                sp.dma_start(K.gat_pairs[E_GAT:E_GAT + P], tail[:]).then_inc(out_s, 16)
                sp.wait_ge(out_s, 48)

            @block.gpsimd
            def _(pool):
                pool.memset(tail[:, 0:1], 0).then_inc(chain, 1)
                pool.memset(tail[:, 1:2], -1).then_inc(chain, 1)
                pool.wait_ge(chain, 2)
                pool.sem_inc(pad, 1)
                pool.wait_ge(loaded, 80)
                for a in range(2):
                    pool.tensor_copy(K.gat_pay[:, :, a], raw2[:, a]).then_inc(chain, 1)

            @block.scalar
            def _(act):
                act.wait_ge(loaded, 80)
                for a in range(2):
                    act.copy(K.gcn_pay[0:c, :, a], raw[0:c, a]).then_inc(copied, 1)

            @block.vector
            def _(dve):
                n = [0]
                dv = m.sem("le_dve")

                def done(ins):
                    n[0] += 1
                    ins.then_inc(dv, 1)
                    dve.wait_ge(dv, n[0])

                dve.wait_ge(loaded, 80)
                scale, bias = 1.0 / TN, 0.5 / TN - 0.5
                done(dve.tensor_scalar(ti[0:c], raw[0:c, 1], scale, bias, ALU.mult, ALU.add))
                done(dve.tensor_copy(K.gcn_tile[0:c], ti[0:c]))
                done(dve.scalar_tensor_tensor(K.gcn_node[0:c], ti[0:c], -float(TN), raw[0:c, 1], ALU.mult, ALU.add))
                done(dve.tensor_scalar(ti[:, 0:GAT_C], raw2[:, 1], scale, bias, ALU.mult, ALU.add))
                done(dve.tensor_copy(K.gat_tile[:], ti[:, 0:GAT_C]))
                done(dve.memset(fall[:], 0.0))
                done(dve.tensor_tensor(falls[0:c, 1:GCN_C], raw[0:c, 1, 1:GCN_C], raw[0:c, 1, 0:GCN_C - 1], ALU.is_lt))
                done(dve.tensor_reduce(fall[0:c, 0:1], falls[0:c, 1:GCN_C], AX.X, ALU.max))
                done(dve.tensor_tensor(fall[0:c - 1, 1:2], after[0:c - 1], raw[0:c - 1, 1, GCN_C - 1:GCN_C], ALU.is_lt))
                done(dve.tensor_tensor(fall[:, 0:1], fall[:, 0:1], fall[:, 1:2], ALU.add))
                dve.sem_inc(fell, 1)
                dve.wait_ge(fell, 2)
                done(dve.tensor_scalar(K.unsorted[:], pfall[0:1], 1.0, None, ALU.min))

            @block.tensor
            def _(pe):
                pe.wait_ge(fell, 1)
                pe.matmul(pfall[:], K.ones[:], fall[:, 0:1], start=True, stop=True).then_inc(fell, 1)


def degrees(nc, K, A, scatter_rounds):
    HB = 16
    rounds = GCN_C // HB
    with ExitStack() as ctx:
        m = Mem(nc, ctx)
        on = m.sb("on", [P, 2, TN, HB], BF16)
        ot = m.sb("ot", [P, 2, NT, HB], BF16)
        number = m.sb("number", [P, TN, HB], BF16)
        pdeg = m.ps("pdeg", [P, NT])
        xin = K.acc[:, 0:2 * SUB, :].rearrange("p (s j) f -> p s j f", s=2)
        st6 = m.sb("dx_st", [P, SUB, 6])
        mv = m.sb("dx_mv", [P, SUB, 2])
        var = m.sb("dx_var", [P, NT, 2])
        numbered, node_s, tile_s, used, done_s, chain, root, x_free, kept = (m.sem("dg_" + x) for x in (
            "numbered", "node", "tile", "used", "done", "chain", "root", "x_free", "kept"))
        xl = [m.sem(f"dg_xl{s}") for s in range(2)]
        c = GCN_P
        scatter = Scatter(m, "dg", K.gat_pairs, GAT_P, K.gat_place, K.gat_pay)
        with nc.Block() as block:
            @block.gpsimd
            def _(pool):
                scatter.run(pool, *scatter_rounds)

            def onehot(eng, out, ids, width, i, s, sem):
                k = i * 2 + s
                eng.wait_ge(used, i * 2 + s)
                eng.tensor_tensor(out[0:c, s], number[0:c, 0:width],
                                  ids[0:c, bass.ds(k * HB, HB)].unsqueeze(1).to_broadcast([c, width, HB]),
                                  ALU.is_equal).then_inc(sem, 1)

            @block.sync
            def _(sp):
                def body(k, i, s):
                    sp.wait_ge(x_free, k + 1)
                    for p0, p1 in ((0, 120), (120, TN)):
                        sp.dma_start(xin[p0:p1, s],
                                     A.x[bass.ds(k * BN, BN)].rearrange("(j p) f -> p j f", p=TN)[p0:p1]
                                     ).then_inc(xl[s], 16)
                blocks(sp, body)

            @block.tensor
            def _(pe):
                def body(i, s, first, last):
                    pe.wait_ge(node_s, i * 2 + s + 1)
                    pe.wait_ge(tile_s, i * 2 + s + 1)
                    for b in range(HB):
                        mm = pe.matmul(pdeg[0:TN], on[0:c, s, :, b], ot[0:c, s, :, b],
                                       start=first and b == 0, stop=last and b == HB - 1)
                    mm.then_inc(used, 1)
                pe.sem_inc(used, 1)
                body(0, 0, True, False)
                body(0, 1, False, False)
                with pe.Fori(1, rounds // 2 - 1) as i:
                    body(i, 0, False, False)
                    body(i, 1, False, False)
                body(rounds // 2 - 1, 0, False, False)
                body(rounds // 2 - 1, 1, False, True)

            @block.vector
            def _(dve):
                def stats(k, i, s):
                    dve.wait_ge(xl[s], i * 32 + 32)
                    for j in range(SUB):
                        dve.bn_stats(st6[0:TN, j], xin[0:TN, s, j]).then_inc(chain, 1)
                    dve.wait_ge(chain, k * (2 * SUB) + SUB)
                    dve.sem_inc(x_free, 1)
                    for j in range(SUB):
                        dve.bn_aggr(mv[0:TN, j], st6[0:TN, j]).then_inc(chain, 1)
                    dve.wait_ge(chain, k * (2 * SUB) + 2 * SUB)
                    dve.tensor_copy(K.xmv[0:TN, bass.ds(k * SUB, SUB), :], mv[0:TN]).then_inc(kept, 1)
                dve.tensor_copy(number[:], K.iota_h[:, 0:TN].unsqueeze(2).to_broadcast([P, TN, HB])).then_inc(numbered, 1)
                dve.sem_inc(x_free, 2)
                blocks(dve, stats)
                dve.wait_ge(numbered, 1)
                with dve.Fori(0, rounds // 2) as i:
                    for s in range(2):
                        onehot(dve, on, K.gcn_node, TN, i, s, node_s)
                        onehot(dve, ot, K.gcn_tile, NT, i, s, tile_s)
                dve.wait_ge(kept, NB)
                dve.wait_ge(used, rounds + 1)
                dve.tensor_scalar(var[0:TN, :, 0], K.xmv[0:TN, :, 1], EPS, None, ALU.add).then_inc(done_s, 1)
                dve.tensor_scalar(var[0:TN, :, 1], pdeg[0:TN], 1.0, None, ALU.add).then_inc(done_s, 1)
                dve.tensor_copy(K.degree[0:TN], pdeg[0:TN]).then_inc(kept, 1)
                dve.wait_ge(root, 1)
                dve.reciprocal(var[0:TN], var[0:TN]).then_inc(done_s, 1)
                dve.wait_ge(done_s, 3)
                dve.tensor_copy(K.xrs[0:TN], var[0:TN, :, 0]).then_inc(done_s, 1)
                dve.tensor_copy(K.dinv[0:TN], var[0:TN, :, 1]).then_inc(done_s, 1)

            @block.scalar
            def _(act):
                act.wait_ge(done_s, 2)
                act.activation(var[0:TN], var[0:TN], ACT.Sqrt).then_inc(root, 1)


def counts_of_tiles(nc, K):
    with ExitStack() as ctx:
        m = Mem(nc, ctx)
        upto = m.sb("ct_upto", [P, NT])
        total = m.ps("ct_total", [P, NT])
        summed, chain = m.sem("ct_summed"), m.sem("ct_chain")
        with nc.Block() as block:
            @block.tensor
            def _(pe):
                pe.matmul(total[:], K.ones[0:TN], K.degree[0:TN], start=True, stop=True).then_inc(summed, 1)

            @block.vector
            def _(dve):
                dve.wait_ge(summed, 1)
                dve.tensor_copy(K.cnt[:], total[:]).then_inc(chain, 1)
                dve.wait_ge(chain, 1)
                dve.tensor_tensor_scan(upto[:], K.cnt[:], K.cnt[:], 0.0, ALU.add, ALU.bypass).then_inc(chain, 1)
                dve.wait_ge(chain, 2)
                dve.tensor_tensor(K.base[:], upto[:], K.cnt[:], ALU.subtract).then_inc(chain, 1)


def dense_first(nc, K, A, scatter_rounds):
    with ExitStack() as ctx:
        m = Mem(nc, ctx)
        w1T = m.sb("w1T", [P, KC, D])
        wq = m.sb("wq", [P, KC, D])
        wkv = m.sb("wkv", [P, KC, 2, D])
        b1c = m.sb("b1c", [P, KC])
        bqc = m.sb("bqc", [P, KC])
        bkv = m.sb("bkv", [P, 2, D])
        xin = m.sb("a_xin", [P, 2, SUB, D])
        xn = m.sb("a_xn", [P, 2, SUB, D])
        scratch = K.acc[:].rearrange("p t f -> p (t f)")
        size = 2 * KC * BN
        xnT = scratch[:, 0:size].rearrange("p (s c n) -> p s c n", s=2, c=KC)
        hT = scratch[:, size:2 * size].rearrange("p (s c n) -> p s c n", s=2, c=KC)
        qT = scratch[:, 2 * size:3 * size].rearrange("p (s c n) -> p s c n", s=2, c=KC)
        qm = m.sb("a_qm", [P, KC, BN])
        kb = m.sb("a_kb", [P, 2, D])
        km = m.sb("a_km", [P, 2, D])
        ve = m.sb("a_ve", [P, 2, KC, P + 1])
        stats = m.sb("a_stats", [P, KC, NB, 6])
        hst = m.sb("a_hst", [P, KC, 6])
        ptr = m.ps("a_ptr", [P, KC, 512])
        pqh = m.ps("a_pqh", [P, KC, 512])
        pkv = m.ps("a_pkv", [P, 2, 512])
        pacc = m.ps("a_pacc", [P, KC, 512])
        S = {n: m.sem("a_" + n) for n in (
            "w", "ones", "x_free", "xn", "turned", "xnT", "q", "q_min", "q_sb", "q_exp", "q_sum", "h", "h_sb",
            "h_stat", "kv", "kb", "v", "k_min", "k_exp", "k_sum", "acc", "agg", "mean")}
        x_in = [m.sem(f"a_x_in{s}") for s in range(2)]
        stored = [m.sem(f"a_stored{s}") for s in range(2)]
        scatter = Scatter(m, "df", K.gat_pairs, GAT_P, K.gat_place, K.gat_pay)
        with nc.Block() as block:
            @block.gpsimd
            def _(pool):
                scatter.run(pool, *scatter_rounds)

            @block.sync
            def _(sp):
                sp.dma_start(w1T[:], A.w1T.rearrange("(c p) o -> p c o", p=P)).then_inc(S["w"], 16)
                sp.dma_start(wq[:], A.wq.rearrange("(c p) o -> p c o", p=P)).then_inc(S["w"], 16)
                sp.dma_start(wkv[:, :, 0], A.wk.rearrange("(c p) o -> p c o", p=P)).then_inc(S["w"], 16)
                sp.dma_start(wkv[:, :, 1], A.wv.rearrange("(c p) o -> p c o", p=P)).then_inc(S["w"], 16)
                with nc.allow_non_contiguous_dma(reason="biases"):
                    sp.dma_start(b1c[:], A.b1.rearrange("(c p) -> p c", p=P)).then_inc(S["w"], 16)
                    sp.dma_start(bqc[:], A.bq.rearrange("(c p) -> p c", p=P)).then_inc(S["w"], 16)
                sp.dma_start(bkv[:, 0], A.bk.rearrange("(a o) -> a o", a=1).to_broadcast([P, D])).then_inc(S["w"], 16)
                sp.dma_start(bkv[:, 1], A.bv.rearrange("(a o) -> a o", a=1).to_broadcast([P, D])).then_inc(S["w"], 16)

                def load(k, i, s):
                    sp.wait_ge(S["x_free"], k + 1)
                    for p0, p1 in ((0, 120), (120, TN)):
                        sp.dma_start(xin[p0:p1, s], A.x[bass.ds(k * BN, BN)].rearrange("(j p) f -> p j f", p=TN)[p0:p1]
                                     ).then_inc(x_in[s], 16)

                def store(k, i, s):
                    sp.wait_ge(S["h_sb"], k * 2 + 2)
                    sp.dma_start(K.hT_d[bass.ds(k, 1)].rearrange("a p c n -> p (a c) n"), hT[:, s]
                                 ).then_inc(stored[s], 16)
                    sp.wait_ge(S["q_sum"], k * 2 + 2)
                    sp.dma_start(K.qT_d[bass.ds(k, 1)].rearrange("a p c n -> p (a c) n"), qT[:, s]
                                 ).then_inc(stored[s], 16)

                load(0, 0, 0)
                load(1, 0, 1)
                with sp.Fori(0, (NB - 3) // 2) as i:
                    for s in range(2):
                        load(i * 2 + 2 + s, i + 1, s)
                        store(i * 2 + s, i, s)
                load(NB - 1, 0, 0)
                store(NB - 3, 0, 0)
                store(NB - 2, 0, 1)
                store(NB - 1, 0, 0)
                sp.wait_ge(stored[0], 32 * (NB // 2 + 1))
                sp.wait_ge(stored[1], 32 * (NB // 2))

            @block.tensor
            def _(pe):
                def project(w, s, sem):
                    for o in range(KC):
                        for c in range(KC):
                            mm = pe.matmul(pqh[:, o, 0:BN], w[:, c, o * P:(o + 1) * P], xnT[:, s, c],
                                           start=c == 0, stop=c == KC - 1)
                        mm.then_inc(sem, 1)

                def kv(k, s, j):
                    pe.wait_ge(S["v"], k * SUB + j)
                    for c in range(KC):
                        mm = pe.matmul(pkv[0:TN, j % 2], xnT[:, s, c, j * TN:(j + 1) * TN],
                                       wkv[:, c].rearrange("p a o -> p (a o)"), start=c == 0, stop=c == KC - 1)
                    mm.then_inc(S["kv"], 1)

                def accumulate(k, j, first, last):
                    pe.wait_ge(S["k_sum"], k * SUB + j + 1)
                    for c in range(KC):
                        mm = pe.matmul(pacc[:, c, 0:P + 1], km[0:TN, j % 2, c * P:(c + 1) * P], ve[0:TN, j % 2, c],
                                       start=first and j == 0, stop=last and j == SUB - 1)
                    mm.then_inc(S["acc"], 1)

                def body(k, s, first=False, last=False):
                    pe.wait_ge(S["xnT"], k * KC + KC)
                    pe.wait_ge(S["h_sb"], k * KC)
                    project(wq, s, S["q"])
                    kv(k, s, 0)
                    kv(k, s, 1)
                    pe.wait_ge(S["q_sb"], k * KC + KC)
                    project(w1T, s, S["h"])
                    if not last:
                        transposes_next(k, s)
                    accumulate(k, 0, first, last)
                    kv(k, s, 2)
                    accumulate(k, 1, first, last)
                    kv(k, s, 3)
                    accumulate(k, 2, first, last)
                    accumulate(k, 3, first, last)

                def transposes_next(k, s):
                    pe.wait_ge(S["xn"], k * SUB + 2 * SUB)
                    pe.wait_ge(S["xnT"], k * KC + KC)
                    turn(1 - s)

                def turn(s):
                    for c in range(KC):
                        for j in range(SUB):
                            mm = pe.transpose(ptr[:, c, j * TN:(j + 1) * TN], xn[0:TN, s, j, c * P:(c + 1) * P],
                                              K.ident[0:TN, 0:TN])
                        mm.then_inc(S["turned"], 1)

                pe.wait_ge(S["w"], 16 * 8)
                pe.wait_ge(S["ones"], 1)
                pe.wait_ge(S["xn"], SUB)
                turn(0)
                body(0, 0, first=True)
                body(1, 1)
                with pe.Fori(1, NB // 2) as i:
                    body(i * 2, 0)
                    body(i * 2 + 1, 1)
                body(NB - 1, 0, last=True)

            @block.scalar
            def _(act):
                def turned(k, s):
                    act.wait_ge(S["turned"], k * KC + KC)
                    for c in range(KC):
                        act.copy(xnT[:, s, c], ptr[:, c, 0:BN]).then_inc(S["xnT"], 1)

                def body(k, i, s, last=False):
                    act.wait_ge(stored[s], i * 32)
                    for c in range(KC):
                        act.wait_ge(S["q"], k * KC + c + 1)
                        act.activation(qT[:, s, c], pqh[:, c, 0:BN], ACT.Identity, bias=bqc[:, c:c + 1]
                                       ).then_inc(S["q_sb"], 1)
                    for c in range(KC):
                        act.wait_ge(S["q_min"], k * KC + c + 1)
                        act.activation(qm[:, c], qm[:, c], ACT.Exp).then_inc(S["q_exp"], 1)
                    k_exp(k, 0)
                    k_exp(k, 1)
                    for c in range(KC):
                        act.wait_ge(S["h"], k * KC + c + 1)
                        act.activation(hT[:, s, c], pqh[:, c, 0:BN], ACT.Identity, bias=b1c[:, c:c + 1]
                                       ).then_inc(S["h_sb"], 1)
                    if not last:
                        turned(k + 1, 1 - s)
                    k_exp(k, 2)
                    k_exp(k, 3)

                def k_exp(k, j):
                    act.wait_ge(S["k_min"], k * SUB + j + 1)
                    act.activation(km[0:TN, j % 2], km[0:TN, j % 2], ACT.Exp).then_inc(S["k_exp"], 1)

                act.wait_ge(S["w"], 16 * 8)
                turned(0, 0)
                with act.Fori(0, NB // 2) as i:
                    body(i * 2, i, 0)
                    body(i * 2 + 1, i, 1)
                body(NB - 1, NB // 2, 0, last=True)

            @block.vector
            def _(dve):
                def normalise(k, i, s):
                    dve.wait_ge(x_in[s], i * 32 + 32)
                    dve.wait_ge(S["turned"], i * (2 * KC))
                    for j in range(SUB):
                        t = k * SUB + j
                        ins = dve.tensor_scalar(xn[0:TN, s, j], xin[0:TN, s, j], K.xmv[0:TN, bass.ds(t, 1), 0],
                                                K.xrs[0:TN, bass.ds(t, 1)], ALU.subtract, ALU.mult)
                        ins.then_inc(S["xn"], 1)
                    dve.wait_ge(S["xn"], k * SUB + SUB)
                    dve.sem_inc(S["x_free"], 1)

                def k_part(k, j):
                    s = j % 2
                    dve.wait_ge(S["kv"], k * SUB + j + 1)
                    if j >= 2:
                        dve.wait_ge(S["acc"], k * SUB + j - 1)
                    else:
                        dve.wait_ge(S["acc"], k * SUB)
                    dve.tensor_tensor(kb[0:TN, s], pkv[0:TN, s, 0:D], bkv[0:TN, 0], ALU.add).then_inc(S["kb"], 1)
                    dve.tensor_tensor(ve[0:TN, s, :, 0:P], pkv[0:TN, s, D:2 * D].rearrange("p (c e) -> p c e", c=KC),
                                      bkv[0:TN, 1].rearrange("p (c e) -> p c e", c=KC), ALU.add).then_inc(S["v"], 1)
                    dve.wait_ge(S["kb"], k * SUB + j + 1)
                    dve.tensor_scalar(km[0:TN, s], kb[0:TN, s], 0.0, None, ALU.min).then_inc(S["k_min"], 1)

                def k_sum(k, j):
                    s = j % 2
                    dve.wait_ge(S["k_exp"], k * SUB + j + 1)
                    dve.scalar_tensor_tensor(km[0:TN, s], kb[0:TN, s], 0.0, km[0:TN, s], ALU.max, ALU.add
                                             ).then_inc(S["k_sum"], 1)

                def body(k, i, s, last=False):
                    dve.wait_ge(S["q_sum"], k * KC)
                    for c in range(KC):
                        dve.wait_ge(S["q_sb"], k * KC + c + 1)
                        dve.tensor_scalar(qm[:, c], qT[:, s, c], 0.0, None, ALU.min).then_inc(S["q_min"], 1)
                    if not last:
                        normalise(k + 1, *((i, 1) if s == 0 else (i + 1, 0)))
                    k_part(k, 0)
                    k_part(k, 1)
                    for c in range(KC):
                        dve.wait_ge(S["q_exp"], k * KC + c + 1)
                        dve.scalar_tensor_tensor(qT[:, s, c], qT[:, s, c], 0.0, qm[:, c], ALU.max, ALU.add
                                                 ).then_inc(S["q_sum"], 1)
                    k_sum(k, 0)
                    k_sum(k, 1)
                    for c in range(KC):
                        dve.wait_ge(S["h_sb"], k * KC + c + 1)
                        dve.bn_stats(hst[:, c], hT[:, s, c]).then_inc(S["h_stat"], 1)
                    dve.wait_ge(S["h_stat"], k * KC + KC)
                    dve.tensor_copy(stats[:, :, bass.ds(k, 1), :].rearrange("p c a b -> p c (a b)"), hst[:]).then_inc(S["agg"], 1)
                    dve.wait_ge(S["agg"], k + 1)
                    k_part(k, 2)
                    k_sum(k, 2)
                    k_part(k, 3)
                    k_sum(k, 3)

                dve.memset(ve[:, :, :, P:P + 1], 1.0).then_inc(S["ones"], 1)
                dve.sem_inc(S["x_free"], 2)
                dve.sem_inc(S["v"], 1)
                dve.wait_ge(S["w"], 16 * 8)
                dve.wait_ge(S["ones"], 1)
                normalise(0, 0, 0)
                with dve.Fori(0, NB // 2) as i:
                    body(i * 2, i, 0)
                    body(i * 2 + 1, i, 1)
                body(NB - 1, NB // 2, 0, last=True)
                for c in range(KC):
                    dve.bn_aggr(K.hmv[:, c], stats[:, c].rearrange("p n s -> p (n s)")).then_inc(S["mean"], 1)
                dve.wait_ge(S["acc"], NT)
                dve.tensor_copy(K.kv[:], pacc[:, :, 0:P + 1]).then_inc(S["mean"], 1)
                dve.wait_ge(S["mean"], 3)


def dense_second(nc, K, A, scatter_rounds):
    with ExitStack() as ctx:
        m = Mem(nc, ctx)
        w2 = m.sb("w2", [P, KC, D])
        wgT = m.sb("wgT", [P, KC, D])
        wo = m.sb("wo", [P, KC, D])
        gb = m.sb("gb", [P, 2, KC])
        b2c = m.sb("b2c", [P, KC])
        rows_b = m.sb("rows_b", [P, 2, D])
        W = m.sb("w_both", [P, KC, D])
        bW = m.sb("b_both", [P, D])
        kvm = m.sb("kvm", [P, KC, P])
        kvT = m.sb("kvT", [P, KC, P])
        kvw = m.sb("kvw", [P, KC, D])
        Z = m.sb("zmat", [P, KC, P])
        bn = m.sb("bn", [P, KC, 4])
        scale, shift = m.sb("bn_scale", [P, KC]), m.sb("bn_shift", [P, KC])
        hT = m.sb("b_hT", [P, 2, KC, BN])
        qT = m.sb("b_qT", [P, 2, KC, BN])
        xin = m.sb("b_xin", [P, 2, SUB, D])
        pre = m.sb("b_pre", [P, 2, SUB, D])
        tmp = K.hrow[:].rearrange("p t f -> p (t f)")[:, 0:SUB * D].rearrange("p (j f) -> p j f", j=SUB)
        b2r = K.hrow[:].rearrange("p t f -> p (t f)")[:, SUB * D:SUB * D + KC * P].rearrange("p (c n) -> p c n", c=KC)
        rz = K.gat_dstT[:, 0:KC * BN].rearrange("p (c n) -> p c n", c=KC)
        pz = m.ps("b_pz", [P, KC, 512])
        px = m.ps("b_px", [P, SUB, D])
        pm = m.ps("b_pm", [P, SUB, D])
        pw = m.ps("b_pw", [P, 512])
        S = {n: m.sem("b_" + n) for n in (
            "w", "v", "root", "p", "z", "rz", "qs", "relu", "px", "tmp", "acc", "pm", "pre", "in_free")}
        l_in = [m.sem(f"b_in{s}") for s in range(2)]
        tab_s = [m.sem(f"b_tab{s}") for s in range(2)]
        pre_s = [m.sem(f"b_pre_s{s}") for s in range(2)]
        scatter = Scatter(m, "ds", K.gat_pairs, GAT_P, K.gat_place, K.gat_pay)
        with nc.Block() as block:
            @block.gpsimd
            def _(pool):
                scatter.run(pool, *scatter_rounds)

            @block.sync
            def _(sp):
                for t, a in ((w2, A.w2), (wgT, A.wgT), (wo, A.wo)):
                    sp.dma_start(t[:], a.rearrange("(c p) o -> p c o", p=P)).then_inc(S["w"], 16)
                with nc.allow_non_contiguous_dma(reason="biases"):
                    for t, a in ((gb[:, 0], A.gamma), (gb[:, 1], A.beta), (b2c[:], A.b2)):
                        sp.dma_start(t, a.rearrange("(c p) -> p c", p=P)).then_inc(S["w"], 16)
                for n, a in enumerate((A.bo, A.b_gcn)):
                    sp.dma_start(rows_b[:, n], a.rearrange("(a o) -> a o", a=1).to_broadcast([P, D])
                                 ).then_inc(S["w"], 16)

                def load(k, i, s):
                    sp.wait_ge(S["in_free"], k + 1)
                    sp.dma_start(hT[:, s], K.hT_d[bass.ds(k, 1)].rearrange("a p c n -> p (a c) n")).then_inc(l_in[s], 16)
                    sp.dma_start(qT[:, s], K.qT_d[bass.ds(k, 1)].rearrange("a p c n -> p (a c) n")).then_inc(l_in[s], 16)
                    for p0, p1 in ((0, 120), (120, TN)):
                        sp.dma_start(xin[p0:p1, s], A.x[bass.ds(k * BN, BN)].rearrange("(j p) f -> p j f", p=TN)[p0:p1]
                                     ).then_inc(l_in[s], 16)

                def store(k, i, s):
                    sp.wait_ge(S["acc"], k * SUB + SUB)
                    for p0, p1 in ((0, 120), (120, TN)):
                        sp.dma_start(K.table[bass.ds(k * BN, BN)].rearrange("(j p) f -> p j f", p=TN)[p0:p1],
                                     K.acc[p0:p1, bass.ds(k * SUB, SUB), :]).then_inc(tab_s[s], 16)
                    sp.wait_ge(S["pre"], k * (2 * SUB) + 2 * SUB)
                    for p0, p1 in ((0, 120), (120, TN)):
                        sp.dma_start(K.pre_d[bass.ds(k, 1)].rearrange("a p j f -> p (a j) f")[p0:p1],
                                     pre[p0:p1, s]).then_inc(pre_s[s], 16)

                load(0, 0, 0)
                load(1, 0, 1)
                with sp.Fori(0, (NB - 3) // 2) as i:
                    for s in range(2):
                        load(i * 2 + 2 + s, i + 1, s)
                        store(i * 2 + s, i, s)
                load(NB - 1, 0, 0)
                store(NB - 3, 0, 0)
                store(NB - 2, 0, 1)
                store(NB - 1, 0, 0)
                for s in range(2):
                    sp.wait_ge(tab_s[s], 32 * ((NB + 1 - s) // 2))
                    sp.wait_ge(pre_s[s], 32 * ((NB + 1 - s) // 2))

            @block.tensor
            def _(pe):
                pe.wait_ge(S["w"], 16 * 8)
                for b in range(KC):
                    for a in range(KC):
                        mm = pe.matmul(pw[:, b * D:(b + 1) * D], w2[:, a, b * P:(b + 1) * P], wgT[:, a],
                                       start=a == 0, stop=a == KC - 1, skip_group_check=True)
                mm.then_inc(S["p"], 1)
                pe.wait_ge(S["v"], 4)
                for c in range(KC):
                    mm = pe.transpose(pz[:, 0, c * P:(c + 1) * P], kvm[:, c], K.ident[:])
                mm.then_inc(S["p"], 1)
                for a in range(KC):
                    mm = pe.matmul(pz[:, 1, 0:D], b2r[:, a], wgT[:, a], start=a == 0, stop=a == KC - 1)
                mm.then_inc(S["p"], 1)
                pe.wait_ge(S["v"], 7)
                for c in range(KC):
                    mm = pe.matmul(pw[:, c * D:(c + 1) * D], kvT[:, c], wo[:, c], start=True, stop=True,
                                   skip_group_check=True)
                mm.then_inc(S["p"], 1)
                pe.wait_ge(S["v"], 8)

                def body(k, i, s):
                    pe.wait_ge(l_in[s], i * 64 + 64)
                    pe.wait_ge(S["rz"], k * KC)
                    for c in range(KC):
                        pe.matmul(pz[:, c, 0:BN], Z[:, c], qT[:, s, c], start=True, stop=True).then_inc(S["z"], 1)
                    pe.wait_ge(S["relu"], k * KC + KC)
                    pe.wait_ge(S["tmp"], k * SUB)
                    for j in range(SUB):
                        for c in range(KC):
                            mm = pe.matmul(px[0:TN, j], hT[:, s, c, j * TN:(j + 1) * TN], W[:, c],
                                           start=c == 0, stop=c == KC - 1, skip_group_check=True)
                        mm.then_inc(S["px"], 1)
                    pe.wait_ge(S["qs"], k * KC + KC)
                    pe.wait_ge(S["pre"], k * (2 * SUB))
                    for j in range(SUB):
                        for c in range(KC):
                            mm = pe.matmul(pm[0:TN, j], qT[:, s, c, j * TN:(j + 1) * TN], kvw[:, c],
                                           start=c == 0, stop=c == KC - 1, skip_group_check=True)
                        mm.then_inc(S["pm"], 1)
                blocks(pe, body)

            @block.scalar
            def _(act):
                act.wait_ge(S["v"], 5)
                act.activation(bn[:, :, 1], bn[:, :, 0], ACT.Sqrt).then_inc(S["root"], 1)
                act.wait_ge(S["v"], 8)

                def body(k, i, s):
                    act.wait_ge(l_in[s], i * 64 + 64)
                    for c in range(KC):
                        act.activation(hT[:, s, c], hT[:, s, c], ACT.Relu, bias=shift[:, c:c + 1],
                                       scale=scale[:, c:c + 1]).then_inc(S["relu"], 1)
                    for j in range(SUB):
                        t = k * SUB + j
                        act.wait_ge(S["tmp"], k * SUB + j + 1)
                        act.activation(K.acc[0:TN, bass.ds(t, 1), :].rearrange("p a f -> p (a f)"), tmp[0:TN, j],
                                       ACT.Copy, scale=K.dinv[0:TN, bass.ds(t, 1)]).then_inc(S["acc"], 1)
                blocks(act, body)

            @block.vector
            def _(dve):
                dve.wait_ge(S["w"], 16 * 8)
                for c in range(KC):
                    dve.tensor_tensor(kvm[:, c], K.kv[:, c, 0:P], K.head[:], ALU.mult).then_inc(S["v"], 1)
                for c in range(KC):
                    dve.tensor_scalar(b2r[:, c], K.ones[:], b2c[:, c:c + 1], None, ALU.mult).then_inc(S["v"], 1)
                dve.tensor_scalar(bn[:, :, 0], K.hmv[:, :, 1], EPS, None, ALU.add).then_inc(S["v"], 1)
                dve.wait_ge(S["p"], 3)
                dve.tensor_copy(W[:].rearrange("p c f -> p (c f)"), pw[:]).then_inc(S["v"], 1)
                dve.tensor_copy(kvT[:].rearrange("p c f -> p (c f)"), pz[:, 0, 0:KC * P]).then_inc(S["v"], 1)
                u = m.sem("b_u")
                for c in range(KC):
                    dve.tensor_scalar(Z[:, c], K.head[:], K.kv[:, c, P:P + 1], None, ALU.mult).then_inc(u, 1)
                dve.tensor_copy(bW[:], pz[:, 1, 0:D]).then_inc(u, 1)
                dve.tensor_tensor(rows_b[:, 0], rows_b[:, 0], rows_b[:, 1], ALU.add).then_inc(u, 1)
                dve.wait_ge(S["root"], 1)
                dve.reciprocal(bn[:, :, 2], bn[:, :, 1]).then_inc(u, 1)
                dve.wait_ge(u, 5)
                dve.tensor_tensor(scale[:], bn[:, :, 2], gb[:, 0], ALU.mult).then_inc(u, 1)
                dve.wait_ge(u, 6)
                dve.tensor_tensor(bn[:, :, 3], K.hmv[:, :, 0], scale[:], ALU.mult).then_inc(u, 1)
                dve.wait_ge(u, 7)
                dve.tensor_tensor(shift[:], gb[:, 1], bn[:, :, 3], ALU.subtract).then_inc(u, 1)
                dve.wait_ge(u, 8)
                dve.wait_ge(S["p"], 4)
                dve.tensor_copy(kvw[:].rearrange("p c f -> p (c f)"), pw[:]).then_inc(S["v"], 1)
                dve.sem_inc(S["in_free"], 2)
                dve.wait_ge(S["v"], 8)

                def body(k, i, s):
                    dve.wait_ge(l_in[s], i * 64 + 64)
                    dve.wait_ge(pre_s[s], i * 32)
                    for j in range(SUB):
                        dve.tensor_tensor(pre[0:TN, s, j], xin[0:TN, s, j], rows_b[0:TN, 0], ALU.add
                                          ).then_inc(S["pre"], 1)
                    for c in range(KC):
                        dve.wait_ge(S["z"], k * KC + c + 1)
                        dve.tensor_scalar(rz[:, c], pz[:, c, 0:BN], 1e-6, None, ALU.add).then_inc(S["rz"], 1)
                    dve.wait_ge(S["rz"], k * KC + KC)
                    for c in range(KC):
                        dve.reciprocal(rz[:, c], rz[:, c]).then_inc(r2, 1)
                    dve.wait_ge(r2, k * KC + KC)
                    for c in range(KC):
                        dve.tensor_tensor(qT[:, s, c], qT[:, s, c], rz[:, c], ALU.mult).then_inc(S["qs"], 1)
                    dve.wait_ge(S["acc"], k * SUB)
                    for j in range(SUB):
                        if j % 2 == 0:
                            dve.wait_ge(S["px"], k * SUB + j + 2)
                        dve.tensor_tensor(tmp[0:TN, j], px[0:TN, j], bW[0:TN], ALU.add).then_inc(S["tmp"], 1)
                    dve.wait_ge(S["pre"], k * (2 * SUB) + SUB)
                    for j in range(SUB):
                        if j % 2 == 0:
                            dve.wait_ge(S["pm"], k * SUB + j + 2)
                        dve.tensor_tensor(pre[0:TN, s, j], pre[0:TN, s, j], pm[0:TN, j], ALU.add
                                          ).then_inc(S["pre"], 1)
                    dve.wait_ge(S["pre"], k * (2 * SUB) + 2 * SUB)
                    dve.sem_inc(S["in_free"], 1)
                r2 = m.sem("b_r2")
                blocks(dve, body)


def gather_sum(nc, K):
    W, PAIRS = BATCH, BATCH // 2
    rounds = S_GCN // (W * HALVES)
    with ExitStack() as ctx:
        m = Mem(nc, ctx)
        at = m.sb("g_at", [P, HALVES, W], U32)
        rows = m.sb("g_rows", [P, HALVES, W, D])
        hot = m.sb("g_hot", [P, HALVES, W, TN])
        ps = m.ps("g_ps", [P, HALVES, PAIRS, 512])
        at_s, hot_s, mm_s, add_s, passed = (m.sem("g_" + x) for x in ("at", "hot", "mm", "add", "passed"))
        got = [m.gather_sem(f"g_got{h}") for h in range(HALVES)]
        with nc.Block() as block:
            @block.scalar
            def _(act):
                for h in range(HALVES):
                    act.copy(at[:, h], K.gcn_srcT[:, h * W:(h + 1) * W]).then_inc(at_s, 1)
                with act.Fori(1, rounds) as i:
                    for h in range(HALVES):
                        act.wait_ge(got[h], i * (16 * W))
                        act.copy(at[:, h], K.gcn_srcT[:, bass.ds((i * HALVES + h) * W, W)]).then_inc(at_s, 1)

            @block.gpsimd
            def _(pool):
                with pool.Fori(0, rounds) as i:
                    for h in range(HALVES):
                        pool.wait_ge(at_s, i * HALVES + h + 1)
                        pool.wait_ge(mm_s, (i * HALVES + h) * PAIRS + PAIRS)
                        pool.sem_inc(passed, 1)
                        for b in range(W):
                            pool.indirect_dma_start(
                                out=rows[:, h, b], out_offset=None, in_=K.table,
                                in_offset=bass.IndirectOffsetOnAxis(ap=at[:, h, b:b + 1], axis=0)
                            ).then_inc(got[h], 16)

            @block.tensor
            def _(pe):
                pe.sem_inc(mm_s, HALVES * PAIRS)
                with pe.Fori(0, rounds) as i:
                    for h in range(HALVES):
                        pe.wait_ge(hot_s, i * HALVES + h + 1)
                        pe.wait_ge(got[h], (i + 1) * (16 * W))
                        for j in range(PAIRS):
                            pe.wait_ge(add_s, (i * HALVES + h) * PAIRS + j + 1)
                            for b in (2 * j, 2 * j + 1):
                                mm = pe.matmul(ps[0:TN, h, j, 0:D], hot[:, h, b], rows[:, h, b], start=b == 2 * j,
                                               stop=b == 2 * j + 1)
                            mm.then_inc(mm_s, 1)

            @block.vector
            def _(dve):
                dve.sem_inc(add_s, HALVES * PAIRS)

                def build(n, h):
                    dve.wait_ge(mm_s, n * PAIRS + PAIRS)
                    shape = [P, W, TN]
                    dve.tensor_tensor(hot[:, h], K.iota[:, 0:TN].unsqueeze(1).to_broadcast(shape),
                                      K.gcn_dstT[:, bass.ds(n * W, W)].unsqueeze(2).to_broadcast(shape),
                                      ALU.is_equal).then_inc(hot_s, 1)

                def add(n, h):
                    for j in range(PAIRS):
                        t = dve.value_load(K.gcn_tiles[0:1, bass.ds(n * W + 2 * j, 1)], min_val=0, max_val=NT - 1)
                        a = K.acc[0:TN, bass.ds(t, 1), :].rearrange("p a f -> p (a f)")
                        dve.wait_ge(mm_s, n * PAIRS + HALVES * PAIRS + j + 1)
                        dve.wait_ge(add_s, n * PAIRS + HALVES * PAIRS + j)
                        dve.tensor_tensor(a, a, ps[0:TN, h, j, 0:D], ALU.add).then_inc(add_s, 1)

                build(0, 0)
                with dve.Fori(0, rounds - 1) as i:
                    for h in range(HALVES):
                        n = i * HALVES + h
                        build(n + 1, 1 - h)
                        add(n, h)
                n = (rounds - 1) * HALVES
                build(n + 1, 1)
                add(n, 0)
                add(n + 1, 1)


def second_norm(nc, K, A):
    with ExitStack() as ctx:
        m = Mem(nc, ctx)
        wg = m.sb("wg", [P, KC, GW])
        att = m.sb("att", [P, 2, GW])
        pre = m.sb("c_pre", [P, 2, SUB, D])
        x1 = m.sb("c_x1", [P, 2, SUB, D])
        xf = m.sb("c_xf", [P, 2, SUB, D])
        xfT = m.sb("c_xfT", [P, 2, KC, BN])
        st6 = m.sb("c_st6", [P, SUB, 6])
        mv = m.sb("c_mv", [P, 2, SUB, 2])
        rs = m.sb("c_rs", [P, 2, SUB, 2])
        hg = m.sb("c_hg", [P, NT, GW])
        prod = m.sb("c_prod", [P, NT, GW])
        trow = m.sb("c_trow", [P, NT, TROW])
        ptr = m.ps("c_ptr", [P, 2, KC, 512])
        ph = m.ps("c_ph", [P, 2, 512])
        S = {n: m.sem("c_" + n) for n in (
            "w", "x1", "st", "mv", "eps", "root", "rec", "xf", "turned", "xfT", "h", "h_sb", "prod", "row", "part", "trow", "out", "pass")}
        l_in = [m.sem(f"c_in{s}") for s in range(2)]
        x1_s = [m.sem(f"c_x1s{s}") for s in range(2)]
        xf_s = [m.sem(f"c_xfs{s}") for s in range(2)]
        with nc.Block() as block:
            @block.sync
            def _(sp):
                sp.dma_start(wg[:], A.W_gat.rearrange("(c p) o -> p c o", p=P)).then_inc(S["w"], 16)
                for n, a in enumerate((A.att_src, A.att_dst)):
                    sp.dma_start(att[:, n], a.rearrange("(o h) e -> o (h e)", o=1).to_broadcast([P, GW])
                                 ).then_inc(S["w"], 16)

                def load(k, i, s):
                    sp.wait_ge(S["x1"], k * SUB + SUB)
                    for p0, p1 in ((0, 120), (120, TN)):
                        sp.dma_start(pre[p0:p1, s], K.pre_d[bass.ds(k, 1)].rearrange("a p j f -> p (a j) f")[p0:p1]
                                     ).then_inc(l_in[s], 16)

                def store(k, i, s):
                    sp.wait_ge(S["x1"], k * SUB + 3 * SUB)
                    for p0, p1 in ((0, 120), (120, TN)):
                        sp.dma_start(K.x1_d[bass.ds(k, 1)].rearrange("a p j f -> p (a j) f")[p0:p1], x1[p0:p1, s]
                                     ).then_inc(x1_s[s], 16)
                    sp.wait_ge(S["xfT"], k * KC + KC)
                    sp.dma_start(K.xfT_d[bass.ds(k, 1)].rearrange("a p c n -> p (a c) n"), xfT[:, s]
                                 ).then_inc(xf_s[s], 16)

                load(0, 0, 0)
                load(1, 0, 1)
                with sp.Fori(0, (NB - 3) // 2) as i:
                    for s in range(2):
                        load(i * 2 + 2 + s, i + 1, s)
                        store(i * 2 + s, i, s)
                load(NB - 1, 0, 0)
                store(NB - 3, 0, 0)
                store(NB - 2, 0, 1)
                store(NB - 1, 0, 0)
                for s in range(2):
                    sp.wait_ge(x1_s[s], 32 * ((NB + 1 - s) // 2))
                    sp.wait_ge(xf_s[s], 16 * ((NB + 1 - s) // 2))
                sp.wait_ge(S["trow"], 2)
                sp.dma_start(K.gtab.rearrange("(t p) f -> p t f", p=TN), trow[0:TN]).then_inc(S["out"], 16)
                sp.wait_ge(S["out"], 16)

            @block.vector
            def _(dve):
                dve.sem_inc(S["x1"], 2 * SUB)
                dve.wait_ge(S["w"], 16 * 3)

                def statistics(k, i, s):
                    dve.wait_ge(l_in[s], i * 32 + 32)
                    dve.wait_ge(x1_s[s], i * 32)
                    for j in range(SUB):
                        t = k * SUB + j
                        dve.scalar_tensor_tensor(x1[0:TN, s, j], K.acc[0:TN, bass.ds(t, 1), :].rearrange("p a f -> p (a f)"),
                                                 K.dinv[0:TN, bass.ds(t, 1)], pre[0:TN, s, j], ALU.mult, ALU.add
                                                 ).then_inc(S["x1"], 1)
                    dve.wait_ge(S["x1"], k * SUB + 3 * SUB)
                    for j in range(SUB):
                        dve.bn_stats(st6[0:TN, j], x1[0:TN, s, j]).then_inc(S["st"], 1)
                    dve.wait_ge(S["st"], k * SUB + SUB)
                    dve.sem_inc(S["pass"], 1)
                    for j in range(SUB):
                        dve.bn_aggr(mv[0:TN, s, j], st6[0:TN, j]).then_inc(S["mv"], 1)
                    dve.wait_ge(S["mv"], k * SUB + SUB)
                    dve.tensor_scalar(rs[0:TN, s, :, 0], mv[0:TN, s, :, 1], EPS, None, ALU.add).then_inc(S["eps"], 1)

                def normalise(k, i, s):
                    dve.wait_ge(S["root"], k + 1)
                    dve.reciprocal(rs[0:TN, s, :, 0], rs[0:TN, s, :, 1]).then_inc(S["rec"], 1)
                    dve.wait_ge(S["rec"], k + 1)
                    dve.wait_ge(S["turned"], i * (2 * KC))
                    for j in range(SUB):
                        dve.tensor_scalar(xf[0:TN, s, j], x1[0:TN, s, j], mv[0:TN, s, j, 0:1], rs[0:TN, s, j, 0:1],
                                          ALU.subtract, ALU.mult).then_inc(S["xf"], 1)
                    dve.wait_ge(S["xf"], k * SUB + SUB)

                statistics(0, 0, 0)
                with dve.Fori(0, NB // 2) as i:
                    statistics(i * 2 + 1, i, 1)
                    normalise(i * 2, i, 0)
                    statistics(i * 2 + 2, i + 1, 0)
                    normalise(i * 2 + 1, i, 1)
                normalise(NB - 1, NB // 2, 0)
                dve.wait_ge(S["h_sb"], NB)
                v4 = "p t (h e) -> p t h e"
                n = 0
                shape = [TN, NT, GW]
                dve.tensor_copy(K.hrow[0:TN, :, 0:GW], hg[0:TN]).then_inc(S["row"], 1)
                for a, out in ((0, K.hrow[0:TN, :, GW:ROW]), (1, K.adst[0:TN])):
                    dve.tensor_tensor(prod[0:TN], hg[0:TN], att[0:TN, a].unsqueeze(1).to_broadcast(shape), ALU.mult
                                      ).then_inc(S["prod"], 1)
                    dve.wait_ge(S["prod"], a + 1)
                    dve.tensor_reduce(out, prod[0:TN].rearrange(v4, h=GH), AX.X, ALU.add).then_inc(S["row"], 1)
                    dve.wait_ge(S["row"], a + 2)
                q = slice(0, TN)
                left = K.hrow[q, :, GW:ROW]
                for v in range(PARTS):
                    part = trow[q, :, ROW:TROW].bitcast(BF16)[:, :, v * GH:(v + 1) * GH]
                    dve.tensor_copy(part, left).then_inc(S["part"], 1)
                    dve.wait_ge(S["part"], 2 * v + 1)
                    if v < PARTS - 1:
                        rest = prod[q, :, v * GH:(v + 1) * GH]
                        dve.tensor_tensor(rest, left, part, ALU.subtract).then_inc(S["part"], 1)
                        dve.wait_ge(S["part"], 2 * v + 2)
                        left = rest
                dve.tensor_copy(trow[q, :, 0:ROW], K.hrow[q]).then_inc(S["trow"], 1)
                dve.sem_inc(S["trow"], 1)

            @block.scalar
            def _(act):
                def roots(k, s):
                    act.wait_ge(S["eps"], k + 1)
                    act.activation(rs[0:TN, s, :, 1], rs[0:TN, s, :, 0], ACT.Sqrt).then_inc(S["root"], 1)

                def body(k, i, s):
                    if not (isinstance(k, int) and k == NB - 1):
                        roots(k + 1, 1 - s)
                    act.wait_ge(xf_s[s], i * 16)
                    for c in range(KC):
                        act.wait_ge(S["turned"], k * KC + c + 1)
                        act.copy(xfT[:, s, c], ptr[:, s, c, 0:BN]).then_inc(S["xfT"], 1)
                    act.wait_ge(S["h"], k + 1)
                    act.copy(hg[0:TN, bass.ds(k * SUB, SUB), :], ph[0:TN, s, 0:SUB * GW].rearrange("p (j o) -> p j o", j=SUB)
                             ).then_inc(S["h_sb"], 1)
                roots(0, 0)
                blocks(act, body)

            @block.tensor
            def _(pe):
                pe.wait_ge(S["w"], 16 * 3)

                def body(k, i, s):
                    pe.wait_ge(S["xf"], k * SUB + SUB)
                    pe.wait_ge(S["xfT"], i * (2 * KC))
                    for c in range(KC):
                        for j in range(SUB):
                            mm = pe.transpose(ptr[:, s, c, j * TN:(j + 1) * TN], xf[0:TN, s, j, c * P:(c + 1) * P],
                                              K.ident[0:TN, 0:TN])
                        mm.then_inc(S["turned"], 1)
                    pe.wait_ge(S["xfT"], k * KC + KC)
                    pe.wait_ge(S["h_sb"], i * 2)
                    for j in range(SUB):
                        for c in range(KC):
                            mm = pe.matmul(ph[0:TN, s, j * GW:(j + 1) * GW], xfT[:, s, c, j * TN:(j + 1) * TN], wg[:, c],
                                           start=c == 0, stop=c == KC - 1, skip_group_check=True)
                    mm.then_inc(S["h"], 1)
                blocks(pe, body)


def gat_tables(nc, K):
    G, T = G_GAT, G_GAT * P
    with ExitStack() as ctx:
        m = Mem(nc, ctx)
        step = m.sb("n_step", [P, G])
        at = m.sb("n_at", [P, G, NT])
        first = m.sb("n_first", [P, G])
        diag = m.sb("n_diag", [P, 2, P])
        pt = m.ps("n_pt", [P, 2, 512])
        pc = m.ps("n_pc", [P, 2, 512])
        c, tables, diag_s, spread, turned, used = (m.sem("n_" + x) for x in (
            "c", "tables", "diag", "spread", "turned", "used"))
        with nc.Block() as block:
            @block.vector
            def _(dve):
                n = [0]

                def done(ins):
                    n[0] += 1
                    ins.then_inc(c, 1)
                    dve.wait_ge(c, n[0])

                both = [P, G, NT]
                for g in range(G):
                    done(dve.tensor_scalar(step[:, g:g + 1], K.part[:], float(P * g), None, ALU.add))
                st = step[:].unsqueeze(2).to_broadcast(both)
                starts = K.gat_start[:].unsqueeze(1).to_broadcast(both)
                ends = K.gat_end[:].unsqueeze(1).to_broadcast(both)
                done(dve.tensor_tensor(at[:], ends, st, ALU.is_le))
                done(dve.tensor_tensor(K.step_tile[:], starts, st, ALU.is_le))
                done(dve.tensor_tensor(K.step_tile[:], K.step_tile[:], at[:], ALU.subtract))
                dve.sem_inc(tables, 1)
                done(dve.tensor_tensor(at[:], starts, st, ALU.is_equal))
                done(dve.tensor_reduce(first[:], at[:], AX.X, ALU.add))
                done(dve.scalar_tensor_tensor(K.last[:], ends, -1.0, st, ALU.add, ALU.is_equal))
                for g in range(G):
                    if g >= 2:
                        dve.wait_ge(spread, g - 1)
                    dve.tensor_scalar(diag[:, g % 2], K.ident[:], first[:, g:g + 1], -BIG, ALU.mult, ALU.mult
                                      ).then_inc(diag_s, 1)
                    dve.wait_ge(spread, g + 1)
                    dve.tensor_copy(K.cut[:, g * P:(g + 1) * P], pc[:, g % 2, 0:P]).then_inc(used, 1)
                    dve.wait_ge(turned, g + 1)
                    dve.tensor_copy(K.tile_step[0:NT, g * P:(g + 1) * P], pt[0:NT, g % 2, 0:P]).then_inc(used, 1)

            @block.tensor
            def _(pe):
                pe.wait_ge(tables, 1)
                for g in range(G):
                    if g >= 2:
                        pe.wait_ge(used, 2 * (g - 1))
                    pe.wait_ge(diag_s, g + 1)
                    pe.matmul(pc[:, g % 2, 0:P], K.ones[:], diag[:, g % 2], start=True, stop=True).then_inc(spread, 1)
                    pe.transpose(pt[0:NT, g % 2, 0:P], K.step_tile[:, g], K.ident[:]).then_inc(turned, 1)


def gat_max(nc, K):
    W = BATCH
    rounds = S_GAT // (W * HALVES)
    HW = W * GH
    with ExitStack() as ctx:
        m = Mem(nc, ctx)
        at = m.sb("x_at", [P, HALVES, W], U32)
        rows = m.sb("x_rows", [P, HALVES, W, TROW])
        other = m.sb("x_other", [P, HALVES, W, TN], BF16)
        neg = m.sb("x_neg", [P, P], BF16)
        ident_h = m.sb("x_ident", [P, P], BF16)
        pick_f = m.sb("x_pick_f", [P, HW])
        pick = m.sb("x_pick", [P, HW], BF16)
        aT = m.sb("x_aT", [P, HALVES, P], BF16)
        asr = m.sb("x_asr", [P, HALVES, PARTS, W, GH], BF16)
        px = m.ps("x_px", [P, 2, 2, GH, P])
        pt = m.ps("x_pt", [P, HALVES, 1024], BF16)
        S = {n: m.sem("x_" + n) for n in ("set", "neg", "at", "pass", "other", "asr", "kept", "turned", "aT", "px", "mx")}
        got = [m.gather_sem(f"x_got{h}") for h in range(HALVES)]
        with nc.Block() as block:
            @block.gpsimd
            def _(pool):
                with pool.Fori(0, rounds) as i:
                    for h in range(HALVES):
                        pool.wait_ge(S["at"], i * HALVES + h + 1)
                        pool.wait_ge(S["kept"], i * HALVES + h + 1)
                        pool.sem_inc(S["pass"], 1)
                        for b in range(W):
                            pool.indirect_dma_start(
                                out=rows[:, h, b], out_offset=None, in_=K.gtab,
                                in_offset=bass.IndirectOffsetOnAxis(ap=at[:, h, b:b + 1], axis=0)
                            ).then_inc(got[h], 16)

            @block.scalar
            def _(act):
                act.sem_inc(S["kept"], 2)
                for h in range(HALVES):
                    act.copy(at[:, h], K.gat_srcT[:, h * W:(h + 1) * W]).then_inc(S["at"], 1)
                with act.Fori(0, rounds) as i:
                    for h in range(HALVES):
                        n = i * HALVES + h
                        act.wait_ge(got[h], (i + 1) * (16 * W))
                        act.wait_ge(S["turned"], i * HALVES)
                        act.copy(asr[:, h], rows[:, h, :, ROW:TROW].bitcast(BF16).rearrange("p w (v g) -> p v w g", v=PARTS)
                                 ).then_inc(S["asr"], 1)
                        act.copy(K.feat[:, bass.ds(n * W, W), :], rows[:, h, :, 0:ROW]).then_inc(S["kept"], 1)
                        act.copy(at[:, h], K.gat_srcT[:, bass.ds((n + HALVES) * W, W)]).then_inc(S["at"], 1)
                        act.wait_ge(S["turned"], n + 1)
                        act.wait_ge(S["px"], i * (HALVES * W // 2))
                        act.copy(aT[0:PARTS * HW, h], pt[0:PARTS * HW, h, 0:P]).then_inc(S["aT"], 1)

            @block.tensor
            def _(pe):
                pe.wait_ge(S["neg"], 3)
                with pe.Fori(0, rounds) as i:
                    for h in range(HALVES):
                        n = i * HALVES + h
                        pe.wait_ge(S["asr"], n + 1)
                        pe.wait_ge(S["aT"], i * HALVES)
                        pe.transpose(pt[0:PARTS * HW, h, 0:P], asr[:, h].rearrange("p v w g -> p (v w g)"), ident_h[:]
                                     ).then_inc(S["turned"], 1)
                        pe.wait_ge(S["aT"], n + 1)
                        pe.wait_ge(S["other"], n + 1)
                        for b in range(W):
                            pair, slot = b // 2, (b // 2) % 2
                            if b % 2 == 0:
                                pe.wait_ge(S["mx"], n * (W // 2) + pair + 1)
                            pe.matmul(px[0:TN, slot, b % 2], other[:, h, b], neg[:].unsqueeze(1).to_broadcast([P, GH, P]),
                                      start=True, stop=False, skip_group_check=True)
                            for g in range(GH):
                                r = b * GH + g
                                mm = pe.matmul(px[0:TN, slot, b % 2, g],
                                               pick[0:PARTS * HW, r:r + 1].to_broadcast([PARTS * HW, TN]),
                                               aT[0:PARTS * HW, h], start=False, stop=g == GH - 1, skip_group_check=True)
                            if b % 2 == 1:
                                mm.then_inc(S["px"], 1)

            @block.vector
            def _(dve):
                dve.tensor_scalar(neg[:], K.ident[:], -BIG, None, ALU.mult).then_inc(S["neg"], 1)
                dve.tensor_copy(ident_h[:], K.ident[:]).then_inc(S["neg"], 1)
                dve.tensor_tensor(pick_f[:], K.ident[:, 0:HW], K.ident[:, HW:2 * HW], ALU.add).then_inc(S["set"], 1)
                dve.wait_ge(S["set"], 1)
                dve.tensor_tensor(pick[:], pick_f[:], K.ident[:, 2 * HW:3 * HW], ALU.add).then_inc(S["neg"], 1)
                dve.memset(K.feat[:, S_GAT:G_GAT * P, :], 0.0).then_inc(S["set"], 1)
                dve.memset(K.mx[:, :, S_GAT:G_GAT * P], 0.0).then_inc(S["set"], 1)
                dve.sem_inc(S["mx"], 2)
                with dve.Fori(0, rounds) as i:
                    for h in range(HALVES):
                        n = i * HALVES + h
                        dve.wait_ge(S["px"], i * (HALVES * W // 2))
                        shape = [P, W, TN]
                        dve.tensor_tensor(other[:, h], K.iota[:, 0:TN].unsqueeze(1).to_broadcast(shape),
                                          K.gat_dstT[:, bass.ds(n * W, W)].unsqueeze(2).to_broadcast(shape),
                                          ALU.not_equal).then_inc(S["other"], 1)
                    for h in range(HALVES):
                        n = i * HALVES + h
                        for j in range(W // 2):
                            dve.wait_ge(S["px"], n * (W // 2) + j + 1)
                            dve.tensor_reduce(K.mx[0:TN, :, bass.ds(n * W + 2 * j, 2)].rearrange("p g w -> p w g"),
                                              px[0:TN, j % 2], AX.X, ALU.max).then_inc(S["mx"], 1)


def by_tile(nc, K, tag, values, columns_last, n_cols, select, out):
    G, B = G_GAT, 3
    banks = -(-G // B)
    with ExitStack() as ctx:
        m = Mem(nc, ctx)
        col = m.sb(tag + "_col", [P, 2, G * P])
        turned_sb = m.sb(tag + "_turned_sb", [P, banks, B, P])
        pt = m.ps(tag + "_pt", [P, banks, 512])
        po = m.ps(tag + "_po", [P, 2, 512])
        passed, ready, turned, copied, summed, taken = (m.sem(tag + x) for x in (
            "_passed", "_ready", "_turned", "_copied", "_summed", "_taken"))
        with nc.Block() as block:
            @block.tensor
            def _(pe):
                pe.sem_inc(taken, 2)
                with pe.Fori(0, n_cols // 2) as i:
                    for s in range(2):
                        c = i * 2 + s
                        pe.wait_ge(ready, c + 1)
                        pe.wait_ge(copied, c * banks)
                        for g in range(G):
                            b = g // B
                            mm = pe.transpose(pt[:, b, (g % B) * P:(g % B) * P + TN], col[0:TN, s, g * P:(g + 1) * P],
                                              K.ident[0:TN, 0:TN])
                            if g % B == B - 1 or g == G - 1:
                                mm.then_inc(turned, 1)
                        pe.wait_ge(taken, c + 1)
                        for g in range(G):
                            if g % B == 0:
                                pe.wait_ge(copied, c * banks + g // B + 1)
                            mm = pe.matmul(po[0:TN, s, 0:NT], turned_sb[:, g // B, g % B, 0:TN], select[:, g],
                                           start=g == 0, stop=g == G - 1)
                        mm.then_inc(summed, 1)

            @block.scalar
            def _(act):
                with act.Fori(0, n_cols) as c:
                    act.wait_ge(summed, c)
                    for b in range(banks):
                        w = min(B, G - b * B)
                        act.wait_ge(turned, c * banks + b + 1)
                        act.copy(turned_sb[:, b, 0:w, 0:TN], pt[:, b, 0:w * P].rearrange("p (g n) -> p g n", n=P)[:, :, 0:TN]
                                 ).then_inc(copied, 1)

            @block.vector
            def _(dve):
                def stage(c, s):
                    if columns_last:
                        column = values[0:TN, :, bass.ds(c, 1)].rearrange("p s c -> p (s c)")
                    else:
                        column = values[0:TN, bass.ds(c, 1), :].rearrange("p c s -> p (c s)")
                    dve.sem_inc(passed, 1)
                    dve.tensor_copy(col[0:TN, s], column).then_inc(ready, 1)

                def take(c, s):
                    dve.wait_ge(summed, c + 1)
                    dve.sem_inc(passed, 1)
                    dve.tensor_copy(out[0:TN, :, bass.ds(c, 1)].rearrange("p t c -> p (t c)"), po[0:TN, s, 0:NT]
                                    ).then_inc(taken, 1)

                stage(0, 0)
                stage(1, 1)
                with dve.Fori(0, n_cols // 2 - 1) as i:
                    for s in range(2):
                        c = i * 2 + s
                        dve.wait_ge(turned, c * banks + banks)
                        stage(c + 2, s)
                        take(c, s)
                take(n_cols - 2, 0)
                take(n_cols - 1, 1)


def scan_max(nc, K):
    with ExitStack() as ctx:
        m = Mem(nc, ctx)
        scanned = m.sem("y_scanned")
        with nc.Block() as block:
            @block.vector
            def _(dve):
                for g in range(GH):
                    dve.tensor_tensor_scan(K.mx[0:TN, g], K.cut[0:TN], K.mx[0:TN, g], -BIG, ALU.add, ALU.max
                                           ).then_inc(scanned, 1)


def gat_spread(nc, K, peak, own):
    C, G3 = 2 * GH, 3
    PART = G_GAT * P // G3
    with ExitStack() as ctx:
        m = Mem(nc, ctx)
        am = m.sb("e_am", [P, C, NT])
        amT = m.sb("e_amT", [P, PARTS, C, P], BF16)
        rest = m.sb("e_rest", [P, 2, C, P])
        pt = m.ps("e_pt", [P, 2, 4, P])
        pe_s = m.ps("e_ps", [P, G3, 512])
        passed, c, turned, amT_s, spread, taken, ex = (m.sem("e_" + x) for x in (
            "passed", "c", "turned", "amT", "spread", "taken", "ex"))
        q = slice(0, TN)
        with nc.Block() as block:
            @block.vector
            def _(dve):
                n = [0]

                def done(ins):
                    n[0] += 1
                    ins.then_inc(c, 1)
                    dve.wait_ge(c, n[0])

                asrc = K.hrow[q, :, GW:ROW]
                ad, M = am[q, 0:GH].rearrange("p g t -> p t g"), am[q, GH:C].rearrange("p g t -> p t g")
                done(dve.tensor_tensor(M, peak[q], asrc, ALU.max))
                done(dve.tensor_copy(ad, K.adst[q]))
                done(dve.tensor_tensor(M, M, ad, ALU.add))
                done(dve.tensor_tensor(own[q], asrc, K.adst[q], ALU.add))
                done(dve.scalar_tensor_tensor(M, M, 0.2, M, ALU.mult, ALU.max))
                done(dve.scalar_tensor_tensor(own[q], own[q], 0.2, own[q], ALU.mult, ALU.max))
                done(dve.tensor_tensor(own[q], own[q], M, ALU.subtract))
                dve.wait_ge(turned, 2)
                done(dve.tensor_copy(rest[0:NT, 0, :, 0:TN].rearrange("p (b k) n -> p b k n", b=2), pt[0:NT, :, :, 0:TN]))
                for v in range(PARTS):
                    done(dve.tensor_copy(amT[0:NT, v, :, 0:TN], rest[0:NT, v % 2, :, 0:TN]))
                    if v < PARTS - 1:
                        done(dve.tensor_tensor(rest[0:NT, 1 - v % 2, :, 0:TN], rest[0:NT, v % 2, :, 0:TN],
                                               amT[0:NT, v, :, 0:TN], ALU.subtract))
                dve.sem_inc(amT_s, 1)
                with dve.Fori(0, PARTS * C) as i:
                    for b in range(G3):
                        dve.wait_ge(spread, i * G3 + b + 1)
                        dve.sem_inc(passed, 1)
                        dve.tensor_copy(K.spread[q, bass.ds(i, 1), b * PART:(b + 1) * PART].rearrange("p c s -> p (c s)"),
                                        pe_s[q, b, 0:PART]).then_inc(taken, 1)

            @block.scalar
            def _(act):
                act.wait_ge(c, 7)
                act.activation(own[q], own[q], ACT.Exp).then_inc(ex, 1)

            @block.tensor
            def _(pe):
                pe.sem_inc(taken, G3)
                pe.wait_ge(c, 7)
                for b in range(2):
                    for k in range(4):
                        mm = pe.transpose(pt[0:NT, b, k, 0:TN], am[q, b * 4 + k], K.ident[q, q])
                    mm.then_inc(turned, 1)
                pe.wait_ge(amT_s, 1)
                for k in range(PARTS * C):
                    for b in range(G3):
                        pe.wait_ge(taken, k * G3 + b + 1)
                        pe.matmul(pe_s[q, b, 0:PART], amT[0:NT, k // C, k % C, 0:TN], K.tile_step[0:NT, b * PART:(b + 1) * PART],
                                  start=True, stop=True).then_inc(spread, 1)


def gat_sum(nc, K):
    W, SLOTS = BATCH, 6
    R = G_GAT * P // W
    with ExitStack() as ctx:
        m = Mem(nc, ctx)
        ident_h = m.sb("s_ident", [P, P], BF16)
        hot = m.sb("s_hot", [P, SLOTS, W, P], BF16)
        hotT = m.sb("s_hotT", [P, 2, W, P], BF16)
        mine = m.sb("s_mine", [P, 2, PARTS, 2 * GH, W], BF16)
        parts = m.sb("s_parts", [P, 2, PARTS, W, ROW], BF16)
        rest = m.sb("s_rest", [P, 2, W, ROW])
        z = m.sb("s_z", [P, 2, W, GH])
        z2 = m.sb("s_z2", [P, 2, W, GH])
        msg = m.sb("s_msg", [P, 2, W, ROW])
        pt = m.ps("s_pt", [P, 2, W, P], BF16)
        pb = m.ps("s_pb", [P, 2, 512])
        po = m.ps("s_po", [P, 2, 512])
        S = {n: m.sem("s_" + n) for n in (
            "ident", "hot", "mine", "turned", "hotT", "pb", "z", "e", "msg", "hi", "rest", "mid", "lo", "po", "sum", "pass")}

        def turns(eng, turn):
            def peeled(a, b):
                for t in range(a, b):
                    turn(t, t % SLOTS, lambda d, t=t: 0 <= t - d < R, lambda d, n, t=t: t - d >= n)
            peeled(-1, SLOTS)
            with eng.Fori(1, R // SLOTS - 1) as i:
                for k in range(SLOTS):
                    turn(i * SLOTS + k, k, lambda d: True, lambda d, n: True)
            peeled(R - SLOTS, R + 5)

        with nc.Block() as block:
            @block.vector
            def _(dve):
                def build(n, s, reused):
                    if reused:
                        dve.wait_ge(S["po"], n - SLOTS + 1)
                    shape = [P, W, P]
                    dve.tensor_tensor(hot[:, s], K.iota[:].unsqueeze(1).to_broadcast(shape),
                                      K.gat_dstT[:, bass.ds(n * W, W)].unsqueeze(2).to_broadcast(shape),
                                      ALU.is_equal).then_inc(S["hot"], 1)

                def exponents(n, h):
                    a_src = K.feat[:, bass.ds(n * W, W), GW:ROW]
                    ps = pb[:, h, 0:W * 2 * GH].rearrange("p (w g) -> p w g", w=W)
                    dve.wait_ge(S["pb"], n + 1)
                    dve.tensor_tensor(z[:, h], a_src, ps[:, :, 0:GH], ALU.add).then_inc(S["z"], 1)
                    dve.wait_ge(S["z"], n * 4 + 1)
                    dve.scalar_tensor_tensor(z[:, h], z[:, h], 0.2, z[:, h], ALU.mult, ALU.max).then_inc(S["z"], 1)
                    dve.wait_ge(S["z"], n * 4 + 2)
                    dve.tensor_tensor(z2[:, h], z[:, h], ps[:, :, GH:2 * GH], ALU.subtract).then_inc(S["z"], 1)
                    dve.wait_ge(S["z"], n * 4 + 3)
                    dve.tensor_scalar(z2[:, h], z2[:, h], 0.0, None, ALU.min).then_inc(S["z"], 1)

                def messages(n, h):
                    f = K.feat[:, bass.ds(n * W, W), 0:GW]
                    dve.wait_ge(S["e"], n + 1)
                    w4 = msg[:, h, :, GW:ROW].unsqueeze(3).to_broadcast([P, W, GH, NE])
                    dve.tensor_tensor(msg[:, h, :, 0:GW].rearrange("p w (h e) -> p w h e", h=GH),
                                      f.rearrange("p w (h e) -> p w h e", h=GH), w4, ALU.mult).then_inc(S["msg"], 1)

                def take(n, h):
                    dve.wait_ge(S["po"], n + 1)
                    dve.sem_inc(S["pass"], 1)
                    dve.tensor_copy(K.feat[0:TN, bass.ds(n * W, W), :],
                                    po[0:TN, h, 0:W * ROW].rearrange("p (w c) -> p w c", w=W)).then_inc(S["sum"], 1)

                def turn(m, k, has, reused):
                    if has(2):
                        exponents(m - 2, k % 2)
                    if has(-1):
                        build(m + 1, (k + 1) % SLOTS, reused(-1, SLOTS))
                    if has(2):
                        messages(m - 2, k % 2)
                    if has(5):
                        take(m - 5, (k + 1) % 2)

                dve.tensor_copy(ident_h[:], K.ident[:]).then_inc(S["ident"], 1)
                turns(dve, turn)

            @block.gpsimd
            def _(pool):
                def fetch(n, h, reused):
                    if reused:
                        pool.wait_ge(S["pb"], n - 1)
                    pool.tensor_copy(mine[0:TN, h].rearrange("p v c w -> p (v c) w"),
                                     K.spread[0:TN, :, bass.ds(n * W, W)]).then_inc(S["mine"], 1)

                def first_rest(n, h, reused):
                    pool.wait_ge(S["hi"], n + 1)
                    if reused:
                        pool.wait_ge(S["lo"], n - 1)
                    pool.tensor_tensor(rest[:, h], msg[:, h], parts[:, h, 0], ALU.subtract).then_inc(S["rest"], 1)

                def last_rest(n, h):
                    pool.wait_ge(S["mid"], n + 1)
                    pool.tensor_tensor(parts[:, h, 2], rest[:, h], parts[:, h, 1], ALU.subtract).then_inc(S["lo"], 1)

                def turn(m, k, has, reused):
                    if has(3):
                        first_rest(m - 3, (k + 1) % 2, reused(3, 2))
                    if has(0):
                        fetch(m, k % 2, reused(0, 2))
                    if has(3):
                        last_rest(m - 3, (k + 1) % 2)

                turns(pool, turn)

            @block.scalar
            def _(act):
                def copies(n, h, reused):
                    if reused:
                        act.wait_ge(S["pb"], n - 1)
                    act.wait_ge(S["turned"], n + 1)
                    act.copy(hotT[:, h], pt[:, h]).then_inc(S["hotT"], 1)

                def weights(n, h, reused):
                    act.wait_ge(S["z"], n * 4 + 4)
                    if reused:
                        act.wait_ge(S["rest"], n - 1)
                    act.activation(msg[:, h, :, GW:ROW], z2[:, h], ACT.Exp).then_inc(S["e"], 1)

                def high_part(n, h, reused):
                    act.wait_ge(S["msg"], n + 1)
                    if reused:
                        act.wait_ge(S["po"], n - 1)
                    act.copy(parts[:, h, 0], msg[:, h]).then_inc(S["hi"], 1)

                def middle_part(n, h):
                    act.wait_ge(S["rest"], n + 1)
                    act.copy(parts[:, h, 1], rest[:, h]).then_inc(S["mid"], 1)

                def turn(m, k, has, reused):
                    if has(3):
                        high_part(m - 3, (k + 1) % 2, reused(3, 2))
                    if has(0):
                        copies(m, k % 2, reused(0, 2))
                    if has(3):
                        middle_part(m - 3, (k + 1) % 2)
                    if has(2):
                        weights(m - 2, k % 2, reused(2, 2))

                turns(act, turn)

            @block.tensor
            def _(pe):
                def transpose(n, h, s, reused):
                    pe.wait_ge(S["hot"], n + 1)
                    if reused:
                        pe.wait_ge(S["hotT"], n - 1)
                    for b in range(W):
                        mm = pe.transpose(pt[:, h, b], hot[:, s, b], ident_h[:])
                    mm.then_inc(S["turned"], 1)

                def spread(n, h, reused):
                    pe.wait_ge(S["hotT"], n + 1)
                    pe.wait_ge(S["mine"], n + 1)
                    if reused:
                        pe.wait_ge(S["z"], n * 4 - 5)
                    for b in range(W):
                        for v in range(PARTS):
                            mm = pe.matmul(pb[:, h, b * 2 * GH:(b + 1) * 2 * GH], hotT[0:TN, h, b],
                                           mine[0:TN, h, v, :, b], start=v == 0, stop=v == PARTS - 1,
                                           skip_group_check=True)
                    mm.then_inc(S["pb"], 1)

                def add_up(n, h, s, reused):
                    pe.wait_ge(S["lo"], n + 1)
                    if reused:
                        pe.wait_ge(S["sum"], n - 1)
                    for b in range(W):
                        for v in range(PARTS):
                            mm = pe.matmul(po[:, h, b * ROW:(b + 1) * ROW], hot[:, s, b], parts[:, h, v, b],
                                           start=v == 0, stop=v == PARTS - 1, skip_group_check=True)
                    mm.then_inc(S["po"], 1)

                def turn(m, k, has, reused):
                    if has(0):
                        transpose(m, k % 2, k, reused(0, 2))
                    if has(1):
                        spread(m - 1, (k + 1) % 2, reused(1, 2))
                    if has(4):
                        add_up(m - 4, k % 2, (k - 4) % SLOTS, reused(4, 2))

                pe.wait_ge(S["ident"], 1)
                turns(pe, turn)


def gat_own(nc, K, own, sums):
    with ExitStack() as ctx:
        m = Mem(nc, ctx)
        c = m.sem("o_c")
        q = slice(0, TN)
        v4 = "p t (h e) -> p t h e"
        with nc.Block() as block:
            @block.vector
            def _(dve):
                dve.tensor_tensor(K.gsum[q, :, 0:GW].rearrange(v4, h=GH), K.hrow[q, :, 0:GW].rearrange(v4, h=GH),
                                  own[q].unsqueeze(3).to_broadcast([TN, NT, GH, NE]), ALU.mult).then_inc(c, 1)
                dve.tensor_tensor(K.gsum[q, :, GW:ROW], sums[q, :, GW:ROW], own[q], ALU.add).then_inc(c, 1)
                dve.wait_ge(c, 1)
                dve.tensor_tensor(K.gsum[q, :, 0:GW], K.gsum[q, :, 0:GW], sums[q, :, 0:GW], ALU.add).then_inc(c, 1)


def gates(nc, K, A):
    with ExitStack() as ctx:
        m = Mem(nc, ctx)
        row = m.sb("e_row", [P, 3, GW])
        agg = m.sb("e_agg", [P, NT, GW])
        sq = m.sb("e_sq", [P, NT, GW])
        den = m.sb("e_den", [P, NT, GH])
        st = m.sb("e_st", [P, 4, NT])
        sc = m.sb("e_sc", [P, NT, NE])
        rank = m.sb("e_rank", [P, NT, NE])
        cmp_ = m.sb("e_cmp", [P, NT])
        w_s, v, root, ex = (m.sem("e_" + x) for x in ("w", "v", "root", "exp"))
        q = slice(0, TN)
        with nc.Block() as block:
            @block.sync
            def _(sp):
                for n, a in enumerate((A.b_gat, A.ln_gamma, A.ln_beta)):
                    sp.dma_start(row[:, n], a.rearrange("(a o) -> a o", a=1).to_broadcast([P, GW])).then_inc(w_s, 16)

            @block.scalar
            def _(act):
                act.wait_ge(v, 10)
                act.activation(st[q, 1], st[q, 1], ACT.Sqrt).then_inc(root, 1)
                act.wait_ge(root, 2)
                act.activation(sc[q], sc[q], ACT.Exp).then_inc(ex, 1)

            @block.vector
            def _(dve):
                n = [0]

                def step(ins):
                    n[0] += 1
                    ins.then_inc(v, 1)
                    dve.wait_ge(v, n[0])

                def wide(ap, width=GW):
                    return ap.unsqueeze(2).to_broadcast([TN, NT, width])

                def param(r):
                    return row[q, r].unsqueeze(1).to_broadcast([TN, NT, GW])

                dve.wait_ge(w_s, 48)
                step(dve.tensor_scalar(den[q], K.gsum[q, :, GW:ROW], 1e-16, None, ALU.add))
                step(dve.reciprocal(den[q], den[q]))
                step(dve.tensor_tensor(agg[q].rearrange("p t (h e) -> p t h e", h=GH),
                                       K.gsum[q, :, 0:GW].rearrange("p t (h e) -> p t h e", h=GH),
                                       den[q].unsqueeze(3).to_broadcast([TN, NT, GH, NE]), ALU.mult))
                step(dve.tensor_tensor(agg[q], agg[q], param(0), ALU.add))
                step(dve.tensor_reduce(st[q, 0], agg[q], AX.X, ALU.add))
                step(dve.tensor_scalar(st[q, 0], st[q, 0], 1.0 / GW, None, ALU.mult))
                step(dve.tensor_tensor(agg[q], agg[q], wide(st[q, 0]), ALU.subtract))
                step(dve.tensor_tensor(sq[q], agg[q], agg[q], ALU.mult))
                step(dve.tensor_reduce(st[q, 1], sq[q], AX.X, ALU.add))
                step(dve.tensor_scalar(st[q, 1], st[q, 1], 1.0 / GW, EPS, ALU.mult, ALU.add))
                dve.wait_ge(root, 1)
                step(dve.reciprocal(st[q, 1], st[q, 1]))
                step(dve.tensor_tensor(agg[q], agg[q], wide(st[q, 1]), ALU.mult))
                step(dve.tensor_tensor(agg[q], agg[q], param(1), ALU.mult))
                step(dve.tensor_tensor(agg[q], agg[q], param(2), ALU.add))
                step(dve.tensor_reduce(sc[q], agg[q].rearrange("p t (h e) -> p t e h", h=GH), AX.X, ALU.add))
                step(dve.tensor_scalar(sc[q], sc[q], 1.0 / GH, None, ALU.mult))
                step(dve.tensor_reduce(st[q, 2], sc[q], AX.X, ALU.max))
                for e in range(NE):
                    first = True
                    for f in range(NE):
                        if f == e:
                            continue
                        out = rank[q, :, e] if first else cmp_[q]
                        step(dve.tensor_tensor(out, sc[q, :, f], sc[q, :, e], ALU.is_ge if f < e else ALU.is_gt))
                        if not first:
                            step(dve.tensor_tensor(rank[q, :, e], rank[q, :, e], cmp_[q], ALU.add))
                        first = False
                step(dve.tensor_scalar(rank[q], rank[q], 1.5, None, ALU.is_lt))
                step(dve.tensor_tensor(sc[q], sc[q], wide(st[q, 2], NE), ALU.subtract))
                dve.sem_inc(root, 1)
                dve.wait_ge(ex, 1)
                step(dve.tensor_tensor(sc[q], sc[q], rank[q], ALU.mult))
                step(dve.tensor_reduce(st[q, 3], sc[q], AX.X, ALU.add))
                step(dve.reciprocal(st[q, 3], st[q, 3]))
                step(dve.tensor_tensor(K.gate[q], sc[q], wide(st[q, 3], NE), ALU.mult))


def experts(nc, K, A):
    MC = FF // P
    with ExitStack() as ctx:
        m = Mem(nc, ctx)
        w1 = m.sb("f_w1", [P, NE, KC, FF])
        w2 = m.sb("f_w2", [P, NE, MC, D])
        b1 = m.sb("f_b1", [P, NE, MC])
        b2 = m.sb("f_b2", [P, NE, D])
        xfT = m.sb("f_xfT", [P, 2, KC, BN])
        hh = m.sb("f_hh", [P, 2, MC, BN])
        y = m.sb("f_y", [P, 2, SUB, D])
        ph = m.ps("f_ph", [P, 4, 512])
        py = m.ps("f_py", [P, 2, 2, 512])
        S = {n: m.sem("f_" + n) for n in ("w", "free", "ph", "hh", "py", "y", "yb")}
        l_x = [m.sem(f"f_lx{s}") for s in range(2)]
        l_y = [m.sem(f"f_ly{s}") for s in range(2)]
        out_s = [m.sem(f"f_out{s}") for s in range(2)]
        NY = NE * SUB * 2
        with nc.Block() as block:
            @block.sync
            def _(sp):
                for e in range(NE):
                    sp.dma_start(w1[:, e], A.W1[e].rearrange("(c p) o -> p c o", p=P)).then_inc(S["w"], 16)
                    sp.dma_start(w2[:, e], A.W2[e].rearrange("(c p) o -> p c o", p=P)).then_inc(S["w"], 16)
                    sp.dma_start(b2[:, e], A.b2f[e:e + 1].to_broadcast([P, D])).then_inc(S["w"], 16)
                    with nc.allow_non_contiguous_dma(reason="biases"):
                        sp.dma_start(b1[:, e], A.b1f[e].rearrange("(c p) -> p c", p=P)).then_inc(S["w"], 16)

                def load(k, i, s):
                    sp.wait_ge(S["ph"], k * (NE * MC) + NE * MC)
                    sp.dma_start(xfT[:, s], K.xfT_d[bass.ds(k, 1)].rearrange("a p c n -> p (a c) n")).then_inc(l_x[s], 16)
                    sp.wait_ge(out_s[s], i * 32)
                    for p0, p1 in ((0, 120), (120, TN)):
                        sp.dma_start(y[p0:p1, s], K.x1_d[bass.ds(k, 1)].rearrange("a p j f -> p (a j) f")[p0:p1]
                                     ).then_inc(l_y[s], 16)

                def store(k, i, s):
                    sp.wait_ge(S["y"], k * NY + NY)
                    for p0, p1 in ((0, 120), (120, TN)):
                        sp.dma_start(A.out[bass.ds(k * BN, BN)].rearrange("(j p) f -> p j f", p=TN)[p0:p1], y[p0:p1, s]
                                     ).then_inc(out_s[s], 16)

                load(0, 0, 0)
                load(1, 0, 1)
                with sp.Fori(0, (NB - 3) // 2) as i:
                    for s in range(2):
                        store(i * 2 + s, i, s)
                        load(i * 2 + 2 + s, i + 1, s)
                store(NB - 3, 0, 0)
                load(NB - 1, NB // 2, 0)
                store(NB - 2, 0, 1)
                store(NB - 1, 0, 0)
                for s in range(2):
                    sp.wait_ge(out_s[s], 32 * ((NB + 1 - s) // 2))

            @block.tensor
            def _(pe):
                pe.sem_inc(S["ph"], 2 * NE * MC)
                pe.wait_ge(S["w"], 64 * NE)

                def up(k, s, e):
                    for o in range(MC):
                        n = k * (NE * MC) + e * MC + o
                        pe.wait_ge(S["hh"], n + 1)
                        for c in range(KC):
                            mm = pe.matmul(ph[:, o, 0:BN], w1[:, e, c, o * P:(o + 1) * P], xfT[:, s, c],
                                           start=c == 0, stop=c == KC - 1)
                        mm.then_inc(S["ph"], 1)

                def down(k, s, e):
                    pe.wait_ge(S["hh"], k * (NE * MC) + (e + 1) * MC + MC)
                    pe.wait_ge(S["yb"], k * NE + e + 1)
                    for j in range(SUB):
                        for c in range(MC):
                            mm = pe.matmul(py[0:TN, e % 2, j // 2, (j % 2) * D:(j % 2 + 1) * D],
                                           hh[:, e % 2, c, j * TN:(j + 1) * TN], w2[:, e, c],
                                           start=c == 0, stop=c == MC - 1, skip_group_check=True)
                        mm.then_inc(S["py"], 1)

                def body(k, i, s):
                    pe.wait_ge(l_x[s], i * 16 + 16)
                    up(k, s, 0)
                    for e in range(NE):
                        if e + 1 < NE:
                            up(k, s, e + 1)
                        down(k, s, e)
                blocks(pe, body)

            @block.scalar
            def _(act):
                act.wait_ge(S["w"], 64 * NE)
                act.sem_inc(S["hh"], MC)

                def body(k, i, s):
                    for e in range(NE):
                        if e < 2:
                            act.wait_ge(S["py"], k * (NE * SUB))
                        else:
                            act.wait_ge(S["py"], k * (NE * SUB) + (e - 1) * SUB)
                        for o in range(MC):
                            n = k * (NE * MC) + e * MC + o
                            act.wait_ge(S["ph"], n + 2 * NE * MC + 1)
                            act.activation(hh[:, e % 2, o], ph[:, o, 0:BN], ACT.Gelu, bias=b1[:, e, o:o + 1]
                                           ).then_inc(S["hh"], 1)
                blocks(act, body)

            @block.vector
            def _(dve):
                dve.sem_inc(S["yb"], 2)
                dve.wait_ge(S["w"], 64 * NE)

                def body(k, i, s):
                    dve.wait_ge(l_y[s], i * 32 + 32)
                    for e in range(NE):
                        n0 = k * NY + e * (2 * SUB)
                        for j in range(SUB):
                            dve.wait_ge(S["y"], n0 + (j if e == 0 else j - 0))
                            g = K.gate[0:TN, bass.ds(k * SUB + j, 1), e]
                            dve.scalar_tensor_tensor(y[0:TN, s, j], b2[0:TN, e], g, y[0:TN, s, j], ALU.mult, ALU.add
                                                     ).then_inc(S["y"], 1)
                        for j in range(SUB):
                            if j % 2 == 0:
                                dve.wait_ge(S["py"], k * (NE * SUB) + e * SUB + j + 2)
                            dve.wait_ge(S["y"], n0 + SUB + j)
                            g = K.gate[0:TN, bass.ds(k * SUB + j, 1), e]
                            dve.scalar_tensor_tensor(y[0:TN, s, j], py[0:TN, e % 2, j // 2, (j % 2) * D:(j % 2 + 1) * D],
                                                     g, y[0:TN, s, j], ALU.mult, ALU.add).then_inc(S["y"], 1)
                        dve.wait_ge(S["y"], n0 + 2 * SUB)
                        dve.sem_inc(S["yb"], 1)
                blocks(dve, body)


def program(nc, A):
    with ExitStack() as ctx:
        m = Mem(nc, ctx)

        class K:
            pass
        K.gcn_pairs = m.dram("gcn_pairs", [E_GCN + P, 2], I32)
        K.gat_pairs = m.dram("gat_pairs", [E_GAT + P, 2], I32)
        K.hT_d = m.dram("hT_d", [NB, P, KC, BN])
        K.qT_d = m.dram("qT_d", [NB, P, KC, BN])
        K.xfT_d = m.dram("xfT_d", [NB, P, KC, BN])
        K.pre_d = m.dram("pre_d", [NB, TN, SUB, D])
        K.x1_d = m.dram("x1_d", [NB, TN, SUB, D])
        K.table = m.dram("table", [N, D])
        K.gtab = m.dram("gtab", [N, TROW])
        gcn_td = m.dram("gcn_td", [G_GCN * P], I32)
        constants(nc, m, K)
        K.dinv = m.sb("dinv", [P, NT])
        K.gat_srcT = m.sb("gat_srcT", [P, G_GAT * P], U32)
        K.gat_dstT = m.sb("gat_dstT", [P, G_GAT * P])
        K.gat_start = m.sb("gat_start", [P, NT])
        K.gat_end = m.sb("gat_end", [P, NT])
        K.hrow = m.sb("hrow", [P, NT, ROW])
        K.adst = m.sb("adst", [P, NT, GH])
        with ExitStack() as c1:
            m1 = Mem(nc, c1)
            K.gcn_srcT = m1.sb("gcn_srcT", [P, G_GCN * P], U32)
            K.gcn_dstT = m1.sb("gcn_dstT", [P, G_GCN * P])
            K.gcn_tiles = m1.sb("gcn_tiles", [1, G_GCN * P], I32)
            K.acc = m1.sb("acc", [P, NT, D])
            K.gat_cnt = m1.sb("gat_cnt", [P, NT])
            K.gat_base = m1.sb("gat_base", [P, NT])
            with ExitStack() as c2:
                m2 = Mem(nc, c2)
                K.gat_place = m2.sb("gat_place", [P, GAT_C], U32)
                K.gat_pay = m2.sb("gat_pay", [P, GAT_C, 2], I32)
                K.xmv = m2.sb("xmv", [P, NT, 2])
                K.xrs = m2.sb("xrs", [P, NT])
                K.hmv = m2.sb("hmv", [P, KC, 2])
                K.kv = m2.sb("kv", [P, KC, P + 1])
                rounds = GAT_C // ROUND
                cut1, cut2 = rounds * 2 // 9, rounds * 5 // 8
                with ExitStack() as c5:
                    m5 = Mem(nc, c5)
                    K.gcn_start = m5.sb("gcn_start", [P, NT])
                    K.gcn_end = m5.sb("gcn_end", [P, NT])
                    K.degree = m5.sb("degree", [P, NT])
                    K.cnt = m5.sb("cnt", [P, NT])
                    K.base = m5.sb("base", [P, NT])
                    with ExitStack() as c6:
                        load_edges(nc, Mem(nc, c6), K, A)
                        places(nc, K, "ga", GAT_P, GAT_C, K.gat_tile, K.gat_cnt, K.gat_base, K.gat_place)
                        degrees(nc, K, A, (0, cut1))
                        counts_of_tiles(nc, K)
                        with ExitStack() as c7:
                            K.gcn_place = Mem(nc, c7).sb("gcn_place", [P, GCN_C], U32)
                            places(nc, K, "gc", GCN_P, GCN_C, K.gcn_tile, K.cnt, K.base, K.gcn_place, K.unsorted)
                            scatter_unsorted(nc, K)
                    step_tables(nc, K, "gc", K.gcn_pairs, E_GCN, K.cnt, K.base, UNIT_GCN, G_GCN, K.gcn_srcT,
                                K.gcn_dstT, K.gcn_start, K.gcn_end, K.gcn_tiles, gcn_td)
                dense_first(nc, K, A, (cut1, cut2 - cut1))
                dense_second(nc, K, A, (cut2, rounds - cut2))
            gather_sum(nc, K)
            second_norm(nc, K, A)
            step_tables(nc, K, "ga", K.gat_pairs, E_GAT, K.gat_cnt, K.gat_base, UNIT_GAT, G_GAT, K.gat_srcT, K.gat_dstT,
                        K.gat_start, K.gat_end)
        K.gsum = m.sb("gsum", [P, NT, ROW])
        with ExitStack() as c3:
            m3 = Mem(nc, c3)
            K.amax = m3.sb("amax", [P, NT, GH])
            K.feat = m3.sb("feat", [P, G_GAT * P, ROW])
            K.step_tile = m3.sb("step_tile", [P, G_GAT, NT])
            K.tile_step = m3.sb("tile_step", [P, G_GAT * P], BF16)
            with ExitStack() as c4:
                m4 = Mem(nc, c4)
                K.last = m4.sb("last", [P, G_GAT, NT])
                K.cut = m4.sb("cut", [P, G_GAT * P])
                K.mx = m4.sb("mx", [P, GH, G_GAT * P])
                gat_tables(nc, K)
                gat_max(nc, K)
                scan_max(nc, K)
                by_tile(nc, K, "pk", K.mx, False, GH, K.last, K.amax)
            own = m3.sb("own", [P, NT, GH])
            K.spread = m3.sb("spread", [P, PARTS * 2 * GH, G_GAT * P], BF16)
            gat_spread(nc, K, K.amax, own)
            gat_sum(nc, K)
            sums = m3.sb("sums", [P, NT, ROW])
            by_tile(nc, K, "sm", K.feat, True, ROW, K.step_tile, sums)
            gat_own(nc, K, own, sums)
        K.gate = m.sb("gate", [P, NT, NE])
        gates(nc, K, A)
        experts(nc, K, A)


_ARGS = {
    "x": "x", "src": "src", "dst": "dst", "L0_ffn_edge_index": "edge_index",
    "L0_gnn_b1": "b1", "L0_gnn_gamma": "gamma", "L0_gnn_beta": "beta", "L0_gnn_w2": "w2", "L0_gnn_b2": "b2",
    "L0_gnn_b_gcn": "b_gcn", "L0_mix_wq": "wq", "L0_mix_bq": "bq", "L0_mix_wk": "wk", "L0_mix_bk": "bk",
    "L0_mix_wv": "wv", "L0_mix_bv": "bv", "L0_mix_wo": "wo", "L0_mix_bo": "bo", "L0_ffn_W_gat": "W_gat",
    "L0_ffn_att_src": "att_src", "L0_ffn_att_dst": "att_dst", "L0_ffn_b_gat": "b_gat",
    "L0_ffn_ln_gamma": "ln_gamma", "L0_ffn_ln_beta": "ln_beta", "L0_ffn_W1": "W1", "L0_ffn_b1": "b1f",
    "L0_ffn_W2": "W2", "L0_ffn_b2": "b2f",
}
_TURNED = {"L0_gnn_w1": "w1T", "L0_gnn_w_gcn": "wgT"}


def kernel(**inputs):
    import types

    import numpy as _np
    import concourse.bacc as _bacc
    from concourse import mybir as _mybir
    from concourse.bass_utils import run_bass_kernel_spmd as _run

    nc = _bacc.Bacc("TRN2", target_bir_lowering=False, num_devices=1)
    A = types.SimpleNamespace()
    arrays = {}
    given = [(v, _np.ascontiguousarray(inputs[k])) for k, v in _ARGS.items()]
    given += [(v, _np.ascontiguousarray(_np.transpose(inputs[k]))) for k, v in _TURNED.items()]
    for name, a in given:
        arrays[f"in_{name}"] = a
        A.__dict__[name] = nc.dram_tensor(f"in_{name}", a.shape, _mybir.dt.from_np(a.dtype), kind="ExternalInput").ap()
    A.out = nc.dram_tensor("out_x", (N, D), _mybir.dt.float32, kind="ExternalOutput").ap()
    program(nc, A)
    r = _run(nc, [arrays], core_ids=[0])
    return r.results[0]["out_x"]
```
